# Optimizing a Trainium2 kernel written in Bass

```python
import numpy as np
import jax
import jax.numpy as jnp

def _softmax(x, axis=-1):
    return jax.nn.softmax(x, axis=axis)

def _gelu(x):
    return jax.nn.gelu(x, approximate=True)

def _silu(x):
    return jax.nn.silu(x)

def _sigmoid(x):
    return jax.nn.sigmoid(x)

def _layernorm(x, axis=-1, eps=1e-05):
    m = jnp.mean(x, axis=axis, keepdims=True)
    v = jnp.var(x, axis=axis, keepdims=True)
    return (x - m) / jnp.sqrt(v + eps)

def _scatter_add(tgt, idx, src, axis=0):
    return tgt.at[idx].add(src)

def _segment_sum(src, seg, n):
    return jax.ops.segment_sum(src, seg, n)
kernel_name = 'mk_gnn_preln_d4_gnn_r8_2a85a8'

def setup_inputs(seed: int=0):
    np.random.seed(seed)
    _w = jnp.asarray

    def _rec_inputs():
        import jax
        import jax.numpy as jnp
        _gk = jax.random.key(seed)
        x = -0.0005121 + 1.001 * jax.random.normal(jax.random.fold_in(_gk, 1), (12500, 32), jnp.float32)
        _s = jax.random.randint(jax.random.fold_in(_gk, 2), (100000,), 0, 12500, jnp.int32)
        _d = jax.random.randint(jax.random.fold_in(_gk, 3), (100000,), 0, 12500, jnp.int32)
        _loop = jnp.arange(12500, dtype=jnp.int32)
        src = jnp.concatenate([_s, _d, _loop])
        dst = jnp.concatenate([_d, _s, _loop])
        _o = jnp.argsort(dst, stable=True)
        src = src[_o]
        dst = dst[_o]
        edge_type_16 = jax.random.randint(jax.random.fold_in(_gk, 13), (212500,), 0, 16, jnp.int32)
        edge_type_86 = jax.random.randint(jax.random.fold_in(_gk, 14), (212500,), 0, 86, jnp.int32)
        edge_weight = jax.random.uniform(jax.random.fold_in(_gk, 15), (212500,), jnp.float32, 0.0, 1)
        edge_weight1 = jax.random.uniform(jax.random.fold_in(_gk, 16), (212500, 1), jnp.float32, 0.0, 1)
        return (x, src, dst, edge_type_16, edge_type_86, edge_weight, edge_weight1)
    x, src, dst, edge_type_16, edge_type_86, edge_weight, edge_weight1 = _rec_inputs()

    def _L0_gnn_setup():
        import jax, jax.numpy as jnp
        import numpy as np
        N = 12500
        E = 200000
        IN = 32
        OUT = 32
        R = 16
        B = 8
        key = jax.random.key(seed)
        k = jax.random.split(key, 7)
        inputs = jax.random.normal(k[0], (N, IN), jnp.float32)
        weight = jax.random.normal(k[1], (B, IN, OUT), jnp.float32) * (1.414 * (2.0 / (IN + OUT)) ** 0.5)
        w_comp = jax.random.normal(k[2], (R, B), jnp.float32) * (1.414 * (2.0 / (R + B)) ** 0.5)
        norm = jax.random.uniform(k[3], (E, 1), jnp.float32)
        src = jax.random.randint(k[4], (E,), 0, N)
        dst = jax.random.randint(k[5], (E,), 0, N)
        rel_type = jax.random.randint(k[6], (E,), 0, R)
        return {'inputs': inputs, 'weight': weight, 'w_comp': w_comp, 'norm': norm, 'src': src, 'dst': dst, 'rel_type': rel_type}
    _L0_gnn_all = _L0_gnn_setup()
    _L0_gnn_in = {k: v for k, v in _L0_gnn_all.items() if k in ('weight', 'w_comp')}
    del _L0_gnn_all

    def _L1_gnn_setup():
        import jax, jax.numpy as jnp
        import numpy as np
        N_NODES = 12500
        N_EDGES = 400000
        D_IN = 32
        D_OUT = 32
        K = 3
        key = jax.random.key(seed)
        k1, k2, k3, k4 = jax.random.split(key, 4)
        x = jax.random.normal(k1, (N_NODES, D_IN), dtype=jnp.float32)
        edge_index = jax.random.randint(k2, (2, N_EDGES), 0, N_NODES, dtype=jnp.int32)
        edge_weight = jax.random.uniform(k3, (N_EDGES,), dtype=jnp.float32)
        W = jax.random.normal(k4, (K, D_IN, D_OUT), dtype=jnp.float32) * 0.1
        b = jnp.zeros((D_OUT,), dtype=jnp.float32)
        return {'x': x, 'edge_index': edge_index, 'edge_weight': edge_weight, 'W': W, 'b': b}
    _L1_gnn_all = _L1_gnn_setup()
    _L1_gnn_in = {k: v for k, v in _L1_gnn_all.items() if k in ('W', 'b')}
    del _L1_gnn_all

    def _L2_gnn_setup():
        import jax, jax.numpy as jnp
        import numpy as np
        N_NODES = 6250
        N_EDGES = 100000
        INP_DIM = 32
        OUT_DIM = 32
        ATTN_DIM = 32
        NUM_RELS = 86
        NUM_BASES = 16
        GAMMA = 0.0
        key = jax.random.key(seed)
        ks = jax.random.split(key, 12)
        return {'h': jax.random.normal(ks[0], (N_NODES, INP_DIM), jnp.float32), 'weight': jax.random.normal(ks[1], (NUM_BASES, INP_DIM, OUT_DIM), jnp.float32), 'w_comp': jax.random.normal(ks[2], (NUM_RELS, NUM_BASES), jnp.float32), 'self_loop_weight': jax.random.normal(ks[3], (INP_DIM, OUT_DIM), jnp.float32), 'A1_w': jax.random.normal(ks[4], (ATTN_DIM, INP_DIM), jnp.float32), 'A1_b': jax.random.normal(ks[5], (ATTN_DIM,), jnp.float32), 'A2_w': jax.random.normal(ks[6], (ATTN_DIM, INP_DIM), jnp.float32), 'A2_b': jax.random.normal(ks[7], (ATTN_DIM,), jnp.float32), 'rel_emb': jax.random.normal(ks[8], (NUM_RELS, ATTN_DIM), jnp.float32), 'src': jax.random.randint(ks[9], (N_EDGES,), 0, N_NODES, jnp.int32), 'dst': jax.random.randint(ks[10], (N_EDGES,), 0, N_NODES, jnp.int32), 'etype': jax.random.randint(ks[11], (N_EDGES,), 0, NUM_RELS, jnp.int32)}
    _L2_gnn_all = _L2_gnn_setup()
    _L2_gnn_in = {k: v for k, v in _L2_gnn_all.items() if k in ('weight', 'w_comp', 'self_loop_weight', 'A1_w', 'A1_b', 'A2_w', 'A2_b', 'rel_emb')}
    del _L2_gnn_all

    def _L3_gnn_setup():
        import jax, jax.numpy as jnp
        import numpy as np
        N_NODES = 12500
        key = jax.random.key(seed)
        k1, k2, k3 = jax.random.split(key, 3)
        x = jax.random.normal(k1, (N_NODES, 32), dtype=jnp.float32)
        src = jax.random.randint(k2, (200000,), 0, N_NODES, dtype=jnp.int64)
        dst = jax.random.randint(k3, (200000,), 0, N_NODES, dtype=jnp.int64)
        return {'x': x, 'src': src, 'dst': dst}
    _L3_gnn_all = _L3_gnn_setup()
    _L3_gnn_in = {k: v for k, v in _L3_gnn_all.items() if k in ()}
    del _L3_gnn_all
    return {'x': x, 'src': src, 'dst': dst, 'edge_type_16': edge_type_16, 'edge_type_86': edge_type_86, 'edge_weight': edge_weight, 'edge_weight1': edge_weight1, 'L0_gnn_weight': _L0_gnn_in['weight'], 'L0_gnn_w_comp': _L0_gnn_in['w_comp'], 'L1_gnn_W': _L1_gnn_in['W'], 'L1_gnn_b': _L1_gnn_in['b'], 'L2_gnn_weight': _L2_gnn_in['weight'], 'L2_gnn_w_comp': _L2_gnn_in['w_comp'], 'L2_gnn_self_loop_weight': _L2_gnn_in['self_loop_weight'], 'L2_gnn_A1_w': _L2_gnn_in['A1_w'], 'L2_gnn_A1_b': _L2_gnn_in['A1_b'], 'L2_gnn_A2_w': _L2_gnn_in['A2_w'], 'L2_gnn_A2_b': _L2_gnn_in['A2_b'], 'L2_gnn_rel_emb': _L2_gnn_in['rel_emb']}

def reference(x, src, dst, edge_type_16, edge_type_86, edge_weight, edge_weight1, L0_gnn_weight, L0_gnn_w_comp, L1_gnn_W, L1_gnn_b, L2_gnn_weight, L2_gnn_w_comp, L2_gnn_self_loop_weight, L2_gnn_A1_w, L2_gnn_A1_b, L2_gnn_A2_w, L2_gnn_A2_b, L2_gnn_rel_emb):
    import jax
    import jax.numpy as jnp

    def _L0_gnn_ref(inputs, weight, w_comp, norm, src, dst, rel_type):
        import jax, jax.numpy as jnp
        import numpy as np
        N = 12500
        E = 200000
        IN = 32
        OUT = 32
        R = 16
        B = 8
        n, in_feat = inputs.shape
        num_bases, _, out_feat = weight.shape
        w = jnp.matmul(w_comp, weight.reshape(in_feat, num_bases, out_feat))
        w = w.reshape(-1, in_feat, out_feat)
        h_rel = jnp.einsum('ni,rio->nro', inputs, w)
        msg = h_rel[src, rel_type] * norm
        h = jax.ops.segment_sum(msg, dst, num_segments=n)
        return h

    def _L1_gnn_ref(x, edge_index, edge_weight, W, b):
        import jax, jax.numpy as jnp
        import numpy as np
        N_NODES = 12500
        N_EDGES = 400000
        D_IN = 32
        D_OUT = 32
        K = 3
        src, dst = (edge_index[0], edge_index[1])
        n = x.shape[0]
        deg = jax.ops.segment_sum(edge_weight, dst, num_segments=n)
        dinv = jnp.where(deg > 0, jax.lax.rsqrt(jnp.maximum(deg, 1e-12)), 0.0)
        w_hat = -dinv[dst] * edge_weight * dinv[src]

        def prop(v):
            return jax.ops.segment_sum(w_hat[:, None] * v[src], dst, num_segments=n)
        Tx0 = x
        Tx1 = prop(Tx0)
        out = Tx0 @ W[0] + Tx1 @ W[1]
        Tx2 = 2.0 * prop(Tx1) - Tx0
        out = out + Tx2 @ W[2]
        out = out + b
        return jax.nn.relu(out)

    def _L2_gnn_ref(h, weight, w_comp, self_loop_weight, A1_w, A1_b, A2_w, A2_b, rel_emb, src, dst, etype):
        import jax, jax.numpy as jnp
        import numpy as np
        N_NODES = 6250
        N_EDGES = 100000
        INP_DIM = 32
        OUT_DIM = 32
        ATTN_DIM = 32
        NUM_RELS = 86
        NUM_BASES = 16
        GAMMA = 0.0
        E = src.shape[0]
        N = h.shape[0]
        x = h[src]
        y = h[dst]
        c = w_comp[etype]
        xb = jnp.einsum('ei,bio->ebo', x, weight)
        msg = jnp.einsum('eb,ebo->eo', c, xb)
        x_hat = x @ A1_w.T + A1_b
        y_hat = y @ A2_w.T + A2_b + rel_emb[etype]
        scale = jnp.sqrt(jnp.asarray(INP_DIM, h.dtype))
        a = jnp.tanh(jax.nn.relu(jnp.sum(x_hat * y_hat, axis=-1) / scale))
        a = jnp.where(a > GAMMA, a, jnp.zeros_like(a))
        nei = jax.ops.segment_sum(a[:, None] * msg, dst, num_segments=N)
        last_e = jax.ops.segment_max(jnp.arange(E, dtype=jnp.int32), dst, num_segments=N)
        last_e = jnp.clip(last_e, 0, E - 1)
        curr = h[src[last_e]] @ self_loop_weight
        in_deg = jax.ops.segment_sum(jnp.ones((E,), h.dtype), dst, num_segments=N)
        h_new = jnp.where((in_deg > 0)[:, None], nei + curr, jnp.zeros_like(nei))
        return jax.nn.relu(h_new)

    def _L3_gnn_ref(x, src, dst):
        import jax, jax.numpy as jnp
        import numpy as np
        N_NODES = 12500
        n = x.shape[0]
        msg_sum = jax.ops.segment_sum(x[src], dst, num_segments=n)
        deg = jax.ops.segment_sum(jnp.ones_like(dst, dtype=x.dtype), dst, num_segments=n)
        return msg_sum / jnp.maximum(deg, 1.0)[:, None]
    edge_index = jnp.stack([src, dst])
    h = jnp.maximum(_layernorm(x, axis=-1), 0.0)
    x = x + _L0_gnn_ref(h, L0_gnn_weight, L0_gnn_w_comp, edge_weight1, src, dst, edge_type_16)
    h = jnp.maximum(_layernorm(x, axis=-1), 0.0)
    x = x + _L1_gnn_ref(h, edge_index, edge_weight, L1_gnn_W, L1_gnn_b)
    h = jnp.maximum(_layernorm(x, axis=-1), 0.0)
    x = x + _L2_gnn_ref(h, L2_gnn_weight, L2_gnn_w_comp, L2_gnn_self_loop_weight, L2_gnn_A1_w, L2_gnn_A1_b, L2_gnn_A2_w, L2_gnn_A2_b, L2_gnn_rel_emb, src, dst, edge_type_86)
    h = jnp.maximum(_layernorm(x, axis=-1), 0.0)
    x = x + _L3_gnn_ref(h, src, dst)
    return x

_drawn_inputs = setup_inputs


def setup_inputs(seed=0):
    import zlib

    import numpy as np

    out = dict(_drawn_inputs(seed))
    spreads = {'L1_gnn_b': (0.0, 0.1)}
    factors = {}
    for name, (base, spread) in spreads.items():
        noise = np.random.default_rng([zlib.crc32(name.encode()), seed]).standard_normal(out[name].shape)
        drawn = base * np.exp(spread * noise) if base else spread * noise
        out[name] = jnp.asarray(drawn.astype(out[name].dtype))
    for name, factor in factors.items():
        out[name] = (out[name] * factor).astype(out[name].dtype)
    return out
```

```python
from contextlib import ExitStack

import numpy as np
import concourse.bass as bass
from concourse import mybir
from concourse.alu_op_type import AluOpType as ALU

F32 = mybir.dt.float32
I32 = mybir.dt.int32
ACT = mybir.ActivationFunctionType
X_AXIS = mybir.AxisListType.X

P = 128
N = 12500
E = 212500
D = 32
R0, B0 = 16, 8
R2, B2 = 86, 16
NT = (N + P - 1) // P
NPAD = NT * P
TAIL = N - (NT - 1) * P
CH = 8
GROUP = CH * P
NG = (E + GROUP - 1) // GROUP
SLOTS = 4
STEPS = NG // SLOTS
LAST = E - (NG - 1) * GROUP
LP, LC = LAST // CH, LAST % CH
IC = (NG + SLOTS) * CH
WIN = 128
SW = NPAD + WIN
HG = NG // 2
BT = 14
NB = NT // BT
FT = 2 * STEPS
RP = R2 // 2
PAIR = 2 * (D + 1)
ROW2 = PAIR + D
HALF = [(0, 21), (21, 22)]
WB_DMAS = 12
BUILD = [(0, 0, 7), (0, 7, 7), (0, 14, 7), (1, 21, 7), (1, 28, 7), (1, 35, 7), (1, 42, 1)]
NBUILD = len(BUILD)
EVEN, ODD = 4, 3
HALF_DONE = [(2, 1), (EVEN, ODD)]
EPS = 1e-5
FAR = -1.0e6


def gnn_kernel(nc, x, src, dst, et16, et86, ew, ew1, w0, comp0, w1, b1, w2, comp2, selfw,
               a1w, a1b, a2w, a2b, rel, out):
    def scratch(name, shape, dt=F32):
        return nc.dram_tensor(name, shape, dt, kind="Internal").ap()

    table0 = scratch("table0", (NPAD * R0, D))
    table2 = scratch("table2", (NPAD * RP, ROW2))
    nodes = [scratch(f"nodes{i}", (NPAD, D)) for i in range(4)]
    meta_d = scratch("meta_d", (NG, 2), I32)

    ctx = ExitStack()
    with ctx:
        def sb(name, shape, dt=F32):
            return ctx.enter_context(nc.sbuf_tensor(name, shape, dt))

        def sem(name):
            return ctx.enter_context(nc.semaphore(name))

        src_i = sb("src_i", [P, IC], I32)
        idx_a = sb("idx_a", [P, IC], I32)
        idx_h = sb("idx_h", [P, IC], I32)
        ew_s = sb("ew_s", [P, NG * CH])
        two = sb("two", [P, 2, NG * CH])
        ew1_s = two[:, 0, :]
        lsrc = two[:, 1, :]
        par = two
        drel = sb("drel", [P, NG * CH])
        meta = sb("meta", [1, NG * 2], I32)
        X = sb("X", [P, NT * D])
        H = sb("H", [P, FT * D])
        O = sb("O", [P, FT * D])
        deg = sb("deg", [P, NT])
        dinv = sb("dinv", [P, NT])
        last_i = sb("last_i", [P, NT], I32)
        big = sb("big", [P, SW])
        gbuf = sb("gbuf", [P, SLOTS, CH, ROW2])
        ibuf = sb("ibuf", [P, SLOTS, CH], I32)
        onehot = sb("onehot", [P, CH, WIN])
        prod = sb("prod", [P, CH, WIN])
        cur = sb("cur", [P, CH])
        score = sb("score", [P, CH])
        att = sb("att", [P, CH])
        msg = sb("msg", [P, CH, D])
        msg2 = sb("msg2", [P, CH, 2, D])
        own = sb("own", [P, CH, 2])
        pick = sb("pick", [P, CH, 2])
        att_p = sb("att_p", [P, CH, 2])
        zdiag = sb("zdiag", [P, 4, WIN])
        xhat_t = sb("xhat_t", [P, 2, P])
        tbuf = sb("tbuf", [P, 2, HALF[1][1] * ROW2])
        stage = tbuf[0:36, 0, 0:BT * P]
        t0buf = tbuf[:, 0, 0:2 * R0 * D].rearrange("p (a n) -> p a n", a=2)
        ubuf = sb("ubuf", [P, BT * D])
        sq = sb("sq", [P, BT * D])
        cent = sb("cent", [P, BT * D])
        stat = sb("stat", [P, 4, BT])
        cst = sb("cst", [P, BT * D])
        xhat_e = cst[:, 0:2 * P].rearrange("p (a b) -> p a b", a=2)
        hst = sb("hst", [P, D])
        ht = sb("ht", [D + 1, P])
        iota_i = sb("iota_i", [P, WIN], I32)
        iota = sb("iota", [P, WIN])
        pcol_i = sb("pcol_i", [P, 1], I32)
        pcol = sb("pcol", [P, 1])
        ident = sb("ident", [P, P])
        ones = sb("ones", [P, P])
        w0_s = prod[0:B0, :, :].rearrange("p a b -> p (a b)")
        comp0_s = sb("comp0_s", [B0, 2, D])
        w0f = sb("w0f", [D, R0 * D])
        w1_s = sb("w1_s", [D, 3, D])
        w02 = sb("w02", [D, D])
        b1_s = sb("b1_s", [1, D])
        w2_s = onehot[0:B2, :, :].rearrange("p a b -> p (a b)").rearrange("p (i o) -> p i o", o=D)
        comp2_s = sb("comp2_s", [B2, R2])
        w2f = sb("w2f", [D + 1, R2, D + 1])
        self_s = sb("self_s", [D, D])
        a1 = sb("a1", [D, D + 1])
        a1t = sb("a1t", [D + 1, D])
        a2t = sb("a2t", [D + 1, D])
        relt = sb("relt", [D, R2])
        drow_i = tbuf[0:HG, 0, 0:2 * GROUP].bitcast(I32).rearrange("p (h n) -> p h n", h=2)
        drow = tbuf[0:HG, 1, 0:2 * GROUP].rearrange("p (h n) -> p h n", h=2)
        dst_f = big[:, 0:NG * CH]
        dst_i = big[:, 2048:2048 + NG * CH].bitcast(I32)
        nxt_i = big[:, 4096:4096 + NG * CH].bitcast(I32)
        nxt_f = big[:, 6144:6144 + NG * CH]
        tmp_f = big[:, 8192:8192 + NG * CH]
        bounds_b = big[:, 10240:10240 + 2 * NG].bitcast(I32)
        tmp_i = tbuf[:, 0, 0:0 + IC].bitcast(I32)
        mm_f = sb("mm_f", [HG, 2, 2])
        mm_i = sb("mm_i", [HG, 2, 2], I32)
        mm_w = sb("mm_w", [HG, 2], I32)
        flag = sb("flag", [P, 1])
        mask = sb("mask", [P, NT])
        raw = sb("raw", [P, CH])
        att2 = sb("att2", [P, CH])
        xh = sb("xh", [P, D])
        node = sb("node", [P, 1])
        lsrc_i = sb("lsrc_i", [P, 1], I32)
        flag_i = sb("flag_i", [1, 1], I32)
        last_f = sb("last_f", [P, NT])
        li_a = sb("li_a", [P, NT], I32)
        li_b = sb("li_b", [P, NT], I32)
        key = prod[:, :, :].rearrange("p a b -> p (a b)")
        keyed = onehot[:, :, :].rearrange("p a b -> p (a b)")
        trow = tbuf[:, 0, 0:GROUP].bitcast(I32)
        base = sb("base", [P, 1])
        found = sb("found", [P, 2])
        last_e = sb("last_e", [P, NT])
        lcol = sb("lcol", [P, 1], I32)

        ps_wide = ctx.enter_context(nc.psum_tensor("ps_wide", [P, 4, 512], F32))
        ps_agg = ctx.enter_context(nc.psum_tensor("ps_agg", [P, 512], F32))
        ps_t = ctx.enter_context(nc.psum_tensor("ps_t", [P, 512], F32))
        ps_z = ctx.enter_context(nc.psum_tensor("ps_z", [P, 512], F32))
        ps_h = ctx.enter_context(nc.psum_tensor("ps_h", [P, 512], F32))
        turned = ps_t[:, 0:BT * 36].rearrange("p (t c) -> p t c", c=36)
        wide = ps_wide[:, :, :].rearrange("p a b -> p (a b)")
        zed = ps_z[:, 0:BT * D].rearrange("p (t c) -> p t c", c=D)


        s_x = sem("x_loaded")
        s_src = sem("sources_loaded")
        s_et16 = sem("types16_loaded")
        s_dst = sem("targets_loaded")
        s_nxt = sem("next_targets_loaded")
        s_ew1 = sem("weights1_loaded")
        s_ew = sem("weights_loaded")
        s_et86 = sem("types86_loaded")
        s_rows = sem("target_rows_loaded")
        s_wa = sem("first_layers_weights_loaded")
        s_wb = sem("later_layers_weights_loaded")
        s_pad = sem("padding_set")
        s_iota = sem("iota_made")
        s_const = sem("constants_made")
        s_mm = sem("group_bounds_made")
        s_meta_w = sem("group_bounds_written")
        s_meta_r = sem("group_bounds_read")
        s_idx = sem("row_numbers_known")
        s_idx2 = sem("table2_row_numbers_known")
        s_w0p = sem("w0_product")
        s_w0c = sem("w0_copied")
        s_flagp = sem("unsorted_counts_ready")
        s_flags = sem("unsorted_counts_summed")
        s_flag = sem("unsorted_flag_ready")
        s_lused = sem("target_row_used")
        s_lrow = sem("target_row_loaded")
        s_lcol = sem("last_edges_known")
        s_lgot = sem("last_source_gathered")
        s_last = sem("last_rows_known")
        s_curr = sem("last_sources_rows_gathered")
        s_w2p = sem("w2_product")
        s_w2c = sem("w2_copied")
        s_ypad = sem("yhat_padding_set")
        s_out = sem("output_written")
        s_carry = sem("waits_carried")

        tile = [{n: sem(f"tile{f}_{n}") for n in ("h_ready", "h_staged", "h_turned", "ht_ready", "made", "copied")}
                for f in range(3)]
        s_t0 = [sem("table0_stored_0"), sem("table0_stored_1")]
        s_t2 = [sem("table2_stored_0"), sem("table2_stored_1")]
        s_round = sem("table2_round_made")
        s_even = sem("table2_even_products_copied")
        s_odd = sem("table2_odd_products_copied")
        blk = [{n: sem(f"block{e}_{n}") for n in ("staged", "turned", "read", "u_ready", "u_stored")}
               for e in range(5)]
        s_var = [sem(f"variance_ready_{n}") for n in range(4)]
        s_std = [sem(f"deviation_ready_{n}") for n in range(4)]
        s_cst = sem("last_rows_staged")
        s_ct = sem("last_rows_turned")
        s_ctc = sem("last_rows_turned_copied")
        s_cz = sem("self_product")
        sums = [{n: sem(f"sum{s}_{n}") for n in ("idx_ready", "slot_free", "onehot_ready", "sums_ready", "added", "all_added")}
                for s in range(5)]
        for s in range(5):
            sums[s]["gathered"] = [sem(f"sum{s}_gathered_{k}") for k in range(SLOTS)]
        s_xe = sem("xhat_compact")
        s_xt = sem("xhat_turned")
        s_xtc = sem("xhat_turned_copied")
        s_zd = sem("yhat_window_ready")
        s_pp = [sem("products_ready_0"), sem("products_ready_1")]
        s_sc = sem("scores_ready")
        s_att = sem("attention_ready")
        s_msg = sem("messages_ready")

        WIDTH = [D, D, D, ROW2, D]
        CHN = [D + 3, D, D, D, D]
        IDX = [idx_a, idx_h, idx_h, idx_a, idx_h]
        TABLE = [table0, nodes[0], nodes[1], table2, nodes[3]]
        X3 = X[:, :].rearrange("p (t c) -> p t c", c=D)

        def cols(t, i, w):
            return t[:, bass.ds(i * (BT * w), BT * w)]

        def by_tile(a, c=D):
            return a.rearrange("p (t c) -> p t c", c=c)

        def over(a, n):
            return a.unsqueeze(2).to_broadcast([P, a.shape[1], n])

        def carry_wait(eng):
            eng.sem_inc(s_carry, 1)

        def first_then_loop(eng, n):
            yield 0
            with eng.Fori(1, n) as i:
                yield i

        block = ctx.enter_context(nc.Block())

        @block.sync
        def _(sp):
            def edge_array(to, a, done, n=E):
                c0 = (NG - 1) * CH
                sp.dma_start(to[:, 0:c0].rearrange("p (g c) -> p g c", c=CH),
                             a[0:(NG - 1) * GROUP].rearrange("(g p c) -> p g c", p=P, c=CH)).then_inc(done, 16)
                at = (NG - 1) * GROUP
                full, rest = (n - at) // CH, (n - at) % CH
                sp.dma_start(to[0:full, c0:c0 + CH],
                             a[at:at + full * CH].rearrange("(p c) -> p c", c=CH)).then_inc(done, 16)
                sp.dma_start(to[full:full + 1, c0:c0 + rest],
                             a[at + full * CH:n].rearrange("(o c) -> o c", o=1)).then_inc(done, 16)

            sp.wait_ge(s_pad, 1)
            sp.dma_start(X3[:, 0:NT - 1, :], x[0:(NT - 1) * P, :].rearrange("(t p) c -> p t c", p=P)).then_inc(s_x, 16)
            sp.dma_start(X3[0:TAIL, NT - 1, :], x[(NT - 1) * P:N, :]).then_inc(s_x, 16)
            sp.dma_start(w0_s[:, :].rearrange("b (i o) -> b i o", o=D),
                         w0.rearrange("b i o -> (b i o)").rearrange("(i b o) -> b i o", b=B0, o=D)).then_inc(s_wa, 16)
            turned0 = comp0.rearrange("r b -> b r")
            sp.dma_start(comp0_s[:, 0, 0:R0], turned0, allow_slow_non_contiguous=True).then_inc(s_wa, 16)
            sp.dma_start(comp0_s[:, 1, R0:D], turned0, allow_slow_non_contiguous=True).then_inc(s_wa, 16)
            edge_array(src_i, src, s_src)
            edge_array(idx_a, et16, s_et16)
            for h in range(2):
                rows = HG - h
                sp.dma_start(drow_i[0:rows, h, :],
                             dst[h * HG * GROUP:(h * HG + rows) * GROUP].rearrange("(p n) -> p n", n=GROUP)).then_inc(s_rows, 16)
            sp.dma_start(drow_i[HG - 1:HG, 1, :], dst[E - GROUP:E].rearrange("(p n) -> p n", p=1)).then_inc(s_rows, 16)
            edge_array(dst_i, dst, s_dst)
            edge_array(nxt_i, dst[1:E], s_nxt, E - 1)
            edge_array(ew1_s, ew1.rearrange("e o -> (e o)"), s_ew1)
            edge_array(ew_s, ew, s_ew)
            sp.dma_start(w1_s[:, :, :], w1.rearrange("k i o -> i k o")).then_inc(s_wb, 16)
            sp.dma_start(b1_s[:, :], b1.rearrange("(a c) -> a c", a=1)).then_inc(s_wb, 16)
            sp.dma_start(w2_s[:, :, :], w2).then_inc(s_wb, 16)
            sp.dma_start(comp2_s[:, :], comp2.rearrange("r b -> b r"), allow_slow_non_contiguous=True).then_inc(s_wb, 16)
            sp.dma_start(self_s[:, :], selfw).then_inc(s_wb, 16)
            sp.dma_start(a1[:, 0:D], a1w).then_inc(s_wb, 16)
            sp.dma_start(a1[:, D:D + 1], a1b.rearrange("(k a) -> k a", a=1), allow_slow_non_contiguous=True).then_inc(s_wb, 16)
            for t, w, b in ((a1t, a1w, a1b), (a2t, a2w, a2b)):
                sp.dma_start(t[0:D, :], w.rearrange("k i -> i k"), allow_slow_non_contiguous=True).then_inc(s_wb, 16)
                sp.dma_start(t[D:D + 1, :], b.rearrange("(a k) -> a k", a=1)).then_inc(s_wb, 16)
            sp.dma_start(relt[:, :], rel.rearrange("r k -> k r"), allow_slow_non_contiguous=True).then_inc(s_wb, 16)

            sp.wait_ge(s_mm, 1)
            sp.dma_start(meta_d.rearrange("(h p) w -> p h w", h=2), mm_i[:, :, :]).then_inc(s_meta_w, 16)
            sp.wait_ge(s_meta_w, 16)
            sp.dma_start(meta[:, :], meta_d.rearrange("g w -> (g w)").rearrange("(a n) -> a n", a=1)).then_inc(s_meta_r, 16)
            sp.dma_start(bounds_b, meta_d.rearrange("g w -> (g w)").partition_broadcast(P)).then_inc(s_meta_r, 16)

            with sp.Fori(0, NT // 2) as i:
                for j in range(2):
                    sp.wait_ge(tile[0]["copied"], 2 * i + j + 1)
                    sp.dma_start(table0[bass.ds(i * (2 * P * R0) + j * P * R0, P * R0), :].rearrange("(p r) c -> p (r c)", p=P),
                                 t0buf[:, j, :]).then_inc(s_t0[j], 16)

            sp.wait_ge(s_flag, 1)
            unsorted = sp.value_load(flag_i[0:1, 0:1], min_val=0, max_val=1)
            with sp.If(unsorted > 0):
                with sp.Fori(0, NG - 1) as g:
                    sp.wait_ge(s_lused, g + 1)
                    sp.dma_start(trow, dst[bass.ds(g * GROUP, GROUP)].partition_broadcast(P)).then_inc(s_lrow, 16)
                sp.wait_ge(s_lused, NG)
                sp.dma_start(trow, dst[E - GROUP:E].partition_broadcast(P)).then_inc(s_lrow, 16)

            def store_nodes(e, to, of):
                view = nodes[to].rearrange("(p t) c -> p (t c)", p=P)
                with sp.Fori(0, NB) as i:
                    sp.wait_ge(blk[e]["u_ready"], i + 1)
                    sp.dma_start(view[:, bass.ds(i * (BT * D), BT * D)], of(i)).then_inc(blk[e]["u_stored"], 16)

            store_nodes(0, 0, lambda i: ubuf[:, :])
            sp.wait_ge(sums[0]["all_added"], 1)
            edge_array(idx_a, et86, s_et86)
            store_nodes(1, 1, lambda i: ubuf[:, :])
            store_nodes(2, 2, lambda i: cols(H, i, D))
            with sp.Fori(0, NT) as t:
                for h in range(2):
                    sp.wait_ge(s_even, EVEN * t + HALF_DONE[h][0])
                    carry_wait(sp)
                    sp.wait_ge(s_odd, ODD * t + HALF_DONE[h][1])
                    carry_wait(sp)
                    r0, n = HALF[h]
                    view = table2[bass.ds(t * (P * RP), P * RP), :].rearrange("(p r) c -> p (r c)", p=P)
                    sp.dma_start(view[:, r0 * ROW2:(r0 + n) * ROW2], tbuf[:, h, 0:n * ROW2]).then_inc(s_t2[h], 16)
            store_nodes(3, 3, lambda i: cols(H, i, D))
            sp.wait_ge(blk[4]["u_ready"], NB)
            sp.dma_start(out[0:(NT - 1) * P, :].rearrange("(t p) c -> p t c", p=P), X3[:, 0:NT - 1, :]).then_inc(s_out, 16)
            sp.dma_start(out[(NT - 1) * P:N, :], X3[0:TAIL, NT - 1, :]).then_inc(s_out, 16)
            sp.wait_ge(s_out, 32)

        @block.gpsimd
        def _(pool):
            nc.gpsimd.iota(iota_i[:, :], [[1, WIN]], base=0, channel_multiplier=0)
            nc.gpsimd.iota(pcol_i[:, :], [[1, 1]], base=0, channel_multiplier=1).then_inc(s_iota, 1)


            def gather_rows(s):
                q = sums[s]
                with pool.Fori(0, STEPS) as i:
                    for k in range(SLOTS):
                        pool.wait_ge(q["slot_free"], i * SLOTS + k + 1)
                        pool.wait_ge(q["idx_ready"], i * SLOTS + k + 1)
                        carry_wait(pool)
                        for c in range(CH):
                            nc.gpsimd.indirect_dma_start(
                                out=gbuf[:, k, c, 0:WIDTH[s]], out_offset=None, in_=TABLE[s],
                                in_offset=bass.IndirectOffsetOnAxis(ap=ibuf[:, k, c:c + 1], axis=0),
                            ).then_inc(q["gathered"][k], 16)

            for j in range(2):
                pool.wait_ge(s_t0[j], 16 * (NT // 2))
            gather_rows(0)
            pool.wait_ge(s_flag, 1)
            unsorted = pool.value_load(flag_i[0:1, 0:1], min_val=0, max_val=1)
            with pool.If(unsorted > 0):
                with pool.Fori(0, NT) as t:
                    pool.wait_ge(s_lcol, t + 1)
                    carry_wait(pool)
                    nc.gpsimd.indirect_dma_start(
                        out=lsrc_i[:, :], out_offset=None, in_=src.rearrange("(e o) -> e o", o=1),
                        in_offset=bass.IndirectOffsetOnAxis(ap=lcol[:, 0:1], axis=0)).then_inc(s_lgot, 16)
            pool.wait_ge(blk[0]["u_stored"], 16 * NB)
            gather_rows(1)
            pool.wait_ge(blk[1]["u_stored"], 16 * NB)
            gather_rows(2)
            pool.wait_ge(blk[2]["u_stored"], 16 * NB)
            pool.wait_ge(s_last, 1)
            for t in range(NT):
                nc.gpsimd.indirect_dma_start(
                    out=O[:, t * D:(t + 1) * D], out_offset=None, in_=nodes[2],
                    in_offset=bass.IndirectOffsetOnAxis(ap=last_i[:, t:t + 1], axis=0)).then_inc(s_curr, 16)
            for h in range(2):
                pool.wait_ge(s_t2[h], 16 * NT)
            gather_rows(3)
            pool.wait_ge(blk[3]["u_stored"], 16 * NB)
            gather_rows(4)

        @block.scalar
        def _(act):
            def turn_tile(f, t):
                s = tile[f]
                act.wait_ge(s["h_turned"], t + 1)
                nc.scalar.copy(hst[:, :], H[:, bass.ds(t * D, D)]).then_inc(s["h_staged"], 1)
                act.wait_ge(s["h_turned"], t + 2)
                act.wait_ge(s["made"], t + 1)
                nc.scalar.copy(ht[0:D, :], ps_h[0:D, 0:P]).then_inc(s["ht_ready"], 1)

            def roots(n, width):
                return nc.scalar.activation(stat[:, 1:1 + width, :], stat[:, 1:1 + width, :], ACT.Sqrt)

            def lay_out_rows(s, beside=None):
                q = sums[s]
                for k in range(SLOTS):
                    nc.scalar.copy(ibuf[:, k, :], IDX[s][:, k * CH:(k + 1) * CH]).then_inc(q["idx_ready"], 1)
                count = act.alloc_register(f"act_windows_{s}")
                act.reg_mov(count, 0)
                with act.Fori(0, STEPS) as i:
                    for k in range(SLOTS):
                        if s == 3:
                            attention(i, k, count)
                        act.wait_ge(q["gathered"][k], (i + 1) * (16 * CH))
                        nc.scalar.copy(ibuf[:, k, :], IDX[s][:, bass.ds(i * (SLOTS * CH) + (SLOTS + k) * CH, CH)]
                                       ).then_inc(q["idx_ready"], 1)
                    if s == 1:
                        for j in range(2):
                            turn_tile(1, 2 * i + j)

            def attention(i, k, count):
                g = i * SLOTS + k
                start = act.value_load(meta[0:1, bass.ds(g * 2, 1)], min_val=0, max_val=N - 1)
                windows = act.value_load(meta[0:1, bass.ds(g * 2 + 1, 1)], min_val=1, max_val=NT)
                act.wait_ge(sums[3]["gathered"][k], (i + 1) * (16 * CH))
                nc.scalar.copy(xhat_e[:, :, :].rearrange("p a (b c) -> p (a b) c", c=D), gbuf[:, k, :, PAIR:ROW2]).then_inc(s_xe, 1)
                act.wait_ge(s_xt, g + 1)
                nc.scalar.copy(xhat_t[:, :, :], ps_wide[:, 2, 0:2 * P].rearrange("p (a b) -> p a b", a=2)).then_inc(s_xtc, 1)
                at = act.alloc_register(f"act_at_{k}")
                act.reg_mov(at, start)
                with act.Fori(0, windows) as w:
                    act.reg_add(count, count, 1)
                    n = act.snap(count)
                    a = act.snap(at, min_val=0, max_val=NPAD)
                    act.wait_ge(s_pp[1], n)
                    for c in range(4):
                        last = nc.scalar.copy(zdiag[D * c:D * (c + 1), c, :], big[64:64 + D, bass.ds(a, WIN)])
                    last.then_inc(s_zd, 1)
                    act.wait_ge(s_sc, n + 1)
                    nc.scalar.activation(att[:, :], score[:, :], ACT.Tanh).then_inc(s_att, 1)
                    act.reg_add(at, at, WIN)
                act.free_register(at)

            def stage_blocks(e, norm=None, width=1):
                act.wait_ge(sums[e]["all_added"], 1)
                s = blk[e]
                for i in first_then_loop(act, NB):
                    if not isinstance(i, int):
                        act.wait_ge(s["turned"], i)
                    nc.scalar.copy(stage[0:CHN[e], :], big[0:CHN[e], bass.ds(i * (BT * P), BT * P)]).then_inc(s["staged"], 1)
                    if e == 3:
                        nc.scalar.copy(cst[:, :], cols(O, i, D)).then_inc(s_cst, 1)
                        act.wait_ge(s_ct, i + 1)
                        act.wait_ge(s["turned"], i + 1)
                        nc.scalar.copy(stage[0:D, :], wide[0:D, 0:BT * P]).then_inc(s_ctc, 1)
                        act.wait_ge(s_cz, i + 1)
                    if norm is not None:
                        act.wait_ge(s_var[norm], i + 1)
                        roots(norm, width).then_inc(s_std[norm], 1)

            with act.Fori(0, NB) as i:
                act.wait_ge(s_var[0], i + 1)
                roots(0, 1).then_inc(s_std[0], 1)
            act.wait_ge(s_w0p, 1)
            nc.scalar.copy(w0f[:, :], ps_z[0:D, :]).then_inc(s_w0c, 1)
            act.wait_ge(tile[0]["h_ready"], 1)
            with act.Fori(0, NT) as t:
                turn_tile(0, t)
            act.wait_ge(s_idx, 1)
            lay_out_rows(0)
            stage_blocks(0, 1, 2)
            lay_out_rows(1)
            stage_blocks(1)
            lay_out_rows(2)
            stage_blocks(2, 2)
            act.wait_ge(tile[2]["h_ready"], 1)
            nc.scalar.copy(hst[:, :], H[:, 0:D]).then_inc(tile[2]["h_staged"], 1)
            for t in first_then_loop(act, NT):
                first = isinstance(t, int)
                act.wait_ge(tile[2]["h_turned"], t + 2)
                act.wait_ge(tile[2]["made"], t + 1)
                nc.scalar.copy(ht[0:D, :], ps_h[0:D, 0:P]).then_inc(tile[2]["ht_ready"], 1)
                nc.scalar.copy(hst[:, :], H[:, bass.ds(t * D + D, D)]).then_inc(tile[2]["h_staged"], 1)
                act.wait_ge(tile[2]["made"], t + 2)
                nc.scalar.copy(big[64:64 + D, bass.ds(t * P, P)], ps_agg[0:D, 0:P])
                nc.scalar.copy(xh[:, :], ps_t[:, 0:D]).then_inc(tile[2]["copied"], 1)
                for r, (h, r0, n) in enumerate(BUILD):
                    half0, half_n = HALF[h]
                    rows = tbuf[:, h, 0:half_n * ROW2].rearrange("p (r c) -> p r c", c=ROW2)
                    if r0 == half0:
                        if not first:
                            act.wait_ge(s_t2[h], t * 16)
                        act.wait_ge(tile[2]["copied"], t + 1)
                        nc.scalar.copy(rows[:, :, PAIR:ROW2], xh[:, :].unsqueeze(1).to_broadcast([P, half_n, D]))
                    if r % 2:
                        continue
                    act.wait_ge(s_round, t * NBUILD + r + 1)
                    nc.scalar.copy(rows[:, r0 - half0:r0 - half0 + n, 0:PAIR],
                                   ps_wide[:, r % 2, 0:n * PAIR].rearrange("p (r c) -> p r c", c=PAIR)).then_inc(s_even, 1)
            act.sem_inc(s_xtc, 1)
            act.wait_ge(s_idx2, 1)
            lay_out_rows(3)
            stage_blocks(3, 3)
            lay_out_rows(4)
            stage_blocks(4)

        @block.tensor
        def _(pe):

            def turn_tile(f, t):
                s = tile[f]
                pe.wait_ge(s["h_staged"], t + 1)
                nc.tensor.transpose(ps_h[0:D, 0:P], hst[:, :], ident[:, :]).then_inc(s["h_turned"], 1)
                pe.wait_ge(s["ht_ready"], t + 1)

            def windows_of_group(s, i, k, count):
                q, g = sums[s], i * SLOTS + k
                windows = pe.value_load(meta[0:1, bass.ds(g * 2 + 1, 1)], min_val=1, max_val=NT)
                if s == 3:
                    pe.wait_ge(s_xe, g + 1)
                    pe.wait_ge(s_xtc, g + 1)
                    for a in range(2):
                        last = nc.tensor.transpose(ps_wide[:, 2, a * P:(a + 1) * P],
                                                   xhat_e[:, a, :], ident[:, :])
                    last.then_inc(s_xt, 1)
                    pe.wait_ge(s_xtc, g + 2)
                    carry_wait(pe)
                with pe.Fori(0, windows) as w:
                    pe.reg_add(count, count, 1)
                    n = pe.snap(count)
                    if s == 3:
                        pe.wait_ge(s_zd, n)
                        pe.wait_ge(s_sc, n)
                        for a in range(2):
                            nc.tensor.matmul(ps_wide[:, a, :], xhat_t[:, a, :],
                                             zdiag[:, :, :].rearrange("p a b -> p (a b)"),
                                             start=True, stop=True).then_inc(s_pp[a], 1)
                        pe.wait_ge(s_msg, n)
                    pe.wait_ge(q["onehot_ready"], n)
                    pe.wait_ge(q["added"], n)
                    for c in range(CH):
                        lhs = msg[:, c, :] if s == 3 else gbuf[:, k, c, 0:CHN[s]]
                        last = nc.tensor.matmul(ps_agg[0:CHN[s], 0:WIN], lhs, onehot[:, c, :],
                                                start=(c == 0), stop=(c == CH - 1))
                    last.then_inc(q["sums_ready"], 1)

            def sum_edges(s):
                count = pe.alloc_register(f"pe_windows_{s}")
                pe.reg_mov(count, 0)
                with pe.Fori(0, STEPS) as i:
                    for k in range(SLOTS):
                        windows_of_group(s, i, k, count)
                    if s == 1:
                        for j in range(2):
                            t = 2 * i + j
                            turn_tile(1, t)
                            pe.wait_ge(tile[1]["copied"], t + 1)
                            nc.tensor.matmul(ps_z[:, 0:D], ht[0:D, :], w02[:, :], start=True, stop=False)
                            nc.tensor.matmul(ps_z[:, 0:D], ones[0:1, :], b1_s[:, :], start=False,
                                             stop=True).then_inc(tile[1]["made"], 1)

            def turn_blocks(e):
                s = blk[e]
                with pe.Fori(0, NB) as i:
                    pe.wait_ge(s["staged"], i + 1)
                    pe.wait_ge(s["read"], i + 1)
                    carry_wait(pe)
                    if e != 2:
                        for k in range(BT):
                            last = nc.tensor.transpose(turned[:, k, 0:CHN[e]], stage[0:CHN[e], k * P:(k + 1) * P],
                                                       ident[0:CHN[e], 0:CHN[e]])
                    if e in (1, 2):
                        for k in range(BT):
                            last = nc.tensor.matmul(zed[:, k, :], stage[0:D, k * P:(k + 1) * P], w1_s[:, e, :],
                                                    start=True, stop=True)
                    last.then_inc(s["turned"], 1)
                    if e == 3:
                        pe.wait_ge(s_cst, i + 1)
                        for k in range(BT):
                            last = nc.tensor.transpose(wide[0:D, k * P:(k + 1) * P], cst[:, k * D:(k + 1) * D], ident[:, :])
                        last.then_inc(s_ct, 1)
                        pe.wait_ge(s_ctc, i + 1)
                        for k in range(BT):
                            last = nc.tensor.matmul(zed[:, k, :], stage[0:D, k * P:(k + 1) * P], self_s[:, :],
                                                    start=True, stop=True)
                        last.then_inc(s_cz, 1)

            for f in range(3):
                pe.sem_inc(tile[f]["h_turned"], 1)
                pe.sem_inc(tile[f]["made"], 1)
            pe.wait_ge(s_wa, 48)
            w0v = w0_s[:, :].rearrange("b (r a o) -> b a r o", a=2, o=D)
            for a in range(2):
                last = nc.tensor.matmul(ps_z[0:D, :].rearrange("p (r o) -> p r o", o=D), comp0_s[:, a, :], w0v[:, a, :, :],
                                        start=(a == 0), stop=(a == 1))
            last.then_inc(s_w0p, 1)
            pe.wait_ge(s_const, 1)
            pe.wait_ge(s_w0c, 1)
            for i in first_then_loop(pe, NT // 2):
                for j in range(2):
                    turn_tile(0, 2 * i + j)
                    if not isinstance(i, int):
                        pe.wait_ge(tile[0]["copied"], 2 * i + j - 1)
                    nc.tensor.matmul(ps_wide[:, j, :], ht[0:D, :], w0f[:, :], start=True, stop=True).then_inc(tile[0]["made"], 1)
            pe.wait_ge(s_flagp, 1)
            nc.tensor.matmul(ps_agg[0:1, 0:1], flag[:, :], ones[:, 0:1], start=True, stop=True).then_inc(s_flags, 1)
            pe.wait_ge(s_wb, 16 * WB_DMAS)
            pe.wait_ge(tile[0]["copied"], NT)
            for r, o0 in enumerate(range(0, D, 5)):
                if r >= 2:
                    pe.wait_ge(s_w2c, r - 1)
                for o in range(o0, min(o0 + 5, D)):
                    last = nc.tensor.matmul(ps_wide[0:D, r % 2, (o - o0) * R2:(o - o0 + 1) * R2], w2_s[:, :, o],
                                            comp2_s[:, :], start=True, stop=True)
                last.then_inc(s_w2p, 1)
            nc.tensor.matmul(ps_z[0:D + 1, 0:R2], a1[:, :], relt[:, :], start=True, stop=True).then_inc(s_w2p, 1)
            pe.wait_ge(s_meta_r, 32)
            sum_edges(0)
            turn_blocks(0)
            sum_edges(1)
            turn_blocks(1)
            sum_edges(2)
            turn_blocks(2)
            pe.wait_ge(tile[2]["h_staged"], 1)
            nc.tensor.transpose(ps_h[0:D, 0:P], hst[:, :], ident[:, :]).then_inc(tile[2]["h_turned"], 1)
            for t in first_then_loop(pe, NT):
                first = isinstance(t, int)
                pe.wait_ge(tile[2]["ht_ready"], t + 1)
                carry_wait(pe)
                if not first:
                    pe.wait_ge(tile[2]["copied"], t)
                    carry_wait(pe)
                nc.tensor.matmul(ps_agg[0:D, 0:P], a2t[:, :], ht[:, :], start=True, stop=True)
                nc.tensor.matmul(ps_t[:, 0:D], ht[:, :], a1t[:, :], start=True, stop=True).then_inc(tile[2]["made"], 1)
                pe.wait_ge(tile[2]["h_staged"], t + 2)
                nc.tensor.transpose(ps_h[0:D, 0:P], hst[:, :], ident[:, :]).then_inc(tile[2]["h_turned"], 1)
                for r, (h, r0, n) in enumerate(BUILD):
                    if not first or r >= 2:
                        copied, each = ((s_even, EVEN), (s_odd, ODD))[r % 2]
                        pe.wait_ge(copied, t * each + r // 2)
                    nc.tensor.matmul(ps_wide[:, r % 2, 0:n * PAIR], ht[:, :],
                                     w2f[:, 2 * r0:2 * (r0 + n), :].rearrange("p r c -> p (r c)"),
                                     start=True, stop=True).then_inc(s_round, 1)
            pe.sem_inc(s_pp[1], 1)
            sum_edges(3)
            turn_blocks(3)
            sum_edges(4)
            turn_blocks(4)

        @block.vector
        def _(dve):
            V = nc.vector

            def normalise(n, i):
                xb, hb, cb = by_tile(cols(X, i, D)), by_tile(cols(H, i, D)), by_tile(cent[:, :])
                V.tensor_reduce(stat[:, 0, :], xb, X_AXIS, ALU.add)
                dve.drain()
                V.tensor_scalar(stat[:, 0, :], stat[:, 0, :], 1.0 / D, None, ALU.mult)
                dve.drain()
                V.tensor_tensor(cb, xb, over(stat[:, 0, :], D), ALU.subtract)
                dve.drain()
                V.tensor_tensor(by_tile(sq[:, :]), cb, cb, ALU.mult)
                dve.drain()
                V.tensor_reduce(stat[:, 1, :], by_tile(sq[:, :]), X_AXIS, ALU.add)
                dve.drain()
                V.tensor_scalar(stat[:, 1, :], stat[:, 1, :], 1.0 / D, EPS, ALU.mult, ALU.add).then_inc(s_var[n], 1)
                dve.wait_ge(s_std[n], i + 1)
                V.reciprocal(stat[:, 1:3, :], stat[:, 1:3, :])
                dve.drain()
                V.tensor_tensor(hb, cb, over(stat[:, 1, :], D), ALU.mult)
                dve.drain()
                V.tensor_scalar(hb, hb, 0.0, None, ALU.max)
                dve.drain()

            def sum_edges(s):
                q = sums[s]
                V.memset(big[0:64, 0:SW], 0.0)
                dve.sem_inc(q["slot_free"], SLOTS)
                dve.sem_inc(q["added"], 1)
                if s == 3:
                    dve.sem_inc(s_sc, 1)
                dve.drain()
                count = dve.alloc_register(f"dve_windows_{s}")
                dve.reg_mov(count, 0)
                at = dve.alloc_register(f"dve_at_{s}")
                with dve.Fori(0, STEPS) as i:
                    for k in range(SLOTS):
                        g = i * SLOTS + k
                        start = dve.value_load(meta[0:1, bass.ds(g * 2, 1)], min_val=0, max_val=N - 1)
                        windows = dve.value_load(meta[0:1, bass.ds(g * 2 + 1, 1)], min_val=1, max_val=NT)
                        dve.reg_mov(at, start)
                        V.tensor_copy(cur[:, :], drel[:, bass.ds(g * CH, CH)])
                        if s == 4:
                            dve.drain()
                        dve.wait_ge(q["gathered"][k], (i + 1) * (16 * CH))
                        rows = gbuf[:, k, :, 0:D]
                        if s < 3:
                            by = ew1_s if s == 0 else ew_s
                            V.tensor_tensor(rows, rows, by[:, bass.ds(g * CH, CH)].unsqueeze(2).to_broadcast([P, CH, D]), ALU.mult)
                        if s == 0:
                            V.tensor_copy(gbuf[:, k, :, D], ew_s[:, bass.ds(g * CH, CH)])
                            V.tensor_copy(gbuf[:, k, :, D + 2], lsrc[:, bass.ds(g * CH, CH)])
                        if s == 3:
                            V.tensor_copy(pick[:, :, :], par[:, :, bass.ds(g * CH, CH)].rearrange("p a c -> p c a"))
                            dve.drain()
                            V.tensor_tensor(own[:, :, :], gbuf[:, k, :, 0:PAIR].rearrange("p c (a d) -> p c a d", a=2)[:, :, :, D],
                                            pick[:, :, :], ALU.mult)
                        if s < 4:
                            dve.drain()
                        else:
                            carry_wait(dve)
                        with dve.Fori(0, windows) as w:
                            dve.reg_add(count, count, 1)
                            n = dve.snap(count)
                            a = dve.snap(at, min_val=0, max_val=NPAD)
                            V.tensor_tensor(onehot[:, :, :], iota[:, :].unsqueeze(1).to_broadcast([P, CH, WIN]),
                                            cur[:, :].unsqueeze(2).to_broadcast([P, CH, WIN]),
                                            ALU.is_equal).then_inc(q["onehot_ready"], 1)
                            if s == 3:
                                attend(k, n)
                            dve.drain()
                            V.tensor_scalar(cur[:, :], cur[:, :], float(-WIN), None, ALU.add)
                            dve.drain()
                            dve.wait_ge(q["sums_ready"], n)
                            into = big[0:CHN[s], bass.ds(a, WIN)]
                            V.tensor_tensor(into, into, ps_agg[0:CHN[s], 0:WIN], ALU.add).then_inc(q["added"], 1)
                            dve.reg_add(at, at, WIN)
                        dve.sem_inc(q["slot_free"], 1)
                    if s == 1:
                        for j in range(2):
                            t = 2 * i + j
                            dve.wait_ge(tile[1]["made"], t + 2)
                            V.tensor_copy(O[:, bass.ds(t * D, D)], ps_z[:, 0:D]).then_inc(tile[1]["copied"], 1)
                dve.drain()
                dve.sem_inc(q["all_added"], 1)

            def attend(k, n):
                dve.drain()
                for a in range(2):
                    dve.wait_ge(s_pp[a], n + 1 if a else n)
                    h = slice(4 * a, 4 * a + 4)
                    V.tensor_tensor(prod[:, h, :], ps_wide[:, a, :].rearrange("p (a b) -> p a b", a=4), onehot[:, h, :], ALU.mult)
                    dve.drain()
                    V.tensor_reduce(raw[:, h], prod[:, h, :], X_AXIS, ALU.add)
                dve.drain()
                V.tensor_tensor(raw[:, :], raw[:, :], own[:, :, 0], ALU.add)
                dve.drain()
                V.tensor_tensor(raw[:, :], raw[:, :], own[:, :, 1], ALU.add)
                dve.drain()
                V.tensor_scalar(score[:, :], raw[:, :], float(1.0 / np.sqrt(D)), 0.0, ALU.mult, ALU.max).then_inc(s_sc, 1)
                dve.wait_ge(s_att, n)
                V.scalar_tensor_tensor(att2[:, :], att[:, :], 0.0, att[:, :], ALU.is_gt, ALU.mult)
                dve.drain()
                V.tensor_tensor(att_p[:, :, :], pick[:, :, :], att2[:, :].unsqueeze(2).to_broadcast([P, CH, 2]), ALU.mult)
                dve.drain()
                V.tensor_tensor(msg2[:, :, :, :], gbuf[:, k, :, 0:PAIR].rearrange("p c (a d) -> p c a d", a=2)[:, :, :, 0:D],
                                att_p[:, :, :].unsqueeze(3).to_broadcast([P, CH, 2, D]), ALU.mult)
                dve.drain()
                V.tensor_tensor(msg[:, :, :], msg2[:, :, 0, :], msg2[:, :, 1, :], ALU.add).then_inc(s_msg, 1)

            V.memset(X[:, (NT - 1) * D:NT * D], 0.0)
            V.memset(comp0_s[:, :, :], 0.0)
            for t in (src_i, idx_a):
                V.memset(t[:, (NG - 1) * CH:IC], 0)
            V.memset(dst_i[:, (NG - 1) * CH:NG * CH], int(FAR))
            V.memset(nxt_i[:, (NG - 1) * CH:NG * CH], int(-2 * FAR))
            for t in (ew_s, two[:, 0, :]):
                V.memset(t[:, (NG - 1) * CH:NG * CH], 0.0)
            dve.drain()
            dve.sem_inc(s_pad, 1)
            V.memset(H[:, NT * D:FT * D], 0.0)
            V.memset(O[:, NT * D:FT * D], 0.0)
            V.memset(big[:, NPAD:SW], 0.0)
            V.memset(zdiag[:, :, :], 0.0)
            V.memset(w2f[D:D + 1, :, 0:D], 0.0)
            V.memset(ht[D:D + 1, :], 1.0)
            V.memset(ones[:, :], 1.0)
            V.memset(gbuf[:, :, :, D + 1], 1.0)
            V.memset(stat[:, :, :], 1.0)
            dve.wait_ge(s_iota, 1)
            V.tensor_copy(iota[:, :], iota_i[:, :])
            V.tensor_copy(pcol[:, :], pcol_i[:, :])
            dve.drain()
            V.tensor_scalar(ident[:, :], iota[:, :], pcol[:, 0:1], None, ALU.is_equal).then_inc(s_const, 1)
            dve.wait_ge(s_x, 32)
            dve.drain()
            with dve.Fori(0, NB) as i:
                normalise(0, i)
            dve.sem_inc(tile[0]["h_ready"], 1)

            dve.wait_ge(s_rows, 48)
            V.tensor_reduce(mm_f[:, :, 0], drow_i, X_AXIS, ALU.min)
            V.tensor_reduce(mm_f[:, :, 1], drow_i, X_AXIS, ALU.max)
            dve.drain()
            V.tensor_tensor(mm_w[:, :], mm_f[:, :, 1], mm_f[:, :, 0], ALU.subtract)
            V.tensor_copy(mm_i[:, :, 0], mm_f[:, :, 0])
            dve.drain()
            V.tensor_scalar(mm_w[:, :], mm_w[:, :], 7, None, ALU.arith_shift_right)
            dve.drain()
            V.tensor_scalar(mm_i[:, :, 1], mm_w[:, :], 1.0, None, ALU.add).then_inc(s_mm, 1)

            dve.wait_ge(s_src, 48)
            V.tensor_scalar(tmp_i, src_i[:, :], P - 1, None, ALU.bitwise_and)
            V.tensor_scalar(idx_h[:, :], src_i[:, :], 7, None, ALU.arith_shift_right)
            dve.drain()
            V.scalar_tensor_tensor(idx_h[:, :], tmp_i, float(NT), idx_h[:, :], ALU.mult, ALU.add)
            dve.wait_ge(s_et16, 48)
            V.scalar_tensor_tensor(idx_a[:, :], src_i[:, :], float(R0), idx_a[:, :], ALU.mult, ALU.add)
            dve.drain()
            dve.sem_inc(s_idx, 1)

            for i in first_then_loop(dve, NT // 2):
                for j in range(2):
                    dve.wait_ge(tile[0]["made"], 2 * i + j + 2)
                    if not isinstance(i, int):
                        dve.wait_ge(s_t0[j], i * 16)
                    V.tensor_copy(t0buf[:, j, :], ps_wide[:, j, :]).then_inc(tile[0]["copied"], 1)

            dve.wait_ge(s_dst, 48)
            dve.wait_ge(s_nxt, 48)
            V.tensor_copy(dst_f, dst_i)
            V.tensor_copy(nxt_f, nxt_i)
            dve.drain()
            V.tensor_tensor(tmp_f, dst_f, nxt_f, ALU.is_gt)
            dve.drain()
            V.tensor_reduce(flag[:, :], tmp_f, X_AXIS, ALU.add).then_inc(s_flagp, 1)
            dve.drain()
            V.tensor_tensor(tmp_f, dst_f, nxt_f, ALU.not_equal)
            dve.drain()
            V.tensor_tensor(lsrc, tmp_f, src_i[:, 0:NG * CH], ALU.mult)
            dve.wait_ge(s_meta_r, 32)
            V.tensor_tensor(drel[:, :].rearrange("p (g c) -> p g c", c=CH), dst_f.rearrange("p (g c) -> p g c", c=CH),
                            bounds_b.rearrange("p (g w) -> p g w", w=2)[:, :, 0].unsqueeze(2).to_broadcast([P, NG, CH]),
                            ALU.subtract)
            dve.wait_ge(s_flags, 1)
            V.tensor_scalar(flag_i[:, :], ps_agg[0:1, 0:1], 0.0, None, ALU.is_gt).then_inc(s_flag, 1)

            for r, o0 in enumerate(range(0, D, 5)):
                n = min(5, D - o0)
                dve.wait_ge(s_w2p, r + 1)
                V.tensor_copy(w2f[0:D, :, o0:o0 + n],
                              ps_wide[0:D, r % 2, 0:n * R2].rearrange("p (o r) -> p r o", r=R2)).then_inc(s_w2c, 1)
            dve.wait_ge(s_w2p, 8)
            V.tensor_copy(w2f[:, :, D], ps_z[0:D + 1, 0:R2])
            V.tensor_tensor(w02[:, :], w1_s[:, 0, :], w1_s[:, 2, :], ALU.subtract)
            dve.sem_inc(tile[1]["copied"], 1)
            for e in range(5):
                dve.sem_inc(blk[e]["read"], 1)
            dve.wait_ge(s_ew, 48)
            dve.wait_ge(s_ew1, 48)
            dve.drain()

            sum_edges(0)

            unsorted = dve.value_load(flag_i[0:1, 0:1], min_val=0, max_val=1)
            with dve.If(unsorted > 0):
                V.memset(last_e[:, :], 0.0)
                V.memset(base[:, :], 0.0)
                for c in range(CH):
                    V.tensor_scalar(key[:, c * P:(c + 1) * P], iota[:, :], float(c * P + 1), None, ALU.add)
                dve.drain()
                dve.sem_inc(s_lused, 1)
                with dve.Fori(0, NG) as g:
                    V.tensor_scalar(base[:, :], base[:, :], float(E - GROUP), None, ALU.min)
                    V.tensor_copy(node[:, :], pcol[:, :])
                    dve.drain()
                    dve.wait_ge(s_lrow, g * 16 + 16)
                    carry_wait(dve)
                    with dve.Fori(0, NT) as t:
                        V.scalar_tensor_tensor(keyed, trow, node[:, 0:1], key, ALU.is_equal, ALU.mult)
                        dve.drain()
                        V.tensor_reduce(found[:, 0:1], keyed, X_AXIS, ALU.max)
                        dve.drain()
                        V.scalar_tensor_tensor(found[:, 1:2], found[:, 0:1], 0.0, base[:, :], ALU.is_gt, ALU.mult)
                        dve.drain()
                        V.tensor_tensor(found[:, 0:1], found[:, 0:1], found[:, 1:2], ALU.add)
                        V.tensor_scalar(node[:, :], node[:, :], float(P), None, ALU.add)
                        dve.drain()
                        V.tensor_tensor(last_e[:, bass.ds(t, 1)], last_e[:, bass.ds(t, 1)], found[:, 0:1], ALU.max)
                        dve.drain()
                    V.tensor_scalar(base[:, :], base[:, :], float(GROUP), None, ALU.add)
                    dve.drain()
                    dve.sem_inc(s_lused, 1)
                with dve.Fori(0, NT) as t:
                    V.tensor_scalar(lcol[:, :], last_e[:, bass.ds(t, 1)], -1.0, 0.0, ALU.add, ALU.max).then_inc(s_lcol, 1)
                    dve.wait_ge(s_lgot, t * 16 + 16)
                    carry_wait(dve)
                    V.tensor_copy(last_e[:, bass.ds(t, 1)], lsrc_i[:, :])
                    dve.drain()

            for i in first_then_loop(dve, NB):
                xb = by_tile(cols(X, i, D))
                dve.wait_ge(blk[0]["turned"], i + 1)
                V.tensor_tensor(xb, xb, turned[:, :, 0:D], ALU.add)
                V.tensor_scalar(stat[:, 2, :], turned[:, :, D], 1e-12, None, ALU.max)
                V.tensor_scalar(stat[:, 3, :], turned[:, :, D], 0.0, None, ALU.is_gt)
                V.tensor_copy(cols(deg, i, 1), turned[:, :, D + 1])
                V.tensor_copy(cols(last_f, i, 1), turned[:, :, D + 2]).then_inc(blk[0]["read"], 1)
                dve.drain()
                normalise(1, i)
                V.tensor_tensor(cols(dinv, i, 1), stat[:, 2, :], stat[:, 3, :], ALU.mult)
                dve.drain()
                if not isinstance(i, int):
                    dve.wait_ge(blk[0]["u_stored"], i * 16)
                V.tensor_tensor(by_tile(ubuf[:, :]), by_tile(cols(H, i, D)), over(cols(dinv, i, 1), D),
                                ALU.mult).then_inc(blk[0]["u_ready"], 1)
            dve.sem_inc(tile[1]["h_ready"], 1)
            with dve.If(unsorted > 0):
                V.tensor_copy(last_f[:, :], last_e[:, :])
                dve.drain()
            V.tensor_copy(li_a[:, :], last_f[:, :])
            dve.drain()
            V.tensor_scalar(li_b[:, :], li_a[:, :], P - 1, None, ALU.bitwise_and)
            V.tensor_scalar(last_i[:, :], li_a[:, :], 7, None, ALU.arith_shift_right)
            dve.drain()
            V.scalar_tensor_tensor(last_i[:, :], li_b[:, :], float(NT), last_i[:, :], ALU.mult, ALU.add).then_inc(s_last, 1)

            sum_edges(1)
            for i in first_then_loop(dve, NB):
                db, ob = over(cols(dinv, i, 1), D), by_tile(cols(O, i, D))
                dve.wait_ge(blk[1]["turned"], i + 1)
                V.scalar_tensor_tensor(by_tile(cent[:, :]), turned[:, :, 0:D], -1.0, db, ALU.mult, ALU.mult)
                V.scalar_tensor_tensor(by_tile(sq[:, :]), zed, -1.0, db, ALU.mult, ALU.mult).then_inc(blk[1]["read"], 1)
                dve.drain()
                if not isinstance(i, int):
                    dve.wait_ge(blk[1]["u_stored"], i * 16)
                V.tensor_tensor(by_tile(ubuf[:, :]), by_tile(cent[:, :]), db, ALU.mult).then_inc(blk[1]["u_ready"], 1)
                V.tensor_tensor(ob, ob, by_tile(sq[:, :]), ALU.add)
                dve.drain()

            dve.wait_ge(s_et86, 48)
            V.tensor_scalar(lsrc.bitcast(I32), idx_a[:, 0:NG * CH], 1, None, ALU.bitwise_and)
            dve.drain()
            V.tensor_copy(ew1_s, lsrc.bitcast(I32))
            dve.drain()
            V.tensor_copy(lsrc, ew1_s)
            V.tensor_scalar(ew1_s, ew1_s, -1.0, 1.0, ALU.mult, ALU.add)
            V.tensor_scalar(idx_a[:, :], idx_a[:, :], 1, None, ALU.arith_shift_right)
            dve.drain()
            V.scalar_tensor_tensor(idx_a[:, :], src_i[:, :], float(RP), idx_a[:, :], ALU.mult, ALU.add).then_inc(s_idx2, 1)

            sum_edges(2)
            with dve.Fori(0, NB) as i:
                db, ob, xb = over(cols(dinv, i, 1), D), by_tile(cols(O, i, D)), by_tile(cols(X, i, D))
                dve.wait_ge(blk[2]["turned"], i + 1)
                V.scalar_tensor_tensor(by_tile(sq[:, :]), zed, -2.0, db, ALU.mult, ALU.mult).then_inc(blk[2]["read"], 1)
                dve.drain()
                V.tensor_tensor(by_tile(sq[:, :]), by_tile(sq[:, :]), ob, ALU.add)
                dve.drain()
                V.scalar_tensor_tensor(xb, by_tile(sq[:, :]), 0.0, xb, ALU.max, ALU.add)
                dve.drain()
                normalise(2, i)
                dve.sem_inc(blk[2]["u_ready"], 1)
            dve.sem_inc(tile[2]["h_ready"], 1)
            for t in first_then_loop(dve, NT):
                for r, (h, r0, n) in enumerate(BUILD):
                    if r % 2 == 0:
                        continue
                    half0, half_n = HALF[h]
                    rows = tbuf[:, h, 0:half_n * ROW2].rearrange("p (r c) -> p r c", c=ROW2)
                    if not isinstance(t, int):
                        dve.wait_ge(s_t2[h], t * 16)
                    dve.wait_ge(s_round, t * NBUILD + r + 1)
                    V.tensor_copy(rows[:, r0 - half0:r0 - half0 + n, 0:PAIR],
                                  ps_wide[:, r % 2, 0:n * PAIR].rearrange("p (r c) -> p r c", c=PAIR)).then_inc(s_odd, 1)

            sum_edges(3)
            V.tensor_scalar(mask[:, :], deg[:, :], 0.0, None, ALU.is_gt)
            dve.wait_ge(s_curr, 16 * NT)
            dve.drain()
            with dve.Fori(0, NB) as i:
                xb = by_tile(cols(X, i, D))
                dve.wait_ge(s_cz, i + 1)
                V.tensor_copy(by_tile(sq[:, :]), zed)
                dve.drain()
                V.tensor_tensor(by_tile(sq[:, :]), by_tile(sq[:, :]), turned[:, :, 0:D], ALU.add).then_inc(blk[3]["read"], 1)
                dve.drain()
                V.tensor_tensor(by_tile(sq[:, :]), by_tile(sq[:, :]), over(cols(mask, i, 1), D), ALU.mult)
                dve.drain()
                V.scalar_tensor_tensor(xb, by_tile(sq[:, :]), 0.0, xb, ALU.max, ALU.add)
                dve.drain()
                normalise(3, i)
                dve.sem_inc(blk[3]["u_ready"], 1)

            sum_edges(4)
            V.tensor_scalar(mask[:, :], deg[:, :], 1.0, None, ALU.max)
            dve.drain()
            V.reciprocal(mask[:, :], mask[:, :])
            dve.drain()
            with dve.Fori(0, NB) as i:
                xb = by_tile(cols(X, i, D))
                dve.wait_ge(blk[4]["turned"], i + 1)
                V.tensor_tensor(by_tile(sq[:, :]), turned[:, :, 0:D], over(cols(mask, i, 1), D), ALU.mult).then_inc(blk[4]["read"], 1)
                dve.drain()
                V.tensor_tensor(xb, xb, by_tile(sq[:, :]), ALU.add).then_inc(blk[4]["u_ready"], 1)
                dve.drain()


INS = ["x", "src", "dst", "edge_type_16", "edge_type_86", "edge_weight", "edge_weight1", "L0_gnn_weight",
       "L0_gnn_w_comp", "L1_gnn_W", "L1_gnn_b", "L2_gnn_weight", "L2_gnn_w_comp", "L2_gnn_self_loop_weight",
       "L2_gnn_A1_w", "L2_gnn_A1_b", "L2_gnn_A2_w", "L2_gnn_A2_b", "L2_gnn_rel_emb"]


def kernel(**inputs):
    import concourse.bacc as bacc
    from concourse.bass_utils import run_bass_kernel_spmd

    nc = bacc.Bacc("TRN2", target_bir_lowering=False, num_devices=1)
    arrays, args = {}, []
    for name in INS:
        a = np.ascontiguousarray(inputs[name])
        arrays[f"in_{name}"] = a
        args.append(nc.dram_tensor(f"in_{name}", a.shape, mybir.dt.from_np(a.dtype), kind="ExternalInput").ap())
    out = nc.dram_tensor("out", (N, D), F32, kind="ExternalOutput").ap()
    gnn_kernel(nc, *args, out)
    r = run_bass_kernel_spmd(nc, [arrays], core_ids=[0])
    return r.results[0]["out"]
```

```python
from contextlib import ExitStack

import numpy as np
import concourse.bass as bass
from concourse import mybir
from concourse.alu_op_type import AluOpType as ALU

F32 = mybir.dt.float32
I32 = mybir.dt.int32
ACT = mybir.ActivationFunctionType
X_AXIS = mybir.AxisListType.X

P = 128
N = 12500
E = 212500
D = 32
R0, B0 = 16, 8
R2, B2 = 86, 16
NT = (N + P - 1) // P
NPAD = NT * P
TAIL = N - (NT - 1) * P
CH = 8
GROUP = CH * P
NG = (E + GROUP - 1) // GROUP
SLOTS = 4
STEPS = NG // SLOTS
PER_SUM = SLOTS + NG
LAST = E - (NG - 1) * GROUP
LP, LC = LAST // CH, LAST % CH
IC = (NG + SLOTS) * CH
WIN = 128
SW = NPAD + WIN
HG = NG // 2
BT = 14
NB = NT // BT
FT = 2 * STEPS
RP = R2 // 2
PAIR = 2 * (D + 1)
ROW2 = PAIR + D
HALF = [(0, 21), (21, 22)]
WB_DMAS = 12
BUILD = [(0, 0, 7), (0, 7, 7), (0, 14, 7), (1, 21, 7), (1, 28, 7), (1, 35, 7), (1, 42, 1)]
NBUILD = len(BUILD)
EVEN, ODD = 4, 3
HALF_DONE = [(2, 1), (EVEN, ODD)]
EPS = 1e-5
FAR = -1.0e6


def gnn_kernel(nc, x, src, dst, et16, et86, ew, ew1, w0, comp0, w1, b1, w2, comp2, selfw,
               a1w, a1b, a2w, a2b, rel, out):
    def scratch(name, shape, dt=F32):
        return nc.dram_tensor(name, shape, dt, kind="Internal").ap()

    table0 = scratch("table0", (NPAD * R0, D))
    table2 = scratch("table2", (NPAD * RP, ROW2))
    nodes = [scratch(f"nodes{i}", (NPAD, D)) for i in range(4)]
    meta_d = scratch("meta_d", (NG, 2), I32)

    ctx = ExitStack()
    with ctx:
        def sb(name, shape, dt=F32):
            return ctx.enter_context(nc.sbuf_tensor(name, shape, dt))

        def sem(name):
            return ctx.enter_context(nc.semaphore(name))

        src_i = sb("src_i", [P, IC], I32)
        idx_a = sb("idx_a", [P, IC], I32)
        idx_h = sb("idx_h", [P, IC], I32)
        ew_s = sb("ew_s", [P, NG * CH])
        two = sb("two", [P, 2, NG * CH])
        ew1_s = two[:, 0, :]
        lsrc = two[:, 1, :]
        par = two
        drel = sb("drel", [P, (NG + 1) * CH])
        meta = sb("meta", [1, (NG + 1) * 2], I32)
        X = sb("X", [P, NT * D])
        H = sb("H", [P, FT * D])
        O = sb("O", [P, FT * D])
        deg = sb("deg", [P, NT])
        dinv = sb("dinv", [P, NT])
        last_i = sb("last_i", [P, NT], I32)
        big = sb("big", [P, SW])
        gbuf = sb("gbuf", [P, SLOTS, CH, ROW2])
        ibuf = sb("ibuf", [P, SLOTS, CH], I32)
        onehot = sb("onehot", [P, CH, WIN])
        prod = sb("prod", [P, CH, WIN])
        cur = sb("cur", [P, CH])
        score = sb("score", [P, CH])
        att = sb("att", [P, CH])
        msg = sb("msg", [P, CH, D])
        msg2 = sb("msg2", [P, CH, 2, D])
        att_p = sb("att_p", [P, CH, 2])
        parts = sb("parts", [P, CH, D + 2])
        ywin = sb("ywin", [D, WIN])
        yw = sb("yw", [WIN, D])
        tbuf = sb("tbuf", [P, 2, HALF[1][1] * ROW2])
        onehots = [onehot, tbuf[:, 0, 0:CH * WIN].rearrange("p (c w) -> p c w", w=WIN)]
        onehot_t = prod
        stage = tbuf[0:36, 0, 0:BT * P]
        t0buf = tbuf[:, 0, 0:2 * R0 * D].rearrange("p (a n) -> p a n", a=2)
        ubuf = sb("ubuf", [P, BT * D])
        sq = sb("sq", [P, BT * D])
        cent = sb("cent", [P, BT * D])
        stat = sb("stat", [P, 4, BT])
        cst = sb("cst", [P, BT * D])
        hst = sb("hst", [P, D])
        ht = sb("ht", [D + 1, P])
        iota_i = sb("iota_i", [P, WIN], I32)
        iota = sb("iota", [P, WIN])
        pcol_i = sb("pcol_i", [P, 1], I32)
        pcol = sb("pcol", [P, 1])
        ident = sb("ident", [P, P])
        ones = sb("ones", [P, P])
        w0_s = prod[0:B0, :, :].rearrange("p a b -> p (a b)")
        comp0_s = sb("comp0_s", [B0, 2, D])
        w0f = sb("w0f", [D, R0 * D])
        w1_s = sb("w1_s", [D, 3, D])
        w02 = sb("w02", [D, D])
        b1_s = sb("b1_s", [1, D])
        w2_s = onehot[0:B2, :, :].rearrange("p a b -> p (a b)").rearrange("p (i o) -> p i o", o=D)
        comp2_s = sb("comp2_s", [B2, R2])
        w2f = sb("w2f", [D + 1, R2, D + 1])
        self_s = sb("self_s", [D, D])
        a1 = sb("a1", [D, D + 1])
        a1t = sb("a1t", [D + 1, D])
        a2t = sb("a2t", [D + 1, D])
        relt = sb("relt", [D, R2])
        drow_i = tbuf[0:HG, 0, 0:2 * GROUP].bitcast(I32).rearrange("p (h n) -> p h n", h=2)
        drow = tbuf[0:HG, 1, 0:2 * GROUP].rearrange("p (h n) -> p h n", h=2)
        dst_f = big[:, 0:NG * CH]
        dst_i = big[:, 2048:2048 + NG * CH].bitcast(I32)
        nxt_i = big[:, 4096:4096 + NG * CH].bitcast(I32)
        nxt_f = big[:, 6144:6144 + NG * CH]
        tmp_f = big[:, 8192:8192 + NG * CH]
        bounds_b = big[:, 10240:10240 + 2 * NG].bitcast(I32)
        tmp_i = tbuf[:, 0, 0:0 + IC].bitcast(I32)
        mm_f = sb("mm_f", [HG, 2, 2])
        mm_i = sb("mm_i", [HG, 2, 2], I32)
        mm_w = sb("mm_w", [HG, 2], I32)
        flag = sb("flag", [P, 1])
        mask = sb("mask", [P, NT])
        raw = sb("raw", [P, CH])
        att2 = sb("att2", [P, CH])
        xh = sb("xh", [P, D])
        node = sb("node", [P, 1])
        lsrc_i = sb("lsrc_i", [P, 1], I32)
        flag_i = sb("flag_i", [1, 1], I32)
        last_f = sb("last_f", [P, NT])
        li_a = sb("li_a", [P, NT], I32)
        li_b = sb("li_b", [P, NT], I32)
        key = prod[:, :, :].rearrange("p a b -> p (a b)")
        keyed = onehot[:, :, :].rearrange("p a b -> p (a b)")
        trow = tbuf[:, 0, 0:GROUP].bitcast(I32)
        base = sb("base", [P, 1])
        found = sb("found", [P, 2])
        last_e = sb("last_e", [P, NT])
        lcol = sb("lcol", [P, 1], I32)

        ps_wide = ctx.enter_context(nc.psum_tensor("ps_wide", [P, 4, 512], F32))
        ps_agg = ctx.enter_context(nc.psum_tensor("ps_agg", [P, 512], F32))
        ps_t = ctx.enter_context(nc.psum_tensor("ps_t", [P, 512], F32))
        ps_z = ctx.enter_context(nc.psum_tensor("ps_z", [P, 512], F32))
        ps_h = ctx.enter_context(nc.psum_tensor("ps_h", [P, 512], F32))
        turned = ps_t[:, 0:BT * 36].rearrange("p (t c) -> p t c", c=36)
        wide = ps_wide[:, :, :].rearrange("p a b -> p (a b)")
        zed = ps_z[:, 0:BT * D].rearrange("p (t c) -> p t c", c=D)
        y_own = [ps_wide[:, 2, 0:CH * D].rearrange("p (c d) -> p c d", d=D),
                 ps_h[:, 0:CH * D].rearrange("p (c d) -> p c d", d=D)]


        s_x = sem("x_loaded")
        s_src = sem("sources_loaded")
        s_et16 = sem("types16_loaded")
        s_dst = sem("targets_and_next_ones_loaded")
        s_ew = sem("both_weights_loaded")
        s_et86 = sem("types86_loaded")
        s_rows = sem("target_rows_loaded")
        s_wa = sem("first_layers_weights_loaded")
        s_wb = sem("later_layers_weights_loaded")
        s_pad = sem("padding_set")
        s_iota = sem("iota_made")
        s_const = sem("constants_made")
        s_mm = sem("group_bounds_made")
        s_meta_w = sem("group_bounds_written")
        s_meta_r = sem("group_bounds_read")
        s_idx = sem("row_numbers_known")
        s_idx2 = sem("table2_row_numbers_known")
        s_w0p = sem("w0_product")
        s_w0c = sem("w0_copied")
        s_flagp = sem("unsorted_counts_ready")
        s_flags = sem("unsorted_counts_summed")
        s_flag = sem("unsorted_flag_ready")
        s_lused = sem("target_row_used")
        s_lrow = sem("target_row_loaded")
        s_lcol = sem("last_edges_known")
        s_lgot = sem("last_source_gathered")
        s_last = sem("last_rows_known")
        s_curr = sem("last_sources_rows_gathered")
        s_w2p = sem("w2_product")
        s_w2c = sem("w2_copied")
        s_ypad = sem("yhat_padding_set")
        s_out = sem("output_written")
        s_carry = sem("waits_carried")

        tile = [{n: sem(f"tile{f}_{n}") for n in ("h_ready", "h_staged", "h_turned", "ht_ready", "made", "copied")}
                for f in range(3)]
        s_t0 = [sem("table0_stored_0"), sem("table0_stored_1")]
        s_t2 = [sem("table2_stored_0"), sem("table2_stored_1")]
        s_round = sem("table2_round_made")
        s_even = sem("table2_even_products_copied")
        s_odd = sem("table2_odd_products_copied")
        blk = [{n: sem(f"block{e}_{n}") for n in ("staged", "turned", "read", "u_ready", "u_stored")[:4 if e == 4 else 5]}
               for e in range(5)]
        s_var = [sem(f"variance_ready_{n}") for n in range(4)]
        s_std = [sem(f"deviation_ready_{n}") for n in range(4)]
        s_cst = sem("last_rows_staged")
        s_ct = sem("last_rows_turned")
        s_ctc = sem("last_rows_turned_copied")
        s_cz = sem("self_product")
        s_free = sem("gather_slot_free")
        s_rows_known = sem("gather_row_numbers_laid_out")
        sums = [{n: sem(f"sum{s}_{n}") for n in ("onehot_ready", "sums_ready", "all_added", "added")[:3 if s == 3 else 4]}
                for s in range(5)]
        for s in range(5):
            sums[s]["gathered"] = [sem(f"sum{s}_gathered_{k}") for k in range(SLOTS)]
        attn, more = [{n: sem(f"attention_{m}_{n}") for n in ("y_window", "turned", "laid_out", "y_own", "scores",
                                                            "tanh", "messages")} for m in ("first", "more")]
        more["onehot_ready"] = sem("attention_more_onehot_ready")
        more["sums_ready"] = sem("attention_more_sums_ready")

        WIDTH = [D, D, D, ROW2, D]
        CHN = [D + 3, D, D, D, D]
        IDX = [idx_a, idx_h, idx_h, idx_a, idx_h]
        TABLE = [table0, nodes[0], nodes[1], table2, nodes[3]]
        X3 = X[:, :].rearrange("p (t c) -> p t c", c=D)

        def cols(t, i, w):
            return t[:, bass.ds(i * (BT * w), BT * w)]

        def by_tile(a, c=D):
            return a.rearrange("p (t c) -> p t c", c=c)

        def over(a, n):
            return a.unsqueeze(2).to_broadcast([P, a.shape[1], n])

        def carry_wait(eng):
            eng.sem_inc(s_carry, 1)

        def first_then_loop(eng, n):
            yield 0
            with eng.Fori(1, n) as i:
                yield i

        block = ctx.enter_context(nc.Block())

        @block.sync
        def _(sp):
            def edge_array(to, a, done, n=E):
                c0 = (NG - 1) * CH
                sp.dma_start(to[:, 0:c0].rearrange("p (g c) -> p g c", c=CH),
                             a[0:(NG - 1) * GROUP].rearrange("(g p c) -> p g c", p=P, c=CH)).then_inc(done, 16)
                at = (NG - 1) * GROUP
                full, rest = (n - at) // CH, (n - at) % CH
                sp.dma_start(to[0:full, c0:c0 + CH],
                             a[at:at + full * CH].rearrange("(p c) -> p c", c=CH)).then_inc(done, 16)
                sp.dma_start(to[full:full + 1, c0:c0 + rest],
                             a[at + full * CH:n].rearrange("(o c) -> o c", o=1)).then_inc(done, 16)

            sp.wait_ge(s_pad, 1)
            sp.dma_start(X3[:, 0:NT - 1, :], x[0:(NT - 1) * P, :].rearrange("(t p) c -> p t c", p=P)).then_inc(s_x, 16)
            sp.dma_start(X3[0:TAIL, NT - 1, :], x[(NT - 1) * P:N, :]).then_inc(s_x, 16)
            sp.dma_start(w0_s[:, :].rearrange("b (i o) -> b i o", o=D),
                         w0.rearrange("b i o -> (b i o)").rearrange("(i b o) -> b i o", b=B0, o=D)).then_inc(s_wa, 16)
            turned0 = comp0.rearrange("r b -> b r")
            sp.dma_start(comp0_s[:, 0, 0:R0], turned0, allow_slow_non_contiguous=True).then_inc(s_wa, 16)
            sp.dma_start(comp0_s[:, 1, R0:D], turned0, allow_slow_non_contiguous=True).then_inc(s_wa, 16)
            edge_array(src_i, src, s_src)
            edge_array(idx_a, et16, s_et16)
            for h in range(2):
                rows = HG - h
                sp.dma_start(drow_i[0:rows, h, :],
                             dst[h * HG * GROUP:(h * HG + rows) * GROUP].rearrange("(p n) -> p n", n=GROUP)).then_inc(s_rows, 16)
            sp.dma_start(drow_i[HG - 1:HG, 1, :], dst[E - GROUP:E].rearrange("(p n) -> p n", p=1)).then_inc(s_rows, 16)
            edge_array(dst_i, dst, s_dst)
            edge_array(nxt_i, dst[1:E], s_dst, E - 1)
            edge_array(ew1_s, ew1.rearrange("e o -> (e o)"), s_ew)
            edge_array(ew_s, ew, s_ew)
            sp.dma_start(w1_s[:, :, :], w1.rearrange("k i o -> i k o")).then_inc(s_wb, 16)
            sp.dma_start(b1_s[:, :], b1.rearrange("(a c) -> a c", a=1)).then_inc(s_wb, 16)
            sp.dma_start(w2_s[:, :, :], w2).then_inc(s_wb, 16)
            sp.dma_start(comp2_s[:, :], comp2.rearrange("r b -> b r"), allow_slow_non_contiguous=True).then_inc(s_wb, 16)
            sp.dma_start(self_s[:, :], selfw).then_inc(s_wb, 16)
            sp.dma_start(a1[:, 0:D], a1w).then_inc(s_wb, 16)
            sp.dma_start(a1[:, D:D + 1], a1b.rearrange("(k a) -> k a", a=1), allow_slow_non_contiguous=True).then_inc(s_wb, 16)
            for t, w, b in ((a1t, a1w, a1b), (a2t, a2w, a2b)):
                sp.dma_start(t[0:D, :], w.rearrange("k i -> i k"), allow_slow_non_contiguous=True).then_inc(s_wb, 16)
                sp.dma_start(t[D:D + 1, :], b.rearrange("(a k) -> a k", a=1)).then_inc(s_wb, 16)
            sp.dma_start(relt[:, :], rel.rearrange("r k -> k r"), allow_slow_non_contiguous=True).then_inc(s_wb, 16)

            sp.wait_ge(s_mm, 1)
            sp.dma_start(meta_d.rearrange("(h p) w -> p h w", h=2), mm_i[:, :, :]).then_inc(s_meta_w, 16)
            sp.wait_ge(s_meta_w, 16)
            sp.dma_start(meta[:, 0:2 * NG], meta_d.rearrange("g w -> (g w)").rearrange("(a n) -> a n", a=1)).then_inc(s_meta_r, 16)
            sp.dma_start(bounds_b, meta_d.rearrange("g w -> (g w)").partition_broadcast(P)).then_inc(s_meta_r, 16)

            with sp.Fori(0, NT // 2) as i:
                for j in range(2):
                    sp.wait_ge(tile[0]["copied"], 2 * i + j + 1)
                    sp.dma_start(table0[bass.ds(i * (2 * P * R0) + j * P * R0, P * R0), :].rearrange("(p r) c -> p (r c)", p=P),
                                 t0buf[:, j, :]).then_inc(s_t0[j], 16)

            sp.wait_ge(s_flag, 1)
            unsorted = sp.value_load(flag_i[0:1, 0:1], min_val=0, max_val=1)
            with sp.If(unsorted > 0):
                with sp.Fori(0, NG - 1) as g:
                    sp.wait_ge(s_lused, g + 1)
                    sp.dma_start(trow, dst[bass.ds(g * GROUP, GROUP)].partition_broadcast(P)).then_inc(s_lrow, 16)
                sp.wait_ge(s_lused, NG)
                sp.dma_start(trow, dst[E - GROUP:E].partition_broadcast(P)).then_inc(s_lrow, 16)

            def store_nodes(e, to, of):
                view = nodes[to].rearrange("(p t) c -> p (t c)", p=P)
                with sp.Fori(0, NB) as i:
                    sp.wait_ge(blk[e]["u_ready"], i + 1)
                    sp.dma_start(view[:, bass.ds(i * (BT * D), BT * D)], of(i)).then_inc(blk[e]["u_stored"], 16)

            store_nodes(0, 0, lambda i: ubuf[:, :])
            sp.wait_ge(sums[0]["all_added"], 1)
            edge_array(idx_a, et86, s_et86)
            store_nodes(1, 1, lambda i: ubuf[:, :])
            store_nodes(2, 2, lambda i: cols(H, i, D))
            with sp.Fori(0, NT) as t:
                for h in range(2):
                    sp.wait_ge(s_even, EVEN * t + HALF_DONE[h][0])
                    carry_wait(sp)
                    sp.wait_ge(s_odd, ODD * t + HALF_DONE[h][1])
                    carry_wait(sp)
                    r0, n = HALF[h]
                    view = table2[bass.ds(t * (P * RP), P * RP), :].rearrange("(p r) c -> p (r c)", p=P)
                    sp.dma_start(view[:, r0 * ROW2:(r0 + n) * ROW2], tbuf[:, h, 0:n * ROW2]).then_inc(s_t2[h], 16)
            store_nodes(3, 3, lambda i: cols(H, i, D))
            sp.wait_ge(blk[4]["u_ready"], NB)
            sp.dma_start(out[0:(NT - 1) * P, :].rearrange("(t p) c -> p t c", p=P), X3[:, 0:NT - 1, :]).then_inc(s_out, 16)
            sp.dma_start(out[(NT - 1) * P:N, :], X3[0:TAIL, NT - 1, :]).then_inc(s_out, 16)
            sp.wait_ge(s_out, 32)

        @block.gpsimd
        def _(pool):
            nc.gpsimd.iota(iota_i[:, :], [[1, WIN]], base=0, channel_multiplier=0)
            nc.gpsimd.iota(pcol_i[:, :], [[1, 1]], base=0, channel_multiplier=1).then_inc(s_iota, 1)


            def gather_rows(s):
                q = sums[s]
                with pool.Fori(0, STEPS) as i:
                    for k in range(SLOTS):
                        n = s * PER_SUM + i * SLOTS + k + 1
                        pool.wait_ge(s_free, n)
                        pool.wait_ge(s_rows_known, n)
                        carry_wait(pool)
                        for c in range(CH):
                            nc.gpsimd.indirect_dma_start(
                                out=gbuf[:, k, c, 0:WIDTH[s]], out_offset=None, in_=TABLE[s],
                                in_offset=bass.IndirectOffsetOnAxis(ap=ibuf[:, k, c:c + 1], axis=0),
                            ).then_inc(q["gathered"][k], 16)

            for j in range(2):
                pool.wait_ge(s_t0[j], 16 * (NT // 2))
            gather_rows(0)
            pool.wait_ge(s_flag, 1)
            unsorted = pool.value_load(flag_i[0:1, 0:1], min_val=0, max_val=1)
            with pool.If(unsorted > 0):
                with pool.Fori(0, NT) as t:
                    pool.wait_ge(s_lcol, t + 1)
                    carry_wait(pool)
                    nc.gpsimd.indirect_dma_start(
                        out=lsrc_i[:, :], out_offset=None, in_=src.rearrange("(e o) -> e o", o=1),
                        in_offset=bass.IndirectOffsetOnAxis(ap=lcol[:, 0:1], axis=0)).then_inc(s_lgot, 16)
            pool.wait_ge(blk[0]["u_stored"], 16 * NB)
            gather_rows(1)
            pool.wait_ge(blk[1]["u_stored"], 16 * NB)
            gather_rows(2)
            pool.wait_ge(blk[2]["u_stored"], 16 * NB)
            pool.wait_ge(s_last, 1)
            for t in range(NT):
                nc.gpsimd.indirect_dma_start(
                    out=O[:, t * D:(t + 1) * D], out_offset=None, in_=nodes[2],
                    in_offset=bass.IndirectOffsetOnAxis(ap=last_i[:, t:t + 1], axis=0)).then_inc(s_curr, 16)
            for h in range(2):
                pool.wait_ge(s_t2[h], 16 * NT)
            gather_rows(3)
            pool.wait_ge(blk[3]["u_stored"], 16 * NB)
            gather_rows(4)

        @block.scalar
        def _(act):
            def turn_tile(f, t):
                s = tile[f]
                act.wait_ge(s["h_turned"], t + 1)
                nc.scalar.copy(hst[:, :], H[:, bass.ds(t * D, D)]).then_inc(s["h_staged"], 1)
                act.wait_ge(s["h_turned"], t + 2)
                act.wait_ge(s["made"], t + 1)
                nc.scalar.copy(ht[0:D, :], ps_h[0:D, 0:P]).then_inc(s["ht_ready"], 1)

            def roots(n, width):
                return nc.scalar.activation(stat[:, 1:1 + width, :], stat[:, 1:1 + width, :], ACT.Sqrt)

            def lay_out_rows(s):
                q = sums[s]
                for k in range(SLOTS):
                    nc.scalar.copy(ibuf[:, k, :], IDX[s][:, k * CH:(k + 1) * CH]).then_inc(s_rows_known, 1)
                with act.Fori(0, STEPS) as i:
                    for k in range(SLOTS):
                        act.wait_ge(q["gathered"][k], (i + 1) * (16 * CH))
                        nc.scalar.copy(ibuf[:, k, :], IDX[s][:, bass.ds(i * (SLOTS * CH) + (SLOTS + k) * CH, CH)]
                                       ).then_inc(s_rows_known, 1)
                    if s == 1:
                        for j in range(2):
                            turn_tile(1, 2 * i + j)

            def y_window(start, ready):
                nc.scalar.copy(ywin[:, :], big[64:64 + D, bass.ds(start, WIN)]).then_inc(ready, 1)

            def lay_out_turned(done):
                nc.scalar.copy(onehot_t[:, :, :].rearrange("p c w -> p (c w)"), wide[:, 0:CH * WIN])
                nc.scalar.copy(yw[:, :], ps_wide[:, 3, 0:D]).then_inc(done, 1)

            def attend():
                q = sums[3]
                for k in range(SLOTS):
                    nc.scalar.copy(ibuf[:, k, :], IDX[3][:, k * CH:(k + 1) * CH]).then_inc(s_rows_known, 1)
                count = act.alloc_register("act_more")
                act.reg_mov(count, 0)
                at = act.alloc_register("act_at")
                start = act.value_load(meta[0:1, 0:1], min_val=0, max_val=N - 1)
                y_window(start, attn["y_window"])
                act.wait_ge(attn["turned"], 1)
                lay_out_turned(attn["laid_out"])
                with act.Fori(0, STEPS) as i:
                    for k in range(SLOTS):
                        g = i * SLOTS + k
                        next_start = act.value_load(meta[0:1, bass.ds(g * 2 + 2, 1)], min_val=0, max_val=N - 1)
                        y_window(next_start, attn["y_window"])
                        act.wait_ge(attn["scores"], g + 1)
                        nc.scalar.activation(att[:, :], score[:, :], ACT.Tanh).then_inc(attn["tanh"], 1)
                        act.wait_ge(q["gathered"][k], (i + 1) * (16 * CH))
                        nc.scalar.copy(ibuf[:, k, :], IDX[3][:, bass.ds(i * (SLOTS * CH) + (SLOTS + k) * CH, CH)]
                                       ).then_inc(s_rows_known, 1)
                        act.wait_ge(attn["turned"], g + 2)
                        carry_wait(act)
                        act.wait_ge(attn["y_own"], g + 1)
                        lay_out_turned(attn["laid_out"])
                        windows = act.value_load(meta[0:1, bass.ds(g * 2 + 1, 1)], min_val=1, max_val=NT)
                        with act.If(windows > 1):
                            first = act.value_load(meta[0:1, bass.ds(g * 2, 1)], min_val=0, max_val=N - 1)
                            act.reg_mov(at, first)
                            with act.Fori(1, windows) as w:
                                act.reg_add(count, count, 1)
                                act.reg_add(at, at, WIN)
                                n = act.snap(count)
                                y_window(act.snap(at, min_val=0, max_val=NPAD), more["y_window"])
                                act.wait_ge(more["turned"], n)
                                lay_out_turned(more["laid_out"])
                                act.wait_ge(more["scores"], n)
                                nc.scalar.activation(att[:, :], score[:, :], ACT.Tanh).then_inc(more["tanh"], 1)

            def stage_blocks(e, norm=None, width=1):
                act.wait_ge(sums[e]["all_added"], 1)
                s = blk[e]
                for i in first_then_loop(act, NB):
                    if not isinstance(i, int):
                        act.wait_ge(s["turned"], i)
                    nc.scalar.copy(stage[0:CHN[e], :], big[0:CHN[e], bass.ds(i * (BT * P), BT * P)]).then_inc(s["staged"], 1)
                    if e == 3:
                        nc.scalar.copy(cst[:, :], cols(O, i, D)).then_inc(s_cst, 1)
                        act.wait_ge(s_ct, i + 1)
                        act.wait_ge(s["turned"], i + 1)
                        nc.scalar.copy(stage[0:D, :], wide[0:D, 0:BT * P]).then_inc(s_ctc, 1)
                        act.wait_ge(s_cz, i + 1)
                    if norm is not None:
                        act.wait_ge(s_var[norm], i + 1)
                        roots(norm, width).then_inc(s_std[norm], 1)

            with act.Fori(0, NB) as i:
                act.wait_ge(s_var[0], i + 1)
                roots(0, 1).then_inc(s_std[0], 1)
            act.wait_ge(s_w0p, 1)
            nc.scalar.copy(w0f[:, :], ps_z[0:D, :]).then_inc(s_w0c, 1)
            act.wait_ge(tile[0]["h_ready"], 1)
            with act.Fori(0, NT) as t:
                turn_tile(0, t)
            act.wait_ge(s_idx, 1)
            lay_out_rows(0)
            stage_blocks(0, 1, 2)
            lay_out_rows(1)
            stage_blocks(1)
            lay_out_rows(2)
            stage_blocks(2, 2)
            act.wait_ge(tile[2]["h_ready"], 1)
            nc.scalar.copy(hst[:, :], H[:, 0:D]).then_inc(tile[2]["h_staged"], 1)
            for t in first_then_loop(act, NT):
                first = isinstance(t, int)
                act.wait_ge(tile[2]["h_turned"], t + 2)
                act.wait_ge(tile[2]["made"], t + 1)
                nc.scalar.copy(ht[0:D, :], ps_h[0:D, 0:P]).then_inc(tile[2]["ht_ready"], 1)
                nc.scalar.copy(hst[:, :], H[:, bass.ds(t * D + D, D)]).then_inc(tile[2]["h_staged"], 1)
                act.wait_ge(tile[2]["made"], t + 2)
                nc.scalar.copy(big[64:64 + D, bass.ds(t * P, P)], ps_agg[0:D, 0:P])
                nc.scalar.copy(xh[:, :], ps_t[:, 0:D]).then_inc(tile[2]["copied"], 1)
                for r, (h, r0, n) in enumerate(BUILD):
                    half0, half_n = HALF[h]
                    rows = tbuf[:, h, 0:half_n * ROW2].rearrange("p (r c) -> p r c", c=ROW2)
                    if r0 == half0:
                        if not first:
                            act.wait_ge(s_t2[h], t * 16)
                        act.wait_ge(tile[2]["copied"], t + 1)
                        nc.scalar.copy(rows[:, :, PAIR:ROW2], xh[:, :].unsqueeze(1).to_broadcast([P, half_n, D]))
                    if r % 2:
                        continue
                    act.wait_ge(s_round, t * NBUILD + r + 1)
                    nc.scalar.copy(rows[:, r0 - half0:r0 - half0 + n, 0:PAIR],
                                   ps_wide[:, r % 2, 0:n * PAIR].rearrange("p (r c) -> p r c", c=PAIR)).then_inc(s_even, 1)
            act.wait_ge(s_idx2, 1)
            attend()
            stage_blocks(3, 3)
            lay_out_rows(4)
            stage_blocks(4)

        @block.tensor
        def _(pe):

            def turn_tile(f, t):
                s = tile[f]
                pe.wait_ge(s["h_staged"], t + 1)
                nc.tensor.transpose(ps_h[0:D, 0:P], hst[:, :], ident[:, :]).then_inc(s["h_turned"], 1)
                pe.wait_ge(s["ht_ready"], t + 1)

            def windows_of_group(s, i, k, count):
                q, g = sums[s], i * SLOTS + k
                windows = pe.value_load(meta[0:1, bass.ds(g * 2 + 1, 1)], min_val=1, max_val=NT)
                with pe.Fori(0, windows) as w:
                    pe.reg_add(count, count, 1)
                    n = pe.snap(count)
                    pe.wait_ge(q["onehot_ready"], n)
                    pe.wait_ge(q["added"], n)
                    for c in range(CH):
                        last = nc.tensor.matmul(ps_agg[0:CHN[s], 0:WIN], gbuf[:, k, c, 0:CHN[s]], onehot[:, c, :],
                                                start=(c == 0), stop=(c == CH - 1))
                    last.then_inc(q["sums_ready"], 1)

            def sum_edges(s):
                count = pe.alloc_register(f"pe_windows_{s}")
                pe.reg_mov(count, 0)
                with pe.Fori(0, STEPS) as i:
                    for k in range(SLOTS):
                        windows_of_group(s, i, k, count)
                    if s == 1:
                        for j in range(2):
                            t = 2 * i + j
                            turn_tile(1, t)
                            pe.wait_ge(tile[1]["copied"], t + 1)
                            nc.tensor.matmul(ps_z[:, 0:D], ht[0:D, :], w02[:, :], start=True, stop=False)
                            nc.tensor.matmul(ps_z[:, 0:D], ones[0:1, :], b1_s[:, :], start=False,
                                             stop=True).then_inc(tile[1]["made"], 1)

            def turn_onehots(rows):
                for c in range(CH):
                    nc.tensor.transpose(ps_wide[:, c // 4, (c % 4) * P:(c % 4 + 1) * P], rows[:, c, :], ident[:, :])

            def turn_y(done):
                nc.tensor.transpose(ps_wide[:, 3, 0:D], ywin[:, :], ident[0:D, 0:D]).then_inc(done, 1)

            def pick_y(b, done):
                for c in range(CH):
                    last = nc.tensor.matmul(y_own[b][:, c, :], onehot_t[:, c, :], yw[:, :], start=True, stop=True)
                last.then_inc(done, 1)

            def add_messages(b, done):
                for c in range(CH):
                    last = nc.tensor.matmul(ps_agg[0:D, 0:WIN], msg[:, c, :], onehots[b][:, c, :],
                                            start=(c == 0), stop=(c == CH - 1))
                last.then_inc(done, 1)

            def attend():
                q = sums[3]
                count = pe.alloc_register("pe_more")
                pe.reg_mov(count, 0)
                pe.wait_ge(q["onehot_ready"], 1)
                turn_onehots(onehots[0])
                pe.wait_ge(attn["y_window"], 1)
                turn_y(attn["turned"])
                pe.wait_ge(attn["laid_out"], 1)
                pick_y(0, attn["y_own"])
                with pe.Fori(0, STEPS) as i:
                    for k in range(SLOTS):
                        g, b = i * SLOTS + k, k % 2
                        pe.wait_ge(q["onehot_ready"], g + 2)
                        carry_wait(pe)
                        turn_onehots(onehots[1 - b])
                        pe.wait_ge(attn["y_window"], g + 2)
                        carry_wait(pe)
                        turn_y(attn["turned"])
                        pe.wait_ge(attn["messages"], g + 1)
                        add_messages(b, q["sums_ready"])
                        pe.wait_ge(attn["laid_out"], g + 2)
                        carry_wait(pe)
                        pick_y(1 - b, attn["y_own"])
                        windows = pe.value_load(meta[0:1, bass.ds(g * 2 + 1, 1)], min_val=1, max_val=NT)
                        with pe.If(windows > 1):
                            with pe.Fori(1, windows) as w:
                                pe.reg_add(count, count, 1)
                                n = pe.snap(count)
                                pe.wait_ge(more["onehot_ready"], n)
                                carry_wait(pe)
                                turn_onehots(onehots[b])
                                pe.wait_ge(more["y_window"], n)
                                carry_wait(pe)
                                turn_y(more["turned"])
                                pe.wait_ge(more["laid_out"], n)
                                carry_wait(pe)
                                pick_y(b, more["y_own"])
                                pe.wait_ge(more["messages"], n)
                                add_messages(b, more["sums_ready"])

            def turn_blocks(e):
                s = blk[e]
                with pe.Fori(0, NB) as i:
                    pe.wait_ge(s["staged"], i + 1)
                    pe.wait_ge(s["read"], i + 1)
                    carry_wait(pe)
                    if e != 2:
                        for k in range(BT):
                            last = nc.tensor.transpose(turned[:, k, 0:CHN[e]], stage[0:CHN[e], k * P:(k + 1) * P],
                                                       ident[0:CHN[e], 0:CHN[e]])
                    if e in (1, 2):
                        for k in range(BT):
                            last = nc.tensor.matmul(zed[:, k, :], stage[0:D, k * P:(k + 1) * P], w1_s[:, e, :],
                                                    start=True, stop=True)
                    last.then_inc(s["turned"], 1)
                    if e == 3:
                        pe.wait_ge(s_cst, i + 1)
                        for k in range(BT):
                            last = nc.tensor.transpose(wide[0:D, k * P:(k + 1) * P], cst[:, k * D:(k + 1) * D], ident[:, :])
                        last.then_inc(s_ct, 1)
                        pe.wait_ge(s_ctc, i + 1)
                        for k in range(BT):
                            last = nc.tensor.matmul(zed[:, k, :], stage[0:D, k * P:(k + 1) * P], self_s[:, :],
                                                    start=True, stop=True)
                        last.then_inc(s_cz, 1)

            for f in range(3):
                pe.sem_inc(tile[f]["h_turned"], 1)
                pe.sem_inc(tile[f]["made"], 1)
            pe.wait_ge(s_wa, 48)
            w0v = w0_s[:, :].rearrange("b (r a o) -> b a r o", a=2, o=D)
            for a in range(2):
                last = nc.tensor.matmul(ps_z[0:D, :].rearrange("p (r o) -> p r o", o=D), comp0_s[:, a, :], w0v[:, a, :, :],
                                        start=(a == 0), stop=(a == 1))
            last.then_inc(s_w0p, 1)
            pe.wait_ge(s_const, 1)
            pe.wait_ge(s_w0c, 1)
            for i in first_then_loop(pe, NT // 2):
                for j in range(2):
                    turn_tile(0, 2 * i + j)
                    if not isinstance(i, int):
                        pe.wait_ge(tile[0]["copied"], 2 * i + j - 1)
                    nc.tensor.matmul(ps_wide[:, j, :], ht[0:D, :], w0f[:, :], start=True, stop=True).then_inc(tile[0]["made"], 1)
            pe.wait_ge(s_flagp, 1)
            nc.tensor.matmul(ps_agg[0:1, 0:1], flag[:, :], ones[:, 0:1], start=True, stop=True).then_inc(s_flags, 1)
            pe.wait_ge(s_wb, 16 * WB_DMAS)
            pe.wait_ge(tile[0]["copied"], NT)
            for r, o0 in enumerate(range(0, D, 5)):
                if r >= 2:
                    pe.wait_ge(s_w2c, r - 1)
                for o in range(o0, min(o0 + 5, D)):
                    last = nc.tensor.matmul(ps_wide[0:D, r % 2, (o - o0) * R2:(o - o0 + 1) * R2], w2_s[:, :, o],
                                            comp2_s[:, :], start=True, stop=True)
                last.then_inc(s_w2p, 1)
            nc.tensor.matmul(ps_z[0:D + 1, 0:R2], a1[:, :], relt[:, :], start=True, stop=True).then_inc(s_w2p, 1)
            pe.wait_ge(s_meta_r, 32)
            sum_edges(0)
            turn_blocks(0)
            sum_edges(1)
            turn_blocks(1)
            sum_edges(2)
            turn_blocks(2)
            pe.wait_ge(tile[2]["h_staged"], 1)
            nc.tensor.transpose(ps_h[0:D, 0:P], hst[:, :], ident[:, :]).then_inc(tile[2]["h_turned"], 1)
            for t in first_then_loop(pe, NT):
                first = isinstance(t, int)
                pe.wait_ge(tile[2]["ht_ready"], t + 1)
                carry_wait(pe)
                if not first:
                    pe.wait_ge(tile[2]["copied"], t)
                    carry_wait(pe)
                nc.tensor.matmul(ps_agg[0:D, 0:P], a2t[:, :], ht[:, :], start=True, stop=True)
                nc.tensor.matmul(ps_t[:, 0:D], ht[:, :], a1t[:, :], start=True, stop=True).then_inc(tile[2]["made"], 1)
                pe.wait_ge(tile[2]["h_staged"], t + 2)
                nc.tensor.transpose(ps_h[0:D, 0:P], hst[:, :], ident[:, :]).then_inc(tile[2]["h_turned"], 1)
                for r, (h, r0, n) in enumerate(BUILD):
                    if not first or r >= 2:
                        copied, each = ((s_even, EVEN), (s_odd, ODD))[r % 2]
                        pe.wait_ge(copied, t * each + r // 2)
                    nc.tensor.matmul(ps_wide[:, r % 2, 0:n * PAIR], ht[:, :],
                                     w2f[:, 2 * r0:2 * (r0 + n), :].rearrange("p r c -> p (r c)"),
                                     start=True, stop=True).then_inc(s_round, 1)
            attend()
            turn_blocks(3)
            sum_edges(4)
            turn_blocks(4)

        @block.vector
        def _(dve):
            V = nc.vector

            def normalise(n, i):
                xb, hb, cb = by_tile(cols(X, i, D)), by_tile(cols(H, i, D)), by_tile(cent[:, :])
                V.tensor_reduce(stat[:, 0, :], xb, X_AXIS, ALU.add)
                dve.drain()
                V.tensor_scalar(stat[:, 0, :], stat[:, 0, :], 1.0 / D, None, ALU.mult)
                dve.drain()
                V.tensor_tensor(cb, xb, over(stat[:, 0, :], D), ALU.subtract)
                dve.drain()
                V.tensor_tensor(by_tile(sq[:, :]), cb, cb, ALU.mult)
                dve.drain()
                V.tensor_reduce(stat[:, 1, :], by_tile(sq[:, :]), X_AXIS, ALU.add)
                dve.drain()
                V.tensor_scalar(stat[:, 1, :], stat[:, 1, :], 1.0 / D, EPS, ALU.mult, ALU.add).then_inc(s_var[n], 1)
                dve.wait_ge(s_std[n], i + 1)
                V.reciprocal(stat[:, 1:3, :], stat[:, 1:3, :])
                dve.drain()
                V.tensor_tensor(hb, cb, over(stat[:, 1, :], D), ALU.mult)
                dve.drain()
                V.tensor_scalar(hb, hb, 0.0, None, ALU.max)
                dve.drain()

            def sum_edges(s):
                q = sums[s]
                V.memset(big[0:64, 0:SW], 0.0)
                dve.sem_inc(s_free, SLOTS)
                dve.sem_inc(q["added"], 1)
                dve.drain()
                count = dve.alloc_register(f"dve_windows_{s}")
                dve.reg_mov(count, 0)
                at = dve.alloc_register(f"dve_at_{s}")
                with dve.Fori(0, STEPS) as i:
                    for k in range(SLOTS):
                        g = i * SLOTS + k
                        start = dve.value_load(meta[0:1, bass.ds(g * 2, 1)], min_val=0, max_val=N - 1)
                        windows = dve.value_load(meta[0:1, bass.ds(g * 2 + 1, 1)], min_val=1, max_val=NT)
                        dve.reg_mov(at, start)
                        V.tensor_copy(cur[:, :], drel[:, bass.ds(g * CH, CH)])
                        if s == 4:
                            dve.drain()
                        dve.wait_ge(q["gathered"][k], (i + 1) * (16 * CH))
                        rows = gbuf[:, k, :, 0:D]
                        if s < 3:
                            by = ew1_s if s == 0 else ew_s
                            V.tensor_tensor(rows, rows, by[:, bass.ds(g * CH, CH)].unsqueeze(2).to_broadcast([P, CH, D]), ALU.mult)
                        if s == 0:
                            V.tensor_copy(gbuf[:, k, :, D], ew_s[:, bass.ds(g * CH, CH)])
                            V.tensor_copy(gbuf[:, k, :, D + 2], lsrc[:, bass.ds(g * CH, CH)])
                        if s < 4:
                            dve.drain()
                        else:
                            carry_wait(dve)
                        with dve.Fori(0, windows) as w:
                            dve.reg_add(count, count, 1)
                            n = dve.snap(count)
                            a = dve.snap(at, min_val=0, max_val=NPAD)
                            V.tensor_tensor(onehot[:, :, :], iota[:, :].unsqueeze(1).to_broadcast([P, CH, WIN]),
                                            cur[:, :].unsqueeze(2).to_broadcast([P, CH, WIN]),
                                            ALU.is_equal).then_inc(q["onehot_ready"], 1)
                            dve.drain()
                            V.tensor_scalar(cur[:, :], cur[:, :], float(-WIN), None, ALU.add)
                            dve.drain()
                            dve.wait_ge(q["sums_ready"], n)
                            into = big[0:CHN[s], bass.ds(a, WIN)]
                            V.tensor_tensor(into, into, ps_agg[0:CHN[s], 0:WIN], ALU.add).then_inc(q["added"], 1)
                            dve.reg_add(at, at, WIN)
                        dve.sem_inc(s_free, 1)
                    if s == 1:
                        for j in range(2):
                            t = 2 * i + j
                            dve.wait_ge(tile[1]["made"], t + 2)
                            V.tensor_copy(O[:, bass.ds(t * D, D)], ps_z[:, 0:D]).then_inc(tile[1]["copied"], 1)
                dve.drain()
                if s > 0:
                    dve.sem_inc(q["all_added"], 1)

            def compare(rows, targets, done):
                V.tensor_tensor(rows[:, :, :], iota[:, :].unsqueeze(1).to_broadcast([P, CH, WIN]),
                                targets.unsqueeze(2).to_broadcast([P, CH, WIN]), ALU.is_equal).then_inc(done, 1)

            def weigh(k, g, n, m):
                pairs = gbuf[:, k, :, 0:PAIR].rearrange("p c (a d) -> p c a d", a=2)
                pick = par[:, :, bass.ds(g * CH, CH)].rearrange("p a c -> p c a")
                V.tensor_tensor(parts[:, :, D:D + 2], pairs[:, :, :, D], pick, ALU.mult)
                dve.wait_ge(m["y_own"], n)
                V.tensor_tensor(parts[:, :, 0:D], y_own[k % 2], gbuf[:, k, :, PAIR:ROW2], ALU.mult)
                dve.drain()
                V.tensor_reduce(raw[:, :], parts[:, :, :], X_AXIS, ALU.add)
                dve.drain()
                V.tensor_scalar(score[:, :], raw[:, :], float(1.0 / np.sqrt(D)), 0.0, ALU.mult, ALU.max).then_inc(m["scores"], 1)
                dve.wait_ge(m["tanh"], n)
                V.scalar_tensor_tensor(att2[:, :], att[:, :], 0.0, att[:, :], ALU.is_gt, ALU.mult)
                dve.drain()
                V.tensor_tensor(att_p[:, :, :], pick, att2[:, :].unsqueeze(2).to_broadcast([P, CH, 2]), ALU.mult)
                dve.drain()
                V.tensor_tensor(msg2[:, :, :, :], pairs[:, :, :, 0:D],
                                att_p[:, :, :].unsqueeze(3).to_broadcast([P, CH, 2, D]), ALU.mult)
                dve.drain()
                V.tensor_tensor(msg[:, :, :], msg2[:, :, 0, :], msg2[:, :, 1, :], ALU.add).then_inc(m["messages"], 1)

            def attend():
                q = sums[3]
                V.memset(big[0:64, 0:SW], 0.0)
                dve.sem_inc(s_free, SLOTS)
                for h in range(2):
                    dve.wait_ge(s_t2[h], 16 * NT)
                dve.drain()
                compare(onehots[0], drel[:, 0:CH], q["onehot_ready"])
                count = dve.alloc_register("dve_more")
                dve.reg_mov(count, 0)
                at = dve.alloc_register("dve_at")
                with dve.Fori(0, STEPS) as i:
                    for k in range(SLOTS):
                        g, b = i * SLOTS + k, k % 2
                        compare(onehots[1 - b], drel[:, bass.ds(g * CH + CH, CH)], q["onehot_ready"])
                        dve.wait_ge(q["gathered"][k], (i + 1) * (16 * CH))
                        weigh(k, g, g + 1, attn)
                        start = dve.value_load(meta[0:1, bass.ds(g * 2, 1)], min_val=0, max_val=N - 1)
                        windows = dve.value_load(meta[0:1, bass.ds(g * 2 + 1, 1)], min_val=1, max_val=NT)
                        dve.wait_ge(q["sums_ready"], g + 1)
                        into = big[0:D, bass.ds(start, WIN)]
                        V.tensor_tensor(into, into, ps_agg[0:D, 0:WIN], ALU.add)
                        with dve.If(windows > 1):
                            dve.reg_mov(at, start)
                            V.tensor_copy(cur[:, :], drel[:, bass.ds(g * CH, CH)])
                            with dve.Fori(1, windows) as w:
                                dve.reg_add(count, count, 1)
                                dve.reg_add(at, at, WIN)
                                n = dve.snap(count)
                                a = dve.snap(at, min_val=0, max_val=NPAD)
                                dve.drain()
                                V.tensor_scalar(cur[:, :], cur[:, :], float(-WIN), None, ALU.add)
                                dve.drain()
                                compare(onehots[b], cur[:, :], more["onehot_ready"])
                                weigh(k, g, n, more)
                                dve.wait_ge(more["sums_ready"], n)
                                into = big[0:D, bass.ds(a, WIN)]
                                V.tensor_tensor(into, into, ps_agg[0:D, 0:WIN], ALU.add)
                        dve.drain()
                        dve.sem_inc(s_free, 1)
                dve.drain()
                dve.sem_inc(q["all_added"], 1)

            V.memset(X[:, (NT - 1) * D:NT * D], 0.0)
            V.memset(comp0_s[:, :, :], 0.0)
            for t in (src_i, idx_a):
                V.memset(t[:, (NG - 1) * CH:IC], 0)
            V.memset(dst_i[:, (NG - 1) * CH:NG * CH], int(FAR))
            V.memset(nxt_i[:, (NG - 1) * CH:NG * CH], int(-2 * FAR))
            for t in (ew_s, two[:, 0, :]):
                V.memset(t[:, (NG - 1) * CH:NG * CH], 0.0)
            dve.drain()
            dve.sem_inc(s_pad, 1)
            V.memset(H[:, NT * D:FT * D], 0.0)
            V.memset(O[:, NT * D:FT * D], 0.0)
            V.memset(big[:, NPAD:SW], 0.0)
            V.memset(drel[:, NG * CH:(NG + 1) * CH], FAR)
            V.memset(meta[:, 2 * NG:], 0)
            V.memset(w2f[D:D + 1, :, 0:D], 0.0)
            V.memset(ht[D:D + 1, :], 1.0)
            V.memset(ones[:, :], 1.0)
            V.memset(gbuf[:, :, :, D + 1], 1.0)
            V.memset(stat[:, :, :], 1.0)
            dve.wait_ge(s_iota, 1)
            V.tensor_copy(iota[:, :], iota_i[:, :])
            V.tensor_copy(pcol[:, :], pcol_i[:, :])
            dve.drain()
            V.tensor_scalar(ident[:, :], iota[:, :], pcol[:, 0:1], None, ALU.is_equal).then_inc(s_const, 1)
            dve.wait_ge(s_x, 32)
            dve.drain()
            with dve.Fori(0, NB) as i:
                normalise(0, i)
            dve.sem_inc(tile[0]["h_ready"], 1)

            dve.wait_ge(s_rows, 48)
            V.tensor_reduce(mm_f[:, :, 0], drow_i, X_AXIS, ALU.min)
            V.tensor_reduce(mm_f[:, :, 1], drow_i, X_AXIS, ALU.max)
            dve.drain()
            V.tensor_tensor(mm_w[:, :], mm_f[:, :, 1], mm_f[:, :, 0], ALU.subtract)
            V.tensor_copy(mm_i[:, :, 0], mm_f[:, :, 0])
            dve.drain()
            V.tensor_scalar(mm_w[:, :], mm_w[:, :], 7, None, ALU.arith_shift_right)
            dve.drain()
            V.tensor_scalar(mm_i[:, :, 1], mm_w[:, :], 1.0, None, ALU.add).then_inc(s_mm, 1)

            dve.wait_ge(s_src, 48)
            V.tensor_scalar(tmp_i, src_i[:, :], P - 1, None, ALU.bitwise_and)
            V.tensor_scalar(idx_h[:, :], src_i[:, :], 7, None, ALU.arith_shift_right)
            dve.drain()
            V.scalar_tensor_tensor(idx_h[:, :], tmp_i, float(NT), idx_h[:, :], ALU.mult, ALU.add)
            dve.wait_ge(s_et16, 48)
            V.scalar_tensor_tensor(idx_a[:, :], src_i[:, :], float(R0), idx_a[:, :], ALU.mult, ALU.add)
            dve.drain()
            dve.sem_inc(s_idx, 1)

            for i in first_then_loop(dve, NT // 2):
                for j in range(2):
                    dve.wait_ge(tile[0]["made"], 2 * i + j + 2)
                    if not isinstance(i, int):
                        dve.wait_ge(s_t0[j], i * 16)
                    V.tensor_copy(t0buf[:, j, :], ps_wide[:, j, :]).then_inc(tile[0]["copied"], 1)

            dve.wait_ge(s_dst, 96)
            V.tensor_copy(dst_f, dst_i)
            V.tensor_copy(nxt_f, nxt_i)
            dve.drain()
            V.tensor_tensor(tmp_f, dst_f, nxt_f, ALU.is_gt)
            dve.drain()
            V.tensor_reduce(flag[:, :], tmp_f, X_AXIS, ALU.add).then_inc(s_flagp, 1)
            dve.drain()
            V.tensor_tensor(tmp_f, dst_f, nxt_f, ALU.not_equal)
            dve.drain()
            V.tensor_tensor(lsrc, tmp_f, src_i[:, 0:NG * CH], ALU.mult)
            dve.wait_ge(s_meta_r, 32)
            V.tensor_tensor(drel[:, 0:NG * CH].rearrange("p (g c) -> p g c", c=CH), dst_f.rearrange("p (g c) -> p g c", c=CH),
                            bounds_b.rearrange("p (g w) -> p g w", w=2)[:, :, 0].unsqueeze(2).to_broadcast([P, NG, CH]),
                            ALU.subtract)
            dve.wait_ge(s_flags, 1)
            V.tensor_scalar(flag_i[:, :], ps_agg[0:1, 0:1], 0.0, None, ALU.is_gt).then_inc(s_flag, 1)

            for r, o0 in enumerate(range(0, D, 5)):
                n = min(5, D - o0)
                dve.wait_ge(s_w2p, r + 1)
                V.tensor_copy(w2f[0:D, :, o0:o0 + n],
                              ps_wide[0:D, r % 2, 0:n * R2].rearrange("p (o r) -> p r o", r=R2)).then_inc(s_w2c, 1)
            dve.wait_ge(s_w2p, 8)
            V.tensor_copy(w2f[:, :, D], ps_z[0:D + 1, 0:R2])
            V.tensor_tensor(w02[:, :], w1_s[:, 0, :], w1_s[:, 2, :], ALU.subtract)
            dve.sem_inc(tile[1]["copied"], 1)
            for e in range(5):
                dve.sem_inc(blk[e]["read"], 1)
            dve.wait_ge(s_ew, 96)
            dve.drain()

            sum_edges(0)

            unsorted = dve.value_load(flag_i[0:1, 0:1], min_val=0, max_val=1)
            with dve.If(unsorted > 0):
                V.memset(last_e[:, :], 0.0)
                V.memset(base[:, :], 0.0)
                for c in range(CH):
                    V.tensor_scalar(key[:, c * P:(c + 1) * P], iota[:, :], float(c * P + 1), None, ALU.add)
                dve.drain()
                dve.sem_inc(s_lused, 1)
                with dve.Fori(0, NG) as g:
                    V.tensor_scalar(base[:, :], base[:, :], float(E - GROUP), None, ALU.min)
                    V.tensor_copy(node[:, :], pcol[:, :])
                    dve.drain()
                    dve.wait_ge(s_lrow, g * 16 + 16)
                    carry_wait(dve)
                    with dve.Fori(0, NT) as t:
                        V.scalar_tensor_tensor(keyed, trow, node[:, 0:1], key, ALU.is_equal, ALU.mult)
                        dve.drain()
                        V.tensor_reduce(found[:, 0:1], keyed, X_AXIS, ALU.max)
                        dve.drain()
                        V.scalar_tensor_tensor(found[:, 1:2], found[:, 0:1], 0.0, base[:, :], ALU.is_gt, ALU.mult)
                        dve.drain()
                        V.tensor_tensor(found[:, 0:1], found[:, 0:1], found[:, 1:2], ALU.add)
                        V.tensor_scalar(node[:, :], node[:, :], float(P), None, ALU.add)
                        dve.drain()
                        V.tensor_tensor(last_e[:, bass.ds(t, 1)], last_e[:, bass.ds(t, 1)], found[:, 0:1], ALU.max)
                        dve.drain()
                    V.tensor_scalar(base[:, :], base[:, :], float(GROUP), None, ALU.add)
                    dve.drain()
                    dve.sem_inc(s_lused, 1)
                with dve.Fori(0, NT) as t:
                    V.tensor_scalar(lcol[:, :], last_e[:, bass.ds(t, 1)], -1.0, 0.0, ALU.add, ALU.max).then_inc(s_lcol, 1)
                    dve.wait_ge(s_lgot, t * 16 + 16)
                    carry_wait(dve)
                    V.tensor_copy(last_e[:, bass.ds(t, 1)], lsrc_i[:, :])
                    dve.drain()
            dve.sem_inc(sums[0]["all_added"], 1)

            for i in first_then_loop(dve, NB):
                xb = by_tile(cols(X, i, D))
                dve.wait_ge(blk[0]["turned"], i + 1)
                V.tensor_tensor(xb, xb, turned[:, :, 0:D], ALU.add)
                V.tensor_scalar(stat[:, 2, :], turned[:, :, D], 1e-12, None, ALU.max)
                V.tensor_scalar(stat[:, 3, :], turned[:, :, D], 0.0, None, ALU.is_gt)
                V.tensor_copy(cols(deg, i, 1), turned[:, :, D + 1])
                V.tensor_copy(cols(last_f, i, 1), turned[:, :, D + 2]).then_inc(blk[0]["read"], 1)
                dve.drain()
                normalise(1, i)
                V.tensor_tensor(cols(dinv, i, 1), stat[:, 2, :], stat[:, 3, :], ALU.mult)
                dve.drain()
                if not isinstance(i, int):
                    dve.wait_ge(blk[0]["u_stored"], i * 16)
                V.tensor_tensor(by_tile(ubuf[:, :]), by_tile(cols(H, i, D)), over(cols(dinv, i, 1), D),
                                ALU.mult).then_inc(blk[0]["u_ready"], 1)
            dve.sem_inc(tile[1]["h_ready"], 1)
            with dve.If(unsorted > 0):
                V.tensor_copy(last_f[:, :], last_e[:, :])
                dve.drain()
            V.tensor_copy(li_a[:, :], last_f[:, :])
            dve.drain()
            V.tensor_scalar(li_b[:, :], li_a[:, :], P - 1, None, ALU.bitwise_and)
            V.tensor_scalar(last_i[:, :], li_a[:, :], 7, None, ALU.arith_shift_right)
            dve.drain()
            V.scalar_tensor_tensor(last_i[:, :], li_b[:, :], float(NT), last_i[:, :], ALU.mult, ALU.add).then_inc(s_last, 1)

            sum_edges(1)
            for i in first_then_loop(dve, NB):
                db, ob = over(cols(dinv, i, 1), D), by_tile(cols(O, i, D))
                dve.wait_ge(blk[1]["turned"], i + 1)
                V.scalar_tensor_tensor(by_tile(cent[:, :]), turned[:, :, 0:D], -1.0, db, ALU.mult, ALU.mult)
                V.scalar_tensor_tensor(by_tile(sq[:, :]), zed, -1.0, db, ALU.mult, ALU.mult).then_inc(blk[1]["read"], 1)
                dve.drain()
                if not isinstance(i, int):
                    dve.wait_ge(blk[1]["u_stored"], i * 16)
                V.tensor_tensor(by_tile(ubuf[:, :]), by_tile(cent[:, :]), db, ALU.mult).then_inc(blk[1]["u_ready"], 1)
                V.tensor_tensor(ob, ob, by_tile(sq[:, :]), ALU.add)
                dve.drain()

            dve.wait_ge(s_et86, 48)
            V.tensor_scalar(lsrc.bitcast(I32), idx_a[:, 0:NG * CH], 1, None, ALU.bitwise_and)
            dve.drain()
            V.tensor_copy(ew1_s, lsrc.bitcast(I32))
            dve.drain()
            V.tensor_copy(lsrc, ew1_s)
            V.tensor_scalar(ew1_s, ew1_s, -1.0, 1.0, ALU.mult, ALU.add)
            V.tensor_scalar(idx_a[:, :], idx_a[:, :], 1, None, ALU.arith_shift_right)
            dve.drain()
            V.scalar_tensor_tensor(idx_a[:, :], src_i[:, :], float(RP), idx_a[:, :], ALU.mult, ALU.add).then_inc(s_idx2, 1)

            sum_edges(2)
            with dve.Fori(0, NB) as i:
                db, ob, xb = over(cols(dinv, i, 1), D), by_tile(cols(O, i, D)), by_tile(cols(X, i, D))
                dve.wait_ge(blk[2]["turned"], i + 1)
                V.scalar_tensor_tensor(by_tile(sq[:, :]), zed, -2.0, db, ALU.mult, ALU.mult).then_inc(blk[2]["read"], 1)
                dve.drain()
                V.tensor_tensor(by_tile(sq[:, :]), by_tile(sq[:, :]), ob, ALU.add)
                dve.drain()
                V.scalar_tensor_tensor(xb, by_tile(sq[:, :]), 0.0, xb, ALU.max, ALU.add)
                dve.drain()
                normalise(2, i)
                dve.sem_inc(blk[2]["u_ready"], 1)
            dve.sem_inc(tile[2]["h_ready"], 1)
            for t in first_then_loop(dve, NT):
                for r, (h, r0, n) in enumerate(BUILD):
                    if r % 2 == 0:
                        continue
                    half0, half_n = HALF[h]
                    rows = tbuf[:, h, 0:half_n * ROW2].rearrange("p (r c) -> p r c", c=ROW2)
                    if not isinstance(t, int):
                        dve.wait_ge(s_t2[h], t * 16)
                    dve.wait_ge(s_round, t * NBUILD + r + 1)
                    V.tensor_copy(rows[:, r0 - half0:r0 - half0 + n, 0:PAIR],
                                  ps_wide[:, r % 2, 0:n * PAIR].rearrange("p (r c) -> p r c", c=PAIR)).then_inc(s_odd, 1)

            attend()
            V.tensor_scalar(mask[:, :], deg[:, :], 0.0, None, ALU.is_gt)
            dve.wait_ge(s_curr, 16 * NT)
            dve.drain()
            with dve.Fori(0, NB) as i:
                xb = by_tile(cols(X, i, D))
                dve.wait_ge(s_cz, i + 1)
                V.tensor_copy(by_tile(sq[:, :]), zed)
                dve.drain()
                V.tensor_tensor(by_tile(sq[:, :]), by_tile(sq[:, :]), turned[:, :, 0:D], ALU.add).then_inc(blk[3]["read"], 1)
                dve.drain()
                V.tensor_tensor(by_tile(sq[:, :]), by_tile(sq[:, :]), over(cols(mask, i, 1), D), ALU.mult)
                dve.drain()
                V.scalar_tensor_tensor(xb, by_tile(sq[:, :]), 0.0, xb, ALU.max, ALU.add)
                dve.drain()
                normalise(3, i)
                dve.sem_inc(blk[3]["u_ready"], 1)

            sum_edges(4)
            V.tensor_scalar(mask[:, :], deg[:, :], 1.0, None, ALU.max)
            dve.drain()
            V.reciprocal(mask[:, :], mask[:, :])
            dve.drain()
            with dve.Fori(0, NB) as i:
                xb = by_tile(cols(X, i, D))
                dve.wait_ge(blk[4]["turned"], i + 1)
                V.tensor_tensor(by_tile(sq[:, :]), turned[:, :, 0:D], over(cols(mask, i, 1), D), ALU.mult).then_inc(blk[4]["read"], 1)
                dve.drain()
                V.tensor_tensor(xb, xb, by_tile(sq[:, :]), ALU.add).then_inc(blk[4]["u_ready"], 1)
                dve.drain()


INS = ["x", "src", "dst", "edge_type_16", "edge_type_86", "edge_weight", "edge_weight1", "L0_gnn_weight",
       "L0_gnn_w_comp", "L1_gnn_W", "L1_gnn_b", "L2_gnn_weight", "L2_gnn_w_comp", "L2_gnn_self_loop_weight",
       "L2_gnn_A1_w", "L2_gnn_A1_b", "L2_gnn_A2_w", "L2_gnn_A2_b", "L2_gnn_rel_emb"]


def kernel(**inputs):
    import concourse.bacc as bacc
    from concourse.bass_utils import run_bass_kernel_spmd

    nc = bacc.Bacc("TRN2", target_bir_lowering=False, num_devices=1)
    arrays, args = {}, []
    for name in INS:
        a = np.ascontiguousarray(inputs[name])
        arrays[f"in_{name}"] = a
        args.append(nc.dram_tensor(f"in_{name}", a.shape, mybir.dt.from_np(a.dtype), kind="ExternalInput").ap())
    out = nc.dram_tensor("out", (N, D), F32, kind="ExternalOutput").ap()
    gnn_kernel(nc, *args, out)
    r = run_bass_kernel_spmd(nc, [arrays], core_ids=[0])
    return r.results[0]["out"]
```

```python
from contextlib import ExitStack

import numpy as np
import concourse.bass as bass
from concourse import mybir
from concourse.alu_op_type import AluOpType as ALU

F32 = mybir.dt.float32
I32 = mybir.dt.int32
ACT = mybir.ActivationFunctionType
X_AXIS = mybir.AxisListType.X

P = 128
N = 12500
E = 212500
D = 32
R0, B0 = 16, 8
R2, B2 = 86, 16
NT = (N + P - 1) // P
NPAD = NT * P
TAIL = N - (NT - 1) * P
CH = 8
GROUP = CH * P
NG = (E + GROUP - 1) // GROUP
SLOTS = 4
STEPS = NG // SLOTS
PER_SUM = SLOTS + NG
LAST = E - (NG - 1) * GROUP
LP, LC = LAST // CH, LAST % CH
IC = (NG + SLOTS) * CH
WIN = 80
SW = NPAD + P
SHIFT = 14
SCALE = -(-(1 << SHIFT) // WIN)
MORE = (N - 1) * SCALE >> SHIFT
assert GROUP * N // E < WIN <= P and N <= 1 << SHIFT and (MORE << SHIFT) + N < 1 << 24 and (MORE + 1) * WIN <= SW
HG = NG // 2
BT = 14
NB = NT // BT
FT = 2 * STEPS
RP = R2 // 2
PAIR = 2 * (D + 1)
ROW2 = PAIR + D
HALF = [(0, 21), (21, 22)]
WB_DMAS = 12
BUILD = [(0, 0, 7), (0, 7, 7), (0, 14, 7), (1, 21, 7), (1, 28, 7), (1, 35, 7), (1, 42, 1)]
NBUILD = len(BUILD)
BANKS = 4
HALF_DONE = [3, NBUILD]
EPS = 1e-5
FAR = -1.0e6


def gnn_kernel(nc, x, src, dst, et16, et86, ew, ew1, w0, comp0, w1, b1, w2, comp2, selfw,
               a1w, a1b, a2w, a2b, rel, out):
    def scratch(name, shape, dt=F32):
        return nc.dram_tensor(name, shape, dt, kind="Internal").ap()

    table0 = scratch("table0", (NPAD * R0, D))
    table2 = scratch("table2", (NPAD * RP, ROW2))
    nodes = [scratch(f"nodes{i}", (NPAD, D)) for i in range(4)]
    meta_d = scratch("meta_d", (NG, 1), I32)

    ctx = ExitStack()
    with ctx:
        def sb(name, shape, dt=F32):
            return ctx.enter_context(nc.sbuf_tensor(name, shape, dt))

        def sem(name):
            return ctx.enter_context(nc.semaphore(name))

        src_i = sb("src_i", [P, IC], I32)
        idx_a = sb("idx_a", [P, IC], I32)
        idx_h = sb("idx_h", [P, IC], I32)
        ew_s = sb("ew_s", [P, NG * CH])
        two = sb("two", [P, 2, NG * CH])
        ew1_s = two[:, 0, :]
        lsrc = two[:, 1, :]
        par = two
        drel = sb("drel", [P, (NG + 2) * CH])
        meta = sb("meta", [1, NG + 1], I32)
        whole = sb("whole", [1, NG + 1], I32)
        X = sb("X", [P, NT * D])
        H = sb("H", [P, FT * D])
        O = sb("O", [P, FT * D])
        deg = sb("deg", [P, NT])
        dinv = sb("dinv", [P, NT])
        last_i = sb("last_i", [P, NT], I32)
        big = sb("big", [P, SW])
        gbuf = sb("gbuf", [P, SLOTS, CH, ROW2])
        ibuf = sb("ibuf", [P, SLOTS, CH], I32)
        mem_a = sb("mem_a", [P, GROUP])
        mem_b = sb("mem_b", [P, GROUP])
        cur = sb("cur", [P, CH])
        score = sb("score", [P, CH])
        att = sb("att", [P, CH])
        msg = sb("msg", [P, CH, D])
        msg2 = sb("msg2", [P, CH, 2, D])
        att_p = sb("att_p", [P, CH, 2])
        parts = msg2[:, :, :, :].rearrange("p c a d -> p (c a d)")[:, 0:CH * (D + 2)].rearrange(
            "p (c n) -> p c n", c=CH)
        ywin = sb("ywin", [D, WIN])
        yw = sb("yw", [WIN, D])
        tbuf = sb("tbuf", [P, 2, HALF[1][1] * ROW2])

        def onehot_rows(memory):
            return memory[:, 0:CH * WIN].rearrange("p (c w) -> p c w", w=WIN)

        onehots = [onehot_rows(mem_a), onehot_rows(mem_b)]
        onehots3 = [onehots[0]] + [onehot_rows(tbuf[:, h, at:at + GROUP]) for h, at in ((0, 0), (0, GROUP), (1, 0))]
        onehot_t = mem_b[0:WIN, :].rearrange("p (c e) -> p c e", e=P)
        stage = tbuf[0:36, 0, 0:BT * P]
        t0buf = tbuf[:, 0, 0:2 * R0 * D].rearrange("p (a n) -> p a n", a=2)
        ubuf = sb("ubuf", [P, BT * D])
        sq = sb("sq", [P, BT * D])
        cent = sb("cent", [P, BT * D])
        stat = sb("stat", [P, 4, BT])
        cst = sb("cst", [P, BT * D])
        hst = sb("hst", [P, D])
        ht = sb("ht", [D + 1, P])
        sums_t = sb("sums_t", [D, P])
        tsq = sb("tsq", [P, D])
        tcent = sb("tcent", [P, D])
        tmean = sb("tmean", [P, 1])
        tdev = sb("tdev", [P, 1])
        iota_i = sb("iota_i", [P, P], I32)
        iota = sb("iota", [P, P])
        pcol_i = sb("pcol_i", [P, 1], I32)
        pcol = sb("pcol", [P, 1])
        ident = sb("ident", [P, P])
        ones = sb("ones", [P, P])
        w0_s = mem_b[0:B0, :]
        comp0_s = sb("comp0_s", [B0, 2, D])
        w0f = sb("w0f", [D, R0 * D])
        w1_s = sb("w1_s", [D, 3, D])
        w02 = sb("w02", [D, D])
        b1_s = sb("b1_s", [1, D])
        w2_s = mem_a[0:B2, :].rearrange("p (i o) -> p i o", o=D)
        comp2_s = sb("comp2_s", [B2, R2])
        w2f = sb("w2f", [D + 1, R2, D + 1])
        self_s = sb("self_s", [D, D])
        a1 = sb("a1", [D, D + 1])
        a1t = sb("a1t", [D + 1, D])
        a2t = sb("a2t", [D + 1, D])
        relt = sb("relt", [D, R2])
        drow_i = tbuf[0:HG, 0, 0:2 * GROUP].bitcast(I32).rearrange("p (h n) -> p h n", h=2)
        drow = tbuf[0:HG, 1, 0:2 * GROUP].rearrange("p (h n) -> p h n", h=2)
        dst_f = big[:, 0:NG * CH]
        dst_i = big[:, 2048:2048 + NG * CH].bitcast(I32)
        nxt_i = big[:, 4096:4096 + NG * CH].bitcast(I32)
        nxt_f = big[:, 6144:6144 + NG * CH]
        tmp_f = big[:, 8192:8192 + NG * CH]
        bounds_b = big[:, 10240:10240 + NG].bitcast(I32)
        tmp_i = tbuf[:, 0, 0:0 + IC].bitcast(I32)
        least = [big[0:1, 10752 + 256 * j:10752 + 256 * j + NG + 1] for j in range(2)]
        least_i = big[0:1, 11264:11264 + NG].bitcast(I32)
        mm_f = sb("mm_f", [HG, 2, 2])
        mm_i = sb("mm_i", [HG, 2], I32)
        mm_w = sb("mm_w", [HG, 2], I32)
        flag = sb("flag", [P, 1])
        mask = sb("mask", [P, NT])
        raw = sb("raw", [P, CH])
        att2 = sb("att2", [P, CH])
        xh = sb("xh", [P, D])
        node = sb("node", [P, 1])
        lsrc_i = sb("lsrc_i", [P, 1], I32)
        flag_i = sb("flag_i", [1, 1], I32)
        last_f = sb("last_f", [P, NT])
        li_a = sb("li_a", [P, NT], I32)
        li_b = sb("li_b", [P, NT], I32)
        key, keyed = mem_b[:, :], mem_a[:, :]
        trow = tbuf[:, 0, 0:GROUP].bitcast(I32)
        base = sb("base", [P, 1])
        found = sb("found", [P, 2])
        last_e = sb("last_e", [P, NT])
        lcol = sb("lcol", [P, 1], I32)

        ps_wide = ctx.enter_context(nc.psum_tensor("ps_wide", [P, 4, 512], F32))
        ps_agg = ctx.enter_context(nc.psum_tensor("ps_agg", [P, 512], F32))
        ps_t = ctx.enter_context(nc.psum_tensor("ps_t", [P, 512], F32))
        ps_z = ctx.enter_context(nc.psum_tensor("ps_z", [P, 512], F32))
        ps_h = ctx.enter_context(nc.psum_tensor("ps_h", [P, 512], F32))
        turned = ps_t[:, 0:BT * 36].rearrange("p (t c) -> p t c", c=36)
        wide = ps_wide[:, :, :].rearrange("p a b -> p (a b)")
        zed = ps_z[:, 0:BT * D].rearrange("p (t c) -> p t c", c=D)
        y_own = [ps_wide[:, 2, 0:CH * D].rearrange("p (c d) -> p c d", d=D),
                 ps_h[:, 0:CH * D].rearrange("p (c d) -> p c d", d=D)]


        s_x = sem("x_loaded")
        s_src = sem("sources_loaded")
        s_et16 = sem("types16_loaded")
        s_dst = sem("targets_and_next_ones_loaded")
        s_ew = sem("both_weights_loaded")
        s_et86 = sem("types86_loaded")
        s_rows = sem("target_rows_loaded")
        s_wa = sem("first_layers_weights_loaded")
        s_wb = sem("later_layers_weights_loaded")
        s_pad = sem("padding_set")
        s_iota = sem("iota_made")
        s_const = sem("constants_made")
        s_mm = sem("group_bounds_made")
        s_meta_w = sem("group_bounds_written")
        s_meta_r = sem("group_bounds_read")
        s_idx = sem("row_numbers_known")
        s_idx2 = sem("table2_row_numbers_known")
        s_w0p = sem("w0_product")
        s_w0c = sem("w0_copied")
        s_flagp = sem("unsorted_counts_ready")
        s_flags = sem("unsorted_counts_summed")
        s_flag = sem("unsorted_flag_ready")
        s_lused = sem("target_row_used")
        s_lrow = sem("target_row_loaded")
        s_lcol = sem("last_edges_known")
        s_lgot = sem("last_source_gathered")
        s_last = sem("last_rows_known")
        s_curr = sem("last_sources_rows_gathered")
        s_w2p = sem("w2_product")
        s_w2c = sem("w2_copied")
        s_ypad = sem("yhat_padding_set")
        s_out = sem("output_written")
        s_carry = sem("waits_carried")

        tile = [{n: sem(f"tile{f}_{n}") for n in ("h_ready", "h_staged", "h_turned", "ht_ready", "made", "copied")}
                for f in range(2)]
        tile.append({n: sem(f"tile2_{n}") for n in ("staged", "h_staged", "h_turned", "ht_ready", "made")})
        s_t0 = [sem("table0_stored_0"), sem("table0_stored_1")]
        s_t2 = [sem("table2_stored_0"), sem("table2_stored_1")]
        s_round = sem("table2_round_made")
        s_copied = sem("table2_products_copied")
        s_final = sem("tile_summed")
        s_z = sem("tile_z_product")
        blk = [{n: sem(f"block{e}_{n}") for n in ("staged", "turned", "read", "u_ready", "u_stored")[:4 if e == 4 else 5]}
               for e in range(5)]
        s_var = [sem(f"variance_ready_{n}") for n in range(4)]
        s_std = [sem(f"deviation_ready_{n}") for n in range(4)]
        s_cst = sem("last_rows_staged")
        s_ct = sem("last_rows_turned")
        s_ctc = sem("last_rows_turned_copied")
        s_cz = sem("self_product")
        s_free = sem("gather_slot_free")
        s_rows_known = sem("gather_row_numbers_laid_out")
        s_ready = sem("group_weighed_and_compared")
        s_summed = sem("group_multiplied")
        s_more_ready = sem("more_windows_compared")
        s_more_summed = sem("more_windows_multiplied")
        sums = [{n: sem(f"sum{s}_{n}") for n in ("all_added", "onehot_ready", "sums_ready")[:3 if s == 3 else 1]}
                for s in range(5)]
        for s in range(5):
            sums[s]["gathered"] = [sem(f"sum{s}_gathered_{k}") for k in range(SLOTS)]
        attn, more = [{n: sem(f"attention_{m}_{n}") for n in ("y_window", "turned", "laid_out", "y_own", "scores",
                                                            "tanh", "messages")} for m in ("first", "more")]
        more["onehot_ready"] = sem("attention_more_onehot_ready")
        more["sums_ready"] = sem("attention_more_sums_ready")

        WIDTH = [D, D, D, ROW2, D]
        CHN = [D + 3, D, D, D, D]
        IDX = [idx_a, idx_h, idx_h, idx_a, idx_h]
        TABLE = [table0, nodes[0], nodes[1], table2, nodes[3]]
        X3 = X[:, :].rearrange("p (t c) -> p t c", c=D)

        def cols(t, i, w):
            return t[:, bass.ds(i * (BT * w), BT * w)]

        def by_tile(a, c=D):
            return a.rearrange("p (t c) -> p t c", c=c)

        def over(a, n):
            return a.unsqueeze(2).to_broadcast([P, a.shape[1], n])

        def carry_wait(eng):
            eng.sem_inc(s_carry, 1)

        def bounds_of_group(eng, g):
            both = eng.value_load(meta[0:1, bass.ds(g, 1)], min_val=0, max_val=(MORE << SHIFT) + N)
            start, more = eng.snap(both & ((1 << SHIFT) - 1)), eng.snap(both >> SHIFT)
            return start.with_bounds(min_val=0, max_val=N - 1), more

        def whole_after(eng, g):
            return eng.value_load(whole[0:1, bass.ds(g + 1, 1)], min_val=0, max_val=NT)

        def each_whole_tile(eng, now, done, step):
            before = eng.snap(done, min_val=0, max_val=NT)
            with eng.If(now > before):
                with eng.Fori(before, now) as t:
                    step(t)
            eng.reg_mov(done, now)

        def first_then_loop(eng, n):
            yield 0
            with eng.Fori(1, n) as i:
                yield i

        block = ctx.enter_context(nc.Block())

        @block.sync
        def _(sp):
            def edge_array(to, a, done, n=E):
                c0 = (NG - 1) * CH
                sp.dma_start(to[:, 0:c0].rearrange("p (g c) -> p g c", c=CH),
                             a[0:(NG - 1) * GROUP].rearrange("(g p c) -> p g c", p=P, c=CH)).then_inc(done, 16)
                at = (NG - 1) * GROUP
                full, rest = (n - at) // CH, (n - at) % CH
                sp.dma_start(to[0:full, c0:c0 + CH],
                             a[at:at + full * CH].rearrange("(p c) -> p c", c=CH)).then_inc(done, 16)
                sp.dma_start(to[full:full + 1, c0:c0 + rest],
                             a[at + full * CH:n].rearrange("(o c) -> o c", o=1)).then_inc(done, 16)

            sp.wait_ge(s_pad, 1)
            sp.dma_start(X3[:, 0:NT - 1, :], x[0:(NT - 1) * P, :].rearrange("(t p) c -> p t c", p=P)).then_inc(s_x, 16)
            sp.dma_start(X3[0:TAIL, NT - 1, :], x[(NT - 1) * P:N, :]).then_inc(s_x, 16)
            sp.dma_start(w0_s[:, :].rearrange("b (i o) -> b i o", o=D),
                         w0.rearrange("b i o -> (b i o)").rearrange("(i b o) -> b i o", b=B0, o=D)).then_inc(s_wa, 16)
            turned0 = comp0.rearrange("r b -> b r")
            sp.dma_start(comp0_s[:, 0, 0:R0], turned0, allow_slow_non_contiguous=True).then_inc(s_wa, 16)
            sp.dma_start(comp0_s[:, 1, R0:D], turned0, allow_slow_non_contiguous=True).then_inc(s_wa, 16)
            edge_array(src_i, src, s_src)
            edge_array(idx_a, et16, s_et16)
            for h in range(2):
                rows = HG - h
                sp.dma_start(drow_i[0:rows, h, :],
                             dst[h * HG * GROUP:(h * HG + rows) * GROUP].rearrange("(p n) -> p n", n=GROUP)).then_inc(s_rows, 16)
            sp.dma_start(drow_i[HG - 1:HG, 1, :], dst[E - GROUP:E].rearrange("(p n) -> p n", p=1)).then_inc(s_rows, 16)
            edge_array(dst_i, dst, s_dst)
            edge_array(nxt_i, dst[1:E], s_dst, E - 1)
            edge_array(ew1_s, ew1.rearrange("e o -> (e o)"), s_ew)
            edge_array(ew_s, ew, s_ew)
            sp.dma_start(w1_s[:, :, :], w1.rearrange("k i o -> i k o")).then_inc(s_wb, 16)
            sp.dma_start(b1_s[:, :], b1.rearrange("(a c) -> a c", a=1)).then_inc(s_wb, 16)
            sp.dma_start(w2_s[:, :, :], w2).then_inc(s_wb, 16)
            sp.dma_start(comp2_s[:, :], comp2.rearrange("r b -> b r"), allow_slow_non_contiguous=True).then_inc(s_wb, 16)
            sp.dma_start(self_s[:, :], selfw).then_inc(s_wb, 16)
            sp.dma_start(a1[:, 0:D], a1w).then_inc(s_wb, 16)
            sp.dma_start(a1[:, D:D + 1], a1b.rearrange("(k a) -> k a", a=1), allow_slow_non_contiguous=True).then_inc(s_wb, 16)
            for t, w, b in ((a1t, a1w, a1b), (a2t, a2w, a2b)):
                sp.dma_start(t[0:D, :], w.rearrange("k i -> i k"), allow_slow_non_contiguous=True).then_inc(s_wb, 16)
                sp.dma_start(t[D:D + 1, :], b.rearrange("(a k) -> a k", a=1)).then_inc(s_wb, 16)
            sp.dma_start(relt[:, :], rel.rearrange("r k -> k r"), allow_slow_non_contiguous=True).then_inc(s_wb, 16)

            sp.wait_ge(s_mm, 1)
            sp.dma_start(meta_d.rearrange("(h p) w -> p (h w)", h=2), mm_i[:, :], allow_slow_non_contiguous=True).then_inc(s_meta_w, 16)
            sp.wait_ge(s_meta_w, 16)
            sp.dma_start(meta[:, 0:NG], meta_d.rearrange("g w -> (g w)").rearrange("(a n) -> a n", a=1)).then_inc(s_meta_r, 16)
            sp.dma_start(bounds_b, meta_d.rearrange("g w -> (g w)").partition_broadcast(P)).then_inc(s_meta_r, 16)

            with sp.Fori(0, NT // 2) as i:
                for j in range(2):
                    sp.wait_ge(tile[0]["copied"], 2 * i + j + 1)
                    sp.dma_start(table0[bass.ds(i * (2 * P * R0) + j * P * R0, P * R0), :].rearrange("(p r) c -> p (r c)", p=P),
                                 t0buf[:, j, :]).then_inc(s_t0[j], 16)

            sp.wait_ge(s_flag, 1)
            unsorted = sp.value_load(flag_i[0:1, 0:1], min_val=0, max_val=1)
            with sp.If(unsorted > 0):
                with sp.Fori(0, NG - 1) as g:
                    sp.wait_ge(s_lused, g + 1)
                    sp.dma_start(trow, dst[bass.ds(g * GROUP, GROUP)].partition_broadcast(P)).then_inc(s_lrow, 16)
                sp.wait_ge(s_lused, NG)
                sp.dma_start(trow, dst[E - GROUP:E].partition_broadcast(P)).then_inc(s_lrow, 16)

            def store_nodes(e, to, of):
                view = nodes[to].rearrange("(p t) c -> p (t c)", p=P)
                with sp.Fori(0, NB) as i:
                    sp.wait_ge(blk[e]["u_ready"], i + 1)
                    sp.dma_start(view[:, bass.ds(i * (BT * D), BT * D)], of(i)).then_inc(blk[e]["u_stored"], 16)

            store_nodes(0, 0, lambda i: ubuf[:, :])
            sp.wait_ge(sums[0]["all_added"], 1)
            edge_array(idx_a, et86, s_et86)
            store_nodes(1, 1, lambda i: ubuf[:, :])
            with sp.Fori(0, NB) as i:
                with sp.Fori(0, BT) as j:
                    t = i * BT + j
                    for h in range(2):
                        sp.wait_ge(s_copied, NBUILD * t + BANKS + HALF_DONE[h])
                        carry_wait(sp)
                        r0, n = HALF[h]
                        view = table2[bass.ds(t * (P * RP), P * RP), :].rearrange("(p r) c -> p (r c)", p=P)
                        sp.dma_start(view[:, r0 * ROW2:(r0 + n) * ROW2], tbuf[:, h, 0:n * ROW2]).then_inc(s_t2[h], 16)
                sp.wait_ge(blk[2]["u_ready"], i * BT + BT)
                sp.dma_start(nodes[2].rearrange("(p t) c -> p (t c)", p=P)[:, bass.ds(i * (BT * D), BT * D)],
                             cols(H, i, D)).then_inc(blk[2]["u_stored"], 16)
            store_nodes(3, 3, lambda i: cols(H, i, D))
            sp.wait_ge(blk[4]["u_ready"], NB)
            sp.dma_start(out[0:(NT - 1) * P, :].rearrange("(t p) c -> p t c", p=P), X3[:, 0:NT - 1, :]).then_inc(s_out, 16)
            sp.dma_start(out[(NT - 1) * P:N, :], X3[0:TAIL, NT - 1, :]).then_inc(s_out, 16)
            sp.wait_ge(s_out, 32)

        @block.gpsimd
        def _(pool):
            nc.gpsimd.iota(iota_i[:, :], [[1, P]], base=0, channel_multiplier=0)
            nc.gpsimd.iota(pcol_i[:, :], [[1, 1]], base=0, channel_multiplier=1).then_inc(s_iota, 1)


            def gather_rows(s):
                q = sums[s]
                with pool.Fori(0, STEPS) as i:
                    for k in range(SLOTS):
                        n = s * PER_SUM + i * SLOTS + k + 1
                        pool.wait_ge(s_free, n)
                        pool.wait_ge(s_rows_known, n)
                        carry_wait(pool)
                        for c in range(CH):
                            nc.gpsimd.indirect_dma_start(
                                out=gbuf[:, k, c, 0:WIDTH[s]], out_offset=None, in_=TABLE[s],
                                in_offset=bass.IndirectOffsetOnAxis(ap=ibuf[:, k, c:c + 1], axis=0),
                            ).then_inc(q["gathered"][k], 16)

            for j in range(2):
                pool.wait_ge(s_t0[j], 16 * (NT // 2))
            gather_rows(0)
            pool.wait_ge(s_flag, 1)
            unsorted = pool.value_load(flag_i[0:1, 0:1], min_val=0, max_val=1)
            with pool.If(unsorted > 0):
                with pool.Fori(0, NT) as t:
                    pool.wait_ge(s_lcol, t + 1)
                    carry_wait(pool)
                    nc.gpsimd.indirect_dma_start(
                        out=lsrc_i[:, :], out_offset=None, in_=src.rearrange("(e o) -> e o", o=1),
                        in_offset=bass.IndirectOffsetOnAxis(ap=lcol[:, 0:1], axis=0)).then_inc(s_lgot, 16)
            pool.wait_ge(blk[0]["u_stored"], 16 * NB)
            gather_rows(1)
            pool.wait_ge(blk[1]["u_stored"], 16 * NB)
            gather_rows(2)
            pool.wait_ge(blk[2]["u_stored"], 16 * NB)
            pool.wait_ge(s_last, 1)
            for t in range(NT):
                nc.gpsimd.indirect_dma_start(
                    out=O[:, t * D:(t + 1) * D], out_offset=None, in_=nodes[2],
                    in_offset=bass.IndirectOffsetOnAxis(ap=last_i[:, t:t + 1], axis=0)).then_inc(s_curr, 16)
            for h in range(2):
                pool.wait_ge(s_t2[h], 16 * NT)
            gather_rows(3)
            pool.wait_ge(blk[3]["u_stored"], 16 * NB)
            gather_rows(4)

        @block.scalar
        def _(act):
            def turn_tile(f, t):
                s = tile[f]
                act.wait_ge(s["h_turned"], t + 1)
                nc.scalar.copy(hst[:, :], H[:, bass.ds(t * D, D)]).then_inc(s["h_staged"], 1)
                act.wait_ge(s["h_turned"], t + 2)
                act.wait_ge(s["made"], t + 1)
                nc.scalar.copy(ht[0:D, :], ps_h[0:D, 0:P]).then_inc(s["ht_ready"], 1)

            def roots(n, width):
                return nc.scalar.activation(stat[:, 1:1 + width, :], stat[:, 1:1 + width, :], ACT.Sqrt)

            def lay_out_rows(s):
                q = sums[s]
                for k in range(SLOTS):
                    nc.scalar.copy(ibuf[:, k, :], IDX[s][:, k * CH:(k + 1) * CH]).then_inc(s_rows_known, 1)
                if s == 2:
                    done = act.alloc_register("act_tiles")
                    act.reg_mov(done, 0)
                with act.Fori(0, STEPS) as i:
                    for k in range(SLOTS):
                        act.wait_ge(q["gathered"][k], (i + 1) * (16 * CH))
                        nc.scalar.copy(ibuf[:, k, :], IDX[s][:, bass.ds(i * (SLOTS * CH) + (SLOTS + k) * CH, CH)]
                                       ).then_inc(s_rows_known, 1)
                        if s == 2:
                            each_whole_tile(act, whole_after(act, i * SLOTS + k), done, tile_copies)
                    if s == 1:
                        for j in range(2):
                            turn_tile(1, 2 * i + j)

            def y_window(start, ready):
                nc.scalar.copy(ywin[:, :], big[64:64 + D, bass.ds(start, WIN)]).then_inc(ready, 1)

            def lay_out_turned(done):
                nc.scalar.copy(mem_b[0:WIN, :], wide[0:WIN, 0:GROUP])
                nc.scalar.copy(yw[:, :], ps_wide[0:WIN, 3, 0:D]).then_inc(done, 1)

            def attend():
                q = sums[3]
                for k in range(SLOTS):
                    nc.scalar.copy(ibuf[:, k, :], IDX[3][:, k * CH:(k + 1) * CH]).then_inc(s_rows_known, 1)
                count = act.alloc_register("act_more")
                act.reg_mov(count, 0)
                at = act.alloc_register("act_at")
                y_window(bounds_of_group(act, 0)[0], attn["y_window"])
                act.wait_ge(attn["turned"], 1)
                lay_out_turned(attn["laid_out"])
                with act.Fori(0, STEPS) as i:
                    for k in range(SLOTS):
                        g = i * SLOTS + k
                        y_window(bounds_of_group(act, g + 1)[0], attn["y_window"])
                        act.wait_ge(attn["scores"], g + 1)
                        nc.scalar.activation(att[:, :], score[:, :], ACT.Tanh).then_inc(attn["tanh"], 1)
                        act.wait_ge(q["gathered"][k], (i + 1) * (16 * CH))
                        nc.scalar.copy(ibuf[:, k, :], IDX[3][:, bass.ds(i * (SLOTS * CH) + (SLOTS + k) * CH, CH)]
                                       ).then_inc(s_rows_known, 1)
                        act.wait_ge(attn["turned"], g + 2)
                        carry_wait(act)
                        act.wait_ge(attn["y_own"], g + 1)
                        lay_out_turned(attn["laid_out"])
                        start, windows = bounds_of_group(act, g)
                        with act.If(windows > 0):
                            act.reg_mov(at, start)
                            with act.Fori(0, windows) as w:
                                act.reg_add(count, count, 1)
                                act.reg_add(at, at, WIN)
                                n = act.snap(count)
                                y_window(act.snap(at, min_val=0, max_val=NPAD), more["y_window"])
                                act.wait_ge(more["turned"], n)
                                lay_out_turned(more["laid_out"])
                                act.wait_ge(more["scores"], n)
                                nc.scalar.activation(att[:, :], score[:, :], ACT.Tanh).then_inc(more["tanh"], 1)

            tile_before = act.alloc_register("act_tile_before")
            act.reg_mov(tile_before, 0)

            def tile_copies(t):
                m = tile[2]
                act.wait_ge(s_final, t + 1)
                nc.scalar.copy(sums_t[:, :], big[0:D, bass.ds(t * P, P)]).then_inc(m["staged"], 1)
                act.wait_ge(s_var[2], t + 1)
                nc.scalar.activation(tdev[:, :], tdev[:, :], ACT.Sqrt).then_inc(s_std[2], 1)
                with act.If(t > 0):
                    table_rows(act.snap(tile_before, min_val=0, max_val=NT - 2))
                act.wait_ge(m["h_turned"], t + 1)
                nc.scalar.copy(ht[0:D, :], ps_h[0:D, 0:P]).then_inc(m["ht_ready"], 1)
                act.reg_mov(tile_before, t)

            def table_rows(t):
                act.wait_ge(tile[2]["made"], t + 1)
                nc.scalar.copy(big[64:64 + D, bass.ds(t * P, P)], ps_t[0:D, 0:P])
                nc.scalar.copy(xh[:, :], ps_t[:, P:P + D])
                act.drain()
                for r, (h, r0, n) in enumerate(BUILD):
                    half0, half_n = HALF[h]
                    rows = tbuf[:, h, 0:half_n * ROW2].rearrange("p (r c) -> p r c", c=ROW2)
                    if r0 == half0:
                        if isinstance(t, int):
                            act.wait_ge(s_t2[h], t * 16)
                        else:
                            with act.If(t > 0):
                                act.wait_ge(s_t2[h], t * 16)
                                carry_wait(act)
                        nc.scalar.copy(rows[:, :, PAIR:ROW2], xh[:, :].unsqueeze(1).to_broadcast([P, half_n, D]))
                    act.wait_ge(s_round, t * NBUILD + r + 1)
                    nc.scalar.copy(rows[:, r0 - half0:r0 - half0 + n, 0:PAIR],
                                   ps_wide[:, r % BANKS, 0:n * PAIR].rearrange("p (r c) -> p r c", c=PAIR)).then_inc(s_copied, 1)

            def stage_blocks(e, norm=None, width=1):
                act.wait_ge(sums[e]["all_added"], 1)
                s = blk[e]
                for i in first_then_loop(act, NB):
                    if not isinstance(i, int):
                        act.wait_ge(s["turned"], i)
                    nc.scalar.copy(stage[0:CHN[e], :], big[0:CHN[e], bass.ds(i * (BT * P), BT * P)]).then_inc(s["staged"], 1)
                    if e == 3:
                        nc.scalar.copy(cst[:, :], cols(O, i, D)).then_inc(s_cst, 1)
                        act.wait_ge(s_ct, i + 1)
                        act.wait_ge(s["turned"], i + 1)
                        nc.scalar.copy(stage[0:D, :], wide[0:D, 0:BT * P]).then_inc(s_ctc, 1)
                        act.wait_ge(s_cz, i + 1)
                    if norm is not None:
                        act.wait_ge(s_var[norm], i + 1)
                        roots(norm, width).then_inc(s_std[norm], 1)

            with act.Fori(0, NB) as i:
                act.wait_ge(s_var[0], i + 1)
                roots(0, 1).then_inc(s_std[0], 1)
            act.wait_ge(s_w0p, 1)
            nc.scalar.copy(w0f[:, :], ps_z[0:D, :]).then_inc(s_w0c, 1)
            act.wait_ge(tile[0]["h_ready"], 1)
            with act.Fori(0, NT) as t:
                turn_tile(0, t)
            act.wait_ge(s_idx, 1)
            lay_out_rows(0)
            stage_blocks(0, 1, 2)
            lay_out_rows(1)
            stage_blocks(1)
            act.sem_inc(s_copied, BANKS)
            lay_out_rows(2)
            table_rows(NT - 1)
            act.wait_ge(s_idx2, 1)
            attend()
            stage_blocks(3, 3)
            lay_out_rows(4)
            stage_blocks(4)

        @block.tensor
        def _(pe):

            def turn_tile(f, t):
                s = tile[f]
                pe.wait_ge(s["h_staged"], t + 1)
                nc.tensor.transpose(ps_h[0:D, 0:P], hst[:, :], ident[:, :]).then_inc(s["h_turned"], 1)
                pe.wait_ge(s["ht_ready"], t + 1)

            def add_rows(s, k, b, done):
                for c in range(CH):
                    last = nc.tensor.matmul(ps_agg[0:CHN[s], 0:WIN], gbuf[:, k, c, 0:CHN[s]], onehots[b][:, c, :],
                                            start=(c == 0), stop=(c == CH - 1))
                last.then_inc(done, 1)

            more_windows = pe.alloc_register("pe_more_windows")
            pe.reg_mov(more_windows, 0)

            def sum_edges(s):
                base = (s - (s > 3)) * NG
                if s == 2:
                    done = pe.alloc_register("pe_tiles")
                    pe.reg_mov(done, 0)
                with pe.Fori(0, STEPS) as i:
                    for k in range(SLOTS):
                        g = i * SLOTS + k
                        windows = bounds_of_group(pe, g)[1]
                        if s == 2:
                            now = whole_after(pe, g)
                        pe.wait_ge(s_ready, base + g + 1)
                        add_rows(s, k, k % 2, s_summed)
                        with pe.If(windows > 0):
                            with pe.Fori(0, windows) as w:
                                pe.reg_add(more_windows, more_windows, 1)
                                pe.wait_ge(s_more_ready, pe.snap(more_windows))
                                add_rows(s, k, k % 2, s_more_summed)
                        if s == 2:
                            each_whole_tile(pe, now, done, tile_products)
                    if s == 1:
                        for j in range(2):
                            t = 2 * i + j
                            turn_tile(1, t)
                            pe.wait_ge(tile[1]["copied"], t + 1)
                            nc.tensor.matmul(ps_z[:, 0:D], ht[0:D, :], w02[:, :], start=True, stop=False)
                            nc.tensor.matmul(ps_z[:, 0:D], ones[0:1, :], b1_s[:, :], start=False,
                                             stop=True).then_inc(tile[1]["made"], 1)

            tile_before = pe.alloc_register("pe_tile_before")
            pe.reg_mov(tile_before, 0)

            def tile_products(t):
                m = tile[2]
                pe.wait_ge(m["staged"], t + 1)
                carry_wait(pe)
                nc.tensor.matmul(ps_z[:, 0:D], sums_t[:, :], w1_s[:, 2, :], start=True, stop=True).then_inc(s_z, 1)
                with pe.If(t > 0):
                    table_products(pe.snap(tile_before, min_val=0, max_val=NT - 2))
                pe.wait_ge(m["h_staged"], t + 1)
                carry_wait(pe)
                nc.tensor.transpose(ps_h[0:D, 0:P], hst[:, :], ident[:, :]).then_inc(m["h_turned"], 1)
                pe.reg_mov(tile_before, t)

            def table_products(t):
                m = tile[2]
                pe.wait_ge(m["ht_ready"], t + 1)
                carry_wait(pe)
                nc.tensor.matmul(ps_t[0:D, 0:P], a2t[:, :], ht[:, :], start=True, stop=True)
                nc.tensor.matmul(ps_t[:, P:P + D], ht[:, :], a1t[:, :], start=True, stop=True).then_inc(m["made"], 1)
                for r, (h, r0, n) in enumerate(BUILD):
                    pe.wait_ge(s_copied, t * NBUILD + r + 1)
                    nc.tensor.matmul(ps_wide[:, r % BANKS, 0:n * PAIR], ht[:, :],
                                     w2f[:, 2 * r0:2 * (r0 + n), :].rearrange("p r c -> p (r c)"),
                                     start=True, stop=True).then_inc(s_round, 1)

            def turn_onehots(rows):
                for c in range(CH):
                    nc.tensor.transpose(ps_wide[0:WIN, c // 4, (c % 4) * P:(c % 4 + 1) * P], rows[:, c, :], ident[:, :])

            def turn_y(done):
                nc.tensor.transpose(ps_wide[0:WIN, 3, 0:D], ywin[:, :], ident[0:D, 0:D]).then_inc(done, 1)

            def pick_y(b, done):
                for c in range(CH):
                    last = nc.tensor.matmul(y_own[b][:, c, :], onehot_t[:, c, :], yw[:, :], start=True, stop=True)
                last.then_inc(done, 1)

            def add_messages(k, done):
                for c in range(CH):
                    last = nc.tensor.matmul(ps_agg[0:D, 0:WIN], msg[:, c, :], onehots3[k][:, c, :],
                                            start=(c == 0), stop=(c == CH - 1))
                last.then_inc(done, 1)

            def attend():
                q = sums[3]
                count = pe.alloc_register("pe_more")
                pe.reg_mov(count, 0)
                pe.wait_ge(q["onehot_ready"], 1)
                turn_onehots(onehots3[0])
                pe.wait_ge(attn["y_window"], 1)
                turn_y(attn["turned"])
                pe.wait_ge(attn["laid_out"], 1)
                pick_y(0, attn["y_own"])
                with pe.Fori(0, STEPS) as i:
                    for k in range(SLOTS):
                        g, b = i * SLOTS + k, k % 2
                        pe.wait_ge(q["onehot_ready"], g + 2)
                        carry_wait(pe)
                        turn_onehots(onehots3[(k + 1) % SLOTS])
                        pe.wait_ge(attn["y_window"], g + 2)
                        carry_wait(pe)
                        turn_y(attn["turned"])
                        pe.wait_ge(attn["messages"], g + 1)
                        add_messages(k, q["sums_ready"])
                        pe.wait_ge(attn["laid_out"], g + 2)
                        carry_wait(pe)
                        pick_y(1 - b, attn["y_own"])
                        windows = bounds_of_group(pe, g)[1]
                        with pe.If(windows > 0):
                            with pe.Fori(0, windows) as w:
                                pe.reg_add(count, count, 1)
                                n = pe.snap(count)
                                pe.wait_ge(more["onehot_ready"], n)
                                carry_wait(pe)
                                turn_onehots(onehots3[k])
                                pe.wait_ge(more["y_window"], n)
                                carry_wait(pe)
                                turn_y(more["turned"])
                                pe.wait_ge(more["laid_out"], n)
                                carry_wait(pe)
                                pick_y(b, more["y_own"])
                                pe.wait_ge(more["messages"], n)
                                add_messages(k, more["sums_ready"])

            def turn_blocks(e):
                s = blk[e]
                with pe.Fori(0, NB) as i:
                    pe.wait_ge(s["staged"], i + 1)
                    pe.wait_ge(s["read"], i + 1)
                    carry_wait(pe)
                    for k in range(BT):
                        last = nc.tensor.transpose(turned[:, k, 0:CHN[e]], stage[0:CHN[e], k * P:(k + 1) * P],
                                                   ident[0:CHN[e], 0:CHN[e]])
                    if e == 1:
                        for k in range(BT):
                            last = nc.tensor.matmul(zed[:, k, :], stage[0:D, k * P:(k + 1) * P], w1_s[:, e, :],
                                                    start=True, stop=True)
                    last.then_inc(s["turned"], 1)
                    if e == 3:
                        pe.wait_ge(s_cst, i + 1)
                        for k in range(BT):
                            last = nc.tensor.transpose(wide[0:D, k * P:(k + 1) * P], cst[:, k * D:(k + 1) * D], ident[:, :])
                        last.then_inc(s_ct, 1)
                        pe.wait_ge(s_ctc, i + 1)
                        for k in range(BT):
                            last = nc.tensor.matmul(zed[:, k, :], stage[0:D, k * P:(k + 1) * P], self_s[:, :],
                                                    start=True, stop=True)
                        last.then_inc(s_cz, 1)

            for f in range(2):
                pe.sem_inc(tile[f]["h_turned"], 1)
                pe.sem_inc(tile[f]["made"], 1)
            pe.wait_ge(s_wa, 48)
            w0v = w0_s[:, :].rearrange("b (r a o) -> b a r o", a=2, o=D)
            for a in range(2):
                last = nc.tensor.matmul(ps_z[0:D, :].rearrange("p (r o) -> p r o", o=D), comp0_s[:, a, :], w0v[:, a, :, :],
                                        start=(a == 0), stop=(a == 1))
            last.then_inc(s_w0p, 1)
            pe.wait_ge(s_const, 1)
            pe.wait_ge(s_w0c, 1)
            for i in first_then_loop(pe, NT // 2):
                for j in range(2):
                    turn_tile(0, 2 * i + j)
                    if not isinstance(i, int):
                        pe.wait_ge(tile[0]["copied"], 2 * i + j - 1)
                    nc.tensor.matmul(ps_wide[:, j, :], ht[0:D, :], w0f[:, :], start=True, stop=True).then_inc(tile[0]["made"], 1)
            pe.wait_ge(s_flagp, 1)
            nc.tensor.matmul(ps_agg[0:1, 0:1], flag[:, :], ones[:, 0:1], start=True, stop=True).then_inc(s_flags, 1)
            pe.wait_ge(s_wb, 16 * WB_DMAS)
            pe.wait_ge(tile[0]["copied"], NT)
            for r, o0 in enumerate(range(0, D, 5)):
                if r >= 2:
                    pe.wait_ge(s_w2c, r - 1)
                for o in range(o0, min(o0 + 5, D)):
                    last = nc.tensor.matmul(ps_wide[0:D, r % 2, (o - o0) * R2:(o - o0 + 1) * R2], w2_s[:, :, o],
                                            comp2_s[:, :], start=True, stop=True)
                last.then_inc(s_w2p, 1)
            nc.tensor.matmul(ps_z[0:D + 1, 0:R2], a1[:, :], relt[:, :], start=True, stop=True).then_inc(s_w2p, 1)
            pe.wait_ge(s_meta_r, 32)
            sum_edges(0)
            turn_blocks(0)
            sum_edges(1)
            turn_blocks(1)
            sum_edges(2)
            table_products(NT - 1)
            attend()
            turn_blocks(3)
            sum_edges(4)
            turn_blocks(4)

        @block.vector
        def _(dve):
            V = nc.vector

            def normalise(n, i):
                xb, hb, cb = by_tile(cols(X, i, D)), by_tile(cols(H, i, D)), by_tile(cent[:, :])
                V.tensor_reduce(stat[:, 0, :], xb, X_AXIS, ALU.add)
                dve.drain()
                V.tensor_scalar(stat[:, 0, :], stat[:, 0, :], 1.0 / D, None, ALU.mult)
                dve.drain()
                V.tensor_tensor(cb, xb, over(stat[:, 0, :], D), ALU.subtract)
                dve.drain()
                V.tensor_tensor(by_tile(sq[:, :]), cb, cb, ALU.mult)
                dve.drain()
                V.tensor_reduce(stat[:, 1, :], by_tile(sq[:, :]), X_AXIS, ALU.add)
                dve.drain()
                V.tensor_scalar(stat[:, 1, :], stat[:, 1, :], 1.0 / D, EPS, ALU.mult, ALU.add).then_inc(s_var[n], 1)
                dve.wait_ge(s_std[n], i + 1)
                V.reciprocal(stat[:, 1:3, :], stat[:, 1:3, :])
                dve.drain()
                V.tensor_tensor(hb, cb, over(stat[:, 1, :], D), ALU.mult)
                dve.drain()
                V.tensor_scalar(hb, hb, 0.0, None, ALU.max)
                dve.drain()

            more_windows = dve.alloc_register("dve_more_windows")
            dve.reg_mov(more_windows, 0)
            at = dve.alloc_register("dve_at")

            def sum_edges(s):
                q, base = sums[s], (s - (s > 3)) * NG
                V.memset(big[0:64, 0:SW], 0.0)
                dve.sem_inc(s_free, SLOTS)
                dve.drain()
                compare(onehots[0], drel[:, 0:CH])
                dve.drain()
                if s == 2:
                    done = dve.alloc_register("dve_tiles")
                    dve.reg_mov(done, 0)
                with dve.Fori(0, STEPS) as i:
                    for k in range(SLOTS):
                        g, b = i * SLOTS + k, k % 2
                        dve.wait_ge(q["gathered"][k], (i + 1) * (16 * CH))
                        rows = gbuf[:, k, :, 0:D]
                        if s < 3:
                            by = ew1_s if s == 0 else ew_s
                            V.tensor_tensor(rows, rows, by[:, bass.ds(g * CH, CH)].unsqueeze(2).to_broadcast([P, CH, D]), ALU.mult)
                        if s == 0:
                            V.tensor_copy(gbuf[:, k, :, D], ew_s[:, bass.ds(g * CH, CH)])
                            V.tensor_copy(gbuf[:, k, :, D + 2], lsrc[:, bass.ds(g * CH, CH)])
                        if s < 3:
                            dve.drain()
                        else:
                            carry_wait(dve)
                        dve.sem_inc(s_ready, 1)
                        compare(onehots[1 - b], drel[:, bass.ds(g * CH + CH, CH)])
                        start, windows = bounds_of_group(dve, g)
                        if s == 2:
                            now = whole_after(dve, g)
                        dve.wait_ge(s_summed, base + g + 1)
                        into = big[0:CHN[s], bass.ds(start, WIN)]
                        V.tensor_tensor(into, into, ps_agg[0:CHN[s], 0:WIN], ALU.add)
                        with dve.If(windows > 0):
                            dve.reg_mov(at, start)
                            V.tensor_copy(cur[:, :], drel[:, bass.ds(g * CH, CH)])
                            with dve.Fori(0, windows) as w:
                                dve.reg_add(more_windows, more_windows, 1)
                                dve.reg_add(at, at, WIN)
                                n = dve.snap(more_windows)
                                a = dve.snap(at, min_val=0, max_val=NPAD)
                                dve.drain()
                                V.tensor_scalar(cur[:, :], cur[:, :], float(-WIN), None, ALU.add)
                                dve.drain()
                                compare(onehots[b], cur[:, :]).then_inc(s_more_ready, 1)
                                dve.wait_ge(s_more_summed, n)
                                into = big[0:CHN[s], bass.ds(a, WIN)]
                                V.tensor_tensor(into, into, ps_agg[0:CHN[s], 0:WIN], ALU.add)
                        dve.drain()
                        dve.sem_inc(s_free, 1)
                        if s == 2:
                            each_whole_tile(dve, now, done, tile_norm)
                    if s == 1:
                        for j in range(2):
                            t = 2 * i + j
                            dve.wait_ge(tile[1]["made"], t + 2)
                            V.tensor_copy(O[:, bass.ds(t * D, D)], ps_z[:, 0:D]).then_inc(tile[1]["copied"], 1)
                dve.drain()
                if s > 0:
                    dve.sem_inc(q["all_added"], 1)

            def tile_norm(t):
                xt, dt = X[:, bass.ds(t * D, D)], dinv[:, bass.ds(t, 1)].to_broadcast([P, D])
                dve.drain()
                dve.sem_inc(s_final, 1)
                dve.wait_ge(s_z, t + 1)
                V.scalar_tensor_tensor(tsq[:, :], ps_z[:, 0:D], -2.0, dt, ALU.mult, ALU.mult)
                dve.drain()
                V.tensor_tensor(tsq[:, :], tsq[:, :], O[:, bass.ds(t * D, D)], ALU.add)
                dve.drain()
                V.scalar_tensor_tensor(xt, tsq[:, :], 0.0, xt, ALU.max, ALU.add)
                dve.drain()
                V.tensor_reduce(tmean[:, :], xt, X_AXIS, ALU.add)
                dve.drain()
                V.scalar_tensor_tensor(tcent[:, :], tmean[:, :].to_broadcast([P, D]), -1.0 / D, xt, ALU.mult, ALU.add)
                dve.drain()
                V.tensor_tensor(tsq[:, :], tcent[:, :], tcent[:, :], ALU.mult)
                dve.drain()
                V.tensor_reduce(tdev[:, :], tsq[:, :], X_AXIS, ALU.add)
                dve.drain()
                V.tensor_scalar(tdev[:, :], tdev[:, :], 1.0 / D, EPS, ALU.mult, ALU.add).then_inc(s_var[2], 1)
                dve.wait_ge(s_std[2], t + 1)
                V.reciprocal(tdev[:, :], tdev[:, :])
                dve.drain()
                for to, done in ((hst[:, :], tile[2]["h_staged"]), (H[:, bass.ds(t * D, D)], blk[2]["u_ready"])):
                    V.scalar_tensor_tensor(to, tcent[:, :], 0.0, tdev[:, :].to_broadcast([P, D]), ALU.max,
                                           ALU.mult).then_inc(done, 1)

            def compare(rows, targets):
                return V.tensor_tensor(rows[:, :, :], iota[:, 0:WIN].unsqueeze(1).to_broadcast([P, CH, WIN]),
                                       targets.unsqueeze(2).to_broadcast([P, CH, WIN]), ALU.is_equal)

            def weigh(k, g, n, m):
                pairs = gbuf[:, k, :, 0:PAIR].rearrange("p c (a d) -> p c a d", a=2)
                pick = par[:, :, bass.ds(g * CH, CH)].rearrange("p a c -> p c a")
                V.tensor_tensor(parts[:, :, D:D + 2], pairs[:, :, :, D], pick, ALU.mult)
                dve.wait_ge(m["y_own"], n)
                V.tensor_tensor(parts[:, :, 0:D], y_own[k % 2], gbuf[:, k, :, PAIR:ROW2], ALU.mult)
                dve.drain()
                V.tensor_reduce(raw[:, :], parts[:, :, :], X_AXIS, ALU.add)
                dve.drain()
                V.tensor_scalar(score[:, :], raw[:, :], float(1.0 / np.sqrt(D)), 0.0, ALU.mult, ALU.max).then_inc(m["scores"], 1)
                dve.wait_ge(m["tanh"], n)
                V.scalar_tensor_tensor(att2[:, :], att[:, :], 0.0, att[:, :], ALU.is_gt, ALU.mult)
                dve.drain()
                V.tensor_tensor(att_p[:, :, :], pick, att2[:, :].unsqueeze(2).to_broadcast([P, CH, 2]), ALU.mult)
                dve.drain()
                V.tensor_tensor(msg2[:, :, :, :], pairs[:, :, :, 0:D],
                                att_p[:, :, :].unsqueeze(3).to_broadcast([P, CH, 2, D]), ALU.mult)
                dve.drain()
                V.tensor_tensor(msg[:, :, :], msg2[:, :, 0, :], msg2[:, :, 1, :], ALU.add).then_inc(m["messages"], 1)

            def attend():
                q = sums[3]
                V.memset(big[0:64, 0:SW], 0.0)
                dve.sem_inc(s_free, SLOTS)
                for h in range(2):
                    dve.wait_ge(s_t2[h], 16 * NT)
                dve.drain()
                for k in range(2):
                    compare(onehots3[k], drel[:, k * CH:(k + 1) * CH]).then_inc(q["onehot_ready"], 1)
                count = dve.alloc_register("dve_more")
                dve.reg_mov(count, 0)
                with dve.Fori(0, STEPS) as i:
                    for k in range(SLOTS):
                        g = i * SLOTS + k
                        dve.wait_ge(q["gathered"][k], (i + 1) * (16 * CH))
                        weigh(k, g, g + 1, attn)
                        compare(onehots3[(k + 2) % SLOTS], drel[:, bass.ds(g * CH + 2 * CH, CH)]).then_inc(q["onehot_ready"], 1)
                        start, windows = bounds_of_group(dve, g)
                        dve.wait_ge(q["sums_ready"], g + 1)
                        into = big[0:D, bass.ds(start, WIN)]
                        V.tensor_tensor(into, into, ps_agg[0:D, 0:WIN], ALU.add)
                        with dve.If(windows > 0):
                            dve.reg_mov(at, start)
                            V.tensor_copy(cur[:, :], drel[:, bass.ds(g * CH, CH)])
                            with dve.Fori(0, windows) as w:
                                dve.reg_add(count, count, 1)
                                dve.reg_add(at, at, WIN)
                                n = dve.snap(count)
                                a = dve.snap(at, min_val=0, max_val=NPAD)
                                dve.drain()
                                V.tensor_scalar(cur[:, :], cur[:, :], float(-WIN), None, ALU.add)
                                dve.drain()
                                compare(onehots3[k], cur[:, :]).then_inc(more["onehot_ready"], 1)
                                weigh(k, g, n, more)
                                dve.wait_ge(more["sums_ready"], n)
                                into = big[0:D, bass.ds(a, WIN)]
                                V.tensor_tensor(into, into, ps_agg[0:D, 0:WIN], ALU.add)
                        dve.drain()
                        dve.sem_inc(s_free, 1)
                dve.drain()
                dve.sem_inc(q["all_added"], 1)

            V.memset(X[:, (NT - 1) * D:NT * D], 0.0)
            V.memset(comp0_s[:, :, :], 0.0)
            for t in (src_i, idx_a):
                V.memset(t[:, (NG - 1) * CH:IC], 0)
            V.memset(dst_i[:, (NG - 1) * CH:NG * CH], int(FAR))
            V.memset(nxt_i[:, (NG - 1) * CH:NG * CH], int(-2 * FAR))
            for t in (ew_s, two[:, 0, :]):
                V.memset(t[:, (NG - 1) * CH:NG * CH], 0.0)
            dve.drain()
            dve.sem_inc(s_pad, 1)
            V.memset(H[:, NT * D:FT * D], 0.0)
            V.memset(O[:, NT * D:FT * D], 0.0)
            V.memset(big[:, NPAD:SW], 0.0)
            V.memset(drel[:, NG * CH:(NG + 2) * CH], FAR)
            V.memset(meta[:, NG:NG + 1], 0)
            V.memset(w2f[D:D + 1, :, 0:D], 0.0)
            V.memset(ht[D:D + 1, :], 1.0)
            V.memset(ones[:, :], 1.0)
            V.memset(gbuf[:, :, :, D + 1], 1.0)
            V.memset(stat[:, :, :], 1.0)
            dve.wait_ge(s_iota, 1)
            V.tensor_copy(iota[:, :], iota_i[:, :])
            V.tensor_copy(pcol[:, :], pcol_i[:, :])
            dve.drain()
            V.tensor_scalar(ident[:, :], iota[:, :], pcol[:, 0:1], None, ALU.is_equal).then_inc(s_const, 1)
            dve.wait_ge(s_x, 32)
            dve.drain()
            with dve.Fori(0, NB) as i:
                normalise(0, i)
            dve.sem_inc(tile[0]["h_ready"], 1)

            dve.wait_ge(s_rows, 48)
            V.tensor_reduce(mm_f[:, :, 0], drow_i, X_AXIS, ALU.min)
            V.tensor_reduce(mm_f[:, :, 1], drow_i, X_AXIS, ALU.max)
            dve.drain()
            V.tensor_tensor(mm_w[:, :], mm_f[:, :, 1], mm_f[:, :, 0], ALU.subtract)
            dve.drain()
            V.tensor_scalar(mm_w[:, :], mm_w[:, :], float(SCALE), None, ALU.mult)
            dve.drain()
            V.tensor_scalar(mm_w[:, :], mm_w[:, :], SHIFT, None, ALU.arith_shift_right)
            dve.drain()
            V.scalar_tensor_tensor(mm_i[:, :], mm_w[:, :], float(1 << SHIFT), mm_f[:, :, 0], ALU.mult, ALU.add).then_inc(s_mm, 1)

            dve.wait_ge(s_src, 48)
            V.tensor_scalar(tmp_i, src_i[:, :], P - 1, None, ALU.bitwise_and)
            V.tensor_scalar(idx_h[:, :], src_i[:, :], 7, None, ALU.arith_shift_right)
            dve.drain()
            V.scalar_tensor_tensor(idx_h[:, :], tmp_i, float(NT), idx_h[:, :], ALU.mult, ALU.add)
            dve.wait_ge(s_et16, 48)
            V.scalar_tensor_tensor(idx_a[:, :], src_i[:, :], float(R0), idx_a[:, :], ALU.mult, ALU.add)
            dve.drain()
            dve.sem_inc(s_idx, 1)

            for i in first_then_loop(dve, NT // 2):
                for j in range(2):
                    dve.wait_ge(tile[0]["made"], 2 * i + j + 2)
                    if not isinstance(i, int):
                        dve.wait_ge(s_t0[j], i * 16)
                    V.tensor_copy(t0buf[:, j, :], ps_wide[:, j, :]).then_inc(tile[0]["copied"], 1)

            dve.wait_ge(s_dst, 96)
            V.tensor_copy(dst_f, dst_i)
            V.tensor_copy(nxt_f, nxt_i)
            dve.drain()
            V.tensor_tensor(tmp_f, dst_f, nxt_f, ALU.is_gt)
            dve.drain()
            V.tensor_reduce(flag[:, :], tmp_f, X_AXIS, ALU.add).then_inc(s_flagp, 1)
            dve.drain()
            V.tensor_tensor(tmp_f, dst_f, nxt_f, ALU.not_equal)
            dve.drain()
            V.tensor_tensor(lsrc, tmp_f, src_i[:, 0:NG * CH], ALU.mult)
            dve.wait_ge(s_meta_r, 32)
            V.tensor_scalar(bounds_b, bounds_b, (1 << SHIFT) - 1, None, ALU.bitwise_and)
            V.tensor_scalar(least_i, meta[:, 0:NG], (1 << SHIFT) - 1, None, ALU.bitwise_and)
            dve.drain()
            V.tensor_tensor(drel[:, 0:NG * CH].rearrange("p (g c) -> p g c", c=CH), dst_f.rearrange("p (g c) -> p g c", c=CH),
                            bounds_b.unsqueeze(2).to_broadcast([P, NG, CH]),
                            ALU.subtract)
            V.memset(least[0][:, NG:NG + 1], float(NT * P))
            V.tensor_copy(least[0][:, 0:NG], least_i)
            step, j = 1, 0
            while step <= NG:
                dve.drain()
                V.tensor_tensor(least[1 - j][:, 0:NG + 1 - step], least[j][:, 0:NG + 1 - step], least[j][:, step:NG + 1], ALU.min)
                V.tensor_copy(least[1 - j][:, NG + 1 - step:NG + 1], least[j][:, NG + 1 - step:NG + 1])
                step, j = 2 * step, 1 - j
            dve.drain()
            V.tensor_copy(whole[:, :], least[j][:, :])
            dve.drain()
            V.tensor_scalar(whole[:, :], whole[:, :], 7, None, ALU.arith_shift_right)
            dve.wait_ge(s_flags, 1)
            V.tensor_scalar(flag_i[:, :], ps_agg[0:1, 0:1], 0.0, None, ALU.is_gt).then_inc(s_flag, 1)

            for r, o0 in enumerate(range(0, D, 5)):
                n = min(5, D - o0)
                dve.wait_ge(s_w2p, r + 1)
                V.tensor_copy(w2f[0:D, :, o0:o0 + n],
                              ps_wide[0:D, r % 2, 0:n * R2].rearrange("p (o r) -> p r o", r=R2)).then_inc(s_w2c, 1)
            dve.wait_ge(s_w2p, 8)
            V.tensor_copy(w2f[:, :, D], ps_z[0:D + 1, 0:R2])
            V.tensor_tensor(w02[:, :], w1_s[:, 0, :], w1_s[:, 2, :], ALU.subtract)
            dve.sem_inc(tile[1]["copied"], 1)
            for e in range(5):
                dve.sem_inc(blk[e]["read"], 1)
            dve.wait_ge(s_ew, 96)
            dve.drain()

            sum_edges(0)

            unsorted = dve.value_load(flag_i[0:1, 0:1], min_val=0, max_val=1)
            with dve.If(unsorted > 0):
                V.memset(last_e[:, :], 0.0)
                V.memset(base[:, :], 0.0)
                for c in range(CH):
                    V.tensor_scalar(key[:, c * P:(c + 1) * P], iota[:, :], float(c * P + 1), None, ALU.add)
                dve.drain()
                dve.sem_inc(s_lused, 1)
                with dve.Fori(0, NG) as g:
                    V.tensor_scalar(base[:, :], base[:, :], float(E - GROUP), None, ALU.min)
                    V.tensor_copy(node[:, :], pcol[:, :])
                    dve.drain()
                    dve.wait_ge(s_lrow, g * 16 + 16)
                    carry_wait(dve)
                    with dve.Fori(0, NT) as t:
                        V.scalar_tensor_tensor(keyed, trow, node[:, 0:1], key, ALU.is_equal, ALU.mult)
                        dve.drain()
                        V.tensor_reduce(found[:, 0:1], keyed, X_AXIS, ALU.max)
                        dve.drain()
                        V.scalar_tensor_tensor(found[:, 1:2], found[:, 0:1], 0.0, base[:, :], ALU.is_gt, ALU.mult)
                        dve.drain()
                        V.tensor_tensor(found[:, 0:1], found[:, 0:1], found[:, 1:2], ALU.add)
                        V.tensor_scalar(node[:, :], node[:, :], float(P), None, ALU.add)
                        dve.drain()
                        V.tensor_tensor(last_e[:, bass.ds(t, 1)], last_e[:, bass.ds(t, 1)], found[:, 0:1], ALU.max)
                        dve.drain()
                    V.tensor_scalar(base[:, :], base[:, :], float(GROUP), None, ALU.add)
                    dve.drain()
                    dve.sem_inc(s_lused, 1)
                with dve.Fori(0, NT) as t:
                    V.tensor_scalar(lcol[:, :], last_e[:, bass.ds(t, 1)], -1.0, 0.0, ALU.add, ALU.max).then_inc(s_lcol, 1)
                    dve.wait_ge(s_lgot, t * 16 + 16)
                    carry_wait(dve)
                    V.tensor_copy(last_e[:, bass.ds(t, 1)], lsrc_i[:, :])
                    dve.drain()
            dve.sem_inc(sums[0]["all_added"], 1)

            for i in first_then_loop(dve, NB):
                xb = by_tile(cols(X, i, D))
                dve.wait_ge(blk[0]["turned"], i + 1)
                V.tensor_tensor(xb, xb, turned[:, :, 0:D], ALU.add)
                V.tensor_scalar(stat[:, 2, :], turned[:, :, D], 1e-12, None, ALU.max)
                V.tensor_scalar(stat[:, 3, :], turned[:, :, D], 0.0, None, ALU.is_gt)
                V.tensor_copy(cols(deg, i, 1), turned[:, :, D + 1])
                V.tensor_copy(cols(last_f, i, 1), turned[:, :, D + 2]).then_inc(blk[0]["read"], 1)
                dve.drain()
                normalise(1, i)
                V.tensor_tensor(cols(dinv, i, 1), stat[:, 2, :], stat[:, 3, :], ALU.mult)
                dve.drain()
                if not isinstance(i, int):
                    dve.wait_ge(blk[0]["u_stored"], i * 16)
                V.tensor_tensor(by_tile(ubuf[:, :]), by_tile(cols(H, i, D)), over(cols(dinv, i, 1), D),
                                ALU.mult).then_inc(blk[0]["u_ready"], 1)
            dve.sem_inc(tile[1]["h_ready"], 1)
            with dve.If(unsorted > 0):
                V.tensor_copy(last_f[:, :], last_e[:, :])
                dve.drain()
            V.tensor_copy(li_a[:, :], last_f[:, :])
            dve.drain()
            V.tensor_scalar(li_b[:, :], li_a[:, :], P - 1, None, ALU.bitwise_and)
            V.tensor_scalar(last_i[:, :], li_a[:, :], 7, None, ALU.arith_shift_right)
            dve.drain()
            V.scalar_tensor_tensor(last_i[:, :], li_b[:, :], float(NT), last_i[:, :], ALU.mult, ALU.add).then_inc(s_last, 1)

            sum_edges(1)
            for i in first_then_loop(dve, NB):
                db, ob = over(cols(dinv, i, 1), D), by_tile(cols(O, i, D))
                dve.wait_ge(blk[1]["turned"], i + 1)
                V.scalar_tensor_tensor(by_tile(cent[:, :]), turned[:, :, 0:D], -1.0, db, ALU.mult, ALU.mult)
                V.scalar_tensor_tensor(by_tile(sq[:, :]), zed, -1.0, db, ALU.mult, ALU.mult).then_inc(blk[1]["read"], 1)
                dve.drain()
                if not isinstance(i, int):
                    dve.wait_ge(blk[1]["u_stored"], i * 16)
                V.tensor_tensor(by_tile(ubuf[:, :]), by_tile(cent[:, :]), db, ALU.mult).then_inc(blk[1]["u_ready"], 1)
                V.tensor_tensor(ob, ob, by_tile(sq[:, :]), ALU.add)
                dve.drain()

            dve.wait_ge(s_et86, 48)
            V.tensor_scalar(lsrc.bitcast(I32), idx_a[:, 0:NG * CH], 1, None, ALU.bitwise_and)
            dve.drain()
            V.tensor_copy(ew1_s, lsrc.bitcast(I32))
            dve.drain()
            V.tensor_copy(lsrc, ew1_s)
            V.tensor_scalar(ew1_s, ew1_s, -1.0, 1.0, ALU.mult, ALU.add)
            V.tensor_scalar(idx_a[:, :], idx_a[:, :], 1, None, ALU.arith_shift_right)
            dve.drain()
            V.scalar_tensor_tensor(idx_a[:, :], src_i[:, :], float(RP), idx_a[:, :], ALU.mult, ALU.add).then_inc(s_idx2, 1)

            sum_edges(2)
            attend()
            V.tensor_scalar(mask[:, :], deg[:, :], 0.0, None, ALU.is_gt)
            dve.wait_ge(s_curr, 16 * NT)
            dve.drain()
            with dve.Fori(0, NB) as i:
                xb = by_tile(cols(X, i, D))
                dve.wait_ge(s_cz, i + 1)
                V.tensor_copy(by_tile(sq[:, :]), zed)
                dve.drain()
                V.tensor_tensor(by_tile(sq[:, :]), by_tile(sq[:, :]), turned[:, :, 0:D], ALU.add).then_inc(blk[3]["read"], 1)
                dve.drain()
                V.tensor_tensor(by_tile(sq[:, :]), by_tile(sq[:, :]), over(cols(mask, i, 1), D), ALU.mult)
                dve.drain()
                V.scalar_tensor_tensor(xb, by_tile(sq[:, :]), 0.0, xb, ALU.max, ALU.add)
                dve.drain()
                normalise(3, i)
                dve.sem_inc(blk[3]["u_ready"], 1)

            sum_edges(4)
            V.tensor_scalar(mask[:, :], deg[:, :], 1.0, None, ALU.max)
            dve.drain()
            V.reciprocal(mask[:, :], mask[:, :])
            dve.drain()
            with dve.Fori(0, NB) as i:
                xb = by_tile(cols(X, i, D))
                dve.wait_ge(blk[4]["turned"], i + 1)
                V.tensor_tensor(by_tile(sq[:, :]), turned[:, :, 0:D], over(cols(mask, i, 1), D), ALU.mult).then_inc(blk[4]["read"], 1)
                dve.drain()
                V.tensor_tensor(xb, xb, by_tile(sq[:, :]), ALU.add).then_inc(blk[4]["u_ready"], 1)
                dve.drain()


INS = ["x", "src", "dst", "edge_type_16", "edge_type_86", "edge_weight", "edge_weight1", "L0_gnn_weight",
       "L0_gnn_w_comp", "L1_gnn_W", "L1_gnn_b", "L2_gnn_weight", "L2_gnn_w_comp", "L2_gnn_self_loop_weight",
       "L2_gnn_A1_w", "L2_gnn_A1_b", "L2_gnn_A2_w", "L2_gnn_A2_b", "L2_gnn_rel_emb"]


def kernel(**inputs):
    import concourse.bacc as bacc
    from concourse.bass_utils import run_bass_kernel_spmd

    nc = bacc.Bacc("TRN2", target_bir_lowering=False, num_devices=1)
    arrays, args = {}, []
    for name in INS:
        a = np.ascontiguousarray(inputs[name])
        arrays[f"in_{name}"] = a
        args.append(nc.dram_tensor(f"in_{name}", a.shape, mybir.dt.from_np(a.dtype), kind="ExternalInput").ap())
    out = nc.dram_tensor("out", (N, D), F32, kind="ExternalOutput").ap()
    gnn_kernel(nc, *args, out)
    r = run_bass_kernel_spmd(nc, [arrays], core_ids=[0])
    return r.results[0]["out"]
```
